# Optimizing a Trainium2 kernel written in Bass

```python
import numpy as np
import jax
import jax.numpy as jnp

def _softmax(x, axis=-1):
    return jax.nn.softmax(x, axis=axis)

def _gelu(x):
    return jax.nn.gelu(x, approximate=True)

def _silu(x):
    return jax.nn.silu(x)

def _sigmoid(x):
    return jax.nn.sigmoid(x)

def _layernorm(x, axis=-1, eps=1e-05):
    m = jnp.mean(x, axis=axis, keepdims=True)
    v = jnp.var(x, axis=axis, keepdims=True)
    return (x - m) / jnp.sqrt(v + eps)

def _scatter_add(tgt, idx, src, axis=0):
    return tgt.at[idx].add(src)

def _segment_sum(src, seg, n):
    return jax.ops.segment_sum(src, seg, n)
kernel_name = 'mk_decoder_preln_d1_seqx_r2_293451'

def setup_inputs(seed: int=0):
    np.random.seed(seed)
    _w = jnp.asarray

    def _rec_inputs():
        import jax
        import jax.numpy as jnp
        _rk = jax.random.key(seed)
        x = -0.000929 + 1 * jax.random.normal(jax.random.fold_in(_rk, 1), (4, 1024, 512), jnp.float32)
        _lenS = 1024 - jax.random.randint(jax.random.fold_in(_rk, 7), (4,), 0, max(1, 1024 // 4) + 1, jnp.int32)
        _lenS2 = 1024 - jax.random.randint(jax.random.fold_in(_rk, 8), (4,), 0, max(1, 1024 // 4) + 1, jnp.int32)
        _ctx_1024P = jax.random.normal(jax.random.fold_in(_rk, 11), (4, 16, 512), jnp.float32)
        _ctx_1024c = jax.random.dirichlet(jax.random.fold_in(_rk, 511), 0.3 * jnp.ones((16,), jnp.float32), (4, 1024))
        _ctx_1024t = jnp.einsum('bsk,bkd->bsd', _ctx_1024c, _ctx_1024P)
        _ctx_1024t = _ctx_1024t * jax.lax.rsqrt(jnp.mean(jnp.square(_ctx_1024t)) + 1e-12) * 0.953939
        ctx_1024 = 2.81802e-05 + 1.00001 * (_ctx_1024t + 0.3 * jax.random.normal(jax.random.fold_in(_rk, 611), (4, 1024, 512), jnp.float32))
        _validS = jnp.arange(1024)[None, :] < _lenS[:, None]
        _validS2 = jnp.arange(1024)[None, :] < _lenS2[:, None]
        _causal = jnp.tril(jnp.ones((1024, 1024), dtype=bool))
        mask_BxS2_bf0 = jnp.logical_not(jnp.ones((4, 1024), dtype=bool))
        return (x, ctx_1024, mask_BxS2_bf0)
    x, ctx_1024, mask_BxS2_bf0 = _rec_inputs()

    def _L0_attn_setup():
        import jax, jax.numpy as jnp
        import numpy as np
        import math
        B, S, D_IN, D_KQ, D_OUT = (4, 1024, 512, 512, 512)
        key = jax.random.key(seed)
        ks = jax.random.split(key, 7)
        sc = 0.02
        return {'x': jax.random.normal(ks[0], (B, S, D_IN), jnp.float32), 'Wq': jax.random.normal(ks[1], (D_KQ, D_IN), jnp.float32) * sc, 'bq': jax.random.normal(ks[2], (D_KQ,), jnp.float32) * sc, 'Wk': jax.random.normal(ks[3], (D_KQ, D_IN), jnp.float32) * sc, 'bk': jax.random.normal(ks[4], (D_KQ,), jnp.float32) * sc, 'Wv': jax.random.normal(ks[5], (D_OUT, D_IN), jnp.float32) * sc, 'bv': jax.random.normal(ks[6], (D_OUT,), jnp.float32) * sc}
    _L0_attn_all = _L0_attn_setup()
    _L0_attn_in = {k: v for k, v in _L0_attn_all.items() if k in ('Wq', 'bq', 'Wk', 'bk', 'Wv', 'bv')}
    del _L0_attn_all

    def _L0_xattn_setup():
        import jax, jax.numpy as jnp
        import numpy as np
        D_MODEL = 512
        NUM_HEADS = 16
        STRIDE = 4
        HEAD_DIM = D_MODEL // NUM_HEADS
        SCALE = HEAD_DIM ** (-0.5)
        key = jax.random.key(seed)
        ks = jax.random.split(key, 12)
        B, T, S = (2, 256, 4096)
        inp = {'query': jax.random.normal(ks[0], (B, T, D_MODEL), jnp.float32), 'key': jax.random.normal(ks[1], (B, S, D_MODEL), jnp.float32), 'value': jax.random.normal(ks[2], (B, S, D_MODEL), jnp.float32), 'key_padding_mask': jnp.zeros((B, S), dtype=bool)}
        s = 1.0 / np.sqrt(D_MODEL)
        inp['Wq'] = jax.random.normal(ks[3], (D_MODEL, D_MODEL), jnp.float32) * s
        inp['bq'] = jnp.zeros((D_MODEL,), jnp.float32)
        inp['Wk'] = jax.random.normal(ks[4], (D_MODEL, D_MODEL), jnp.float32) * s
        inp['bk'] = jnp.zeros((D_MODEL,), jnp.float32)
        inp['Wv'] = jax.random.normal(ks[5], (D_MODEL, D_MODEL), jnp.float32) * s
        inp['bv'] = jnp.zeros((D_MODEL,), jnp.float32)
        inp['Wo'] = jax.random.normal(ks[6], (D_MODEL, D_MODEL), jnp.float32) * s
        inp['bo'] = jnpp = jnp.zeros((D_MODEL,), jnp.float32)
        return inp
    _L0_xattn_all = _L0_xattn_setup()
    _L0_xattn_in = {k: v for k, v in _L0_xattn_all.items() if k in ('Wq', 'bq', 'Wk', 'bk', 'Wv', 'bv', 'Wo', 'bo')}
    del _L0_xattn_all

    def _L0_ffn_setup():
        import jax, jax.numpy as jnp
        import numpy as np
        E = 8
        D = 512
        DO = 512
        R = 64
        H = 128
        B, T = (8, 1024)
        key = jax.random.key(seed)
        ks = jax.random.split(key, 12)
        s = lambda k, shape, fan: jax.random.normal(k, shape, jnp.float32) / np.sqrt(fan)
        return {'x': jax.random.normal(ks[0], (B, T, D), jnp.float32), 'W_base': s(ks[1], (D, DO), D), 'b_base': jnp.zeros((DO,), jnp.float32), 'Wd1': s(ks[2], (E, D, H), D), 'bd1': jnp.zeros((E, H), jnp.float32), 'Wd2': s(ks[3], (E, H, D), H), 'bd2': jnp.zeros((E, D), jnp.float32), 'Wa_down': s(ks[4], (E, D, R), D), 'ba_down': jnp.zeros((E, R), jnp.float32), 'Wa_up': s(ks[5], (E, R, DO), R), 'ba_up': jnp.zeros((E, DO), jnp.float32)}
    _L0_ffn_all = _L0_ffn_setup()
    _L0_ffn_in = {k: v for k, v in _L0_ffn_all.items() if k in ('W_base', 'b_base', 'Wd1', 'bd1', 'Wd2', 'bd2', 'Wa_down', 'ba_down', 'Wa_up', 'ba_up')}
    del _L0_ffn_all
    return {'x': x, 'ctx_1024': ctx_1024, 'mask_BxS2_bf0': mask_BxS2_bf0, 'L0_attn_Wq': _L0_attn_in['Wq'], 'L0_attn_bq': _L0_attn_in['bq'], 'L0_attn_Wk': _L0_attn_in['Wk'], 'L0_attn_bk': _L0_attn_in['bk'], 'L0_attn_Wv': _L0_attn_in['Wv'], 'L0_attn_bv': _L0_attn_in['bv'], 'L0_xattn_Wq': _L0_xattn_in['Wq'], 'L0_xattn_bq': _L0_xattn_in['bq'], 'L0_xattn_Wk': _L0_xattn_in['Wk'], 'L0_xattn_bk': _L0_xattn_in['bk'], 'L0_xattn_Wv': _L0_xattn_in['Wv'], 'L0_xattn_bv': _L0_xattn_in['bv'], 'L0_xattn_Wo': _L0_xattn_in['Wo'], 'L0_xattn_bo': _L0_xattn_in['bo'], 'L0_ffn_W_base': _L0_ffn_in['W_base'], 'L0_ffn_b_base': _L0_ffn_in['b_base'], 'L0_ffn_Wd1': _L0_ffn_in['Wd1'], 'L0_ffn_bd1': _L0_ffn_in['bd1'], 'L0_ffn_Wd2': _L0_ffn_in['Wd2'], 'L0_ffn_bd2': _L0_ffn_in['bd2'], 'L0_ffn_Wa_down': _L0_ffn_in['Wa_down'], 'L0_ffn_ba_down': _L0_ffn_in['ba_down'], 'L0_ffn_Wa_up': _L0_ffn_in['Wa_up'], 'L0_ffn_ba_up': _L0_ffn_in['ba_up']}

def reference(x, ctx_1024, mask_BxS2_bf0, L0_attn_Wq, L0_attn_bq, L0_attn_Wk, L0_attn_bk, L0_attn_Wv, L0_attn_bv, L0_xattn_Wq, L0_xattn_bq, L0_xattn_Wk, L0_xattn_bk, L0_xattn_Wv, L0_xattn_bv, L0_xattn_Wo, L0_xattn_bo, L0_ffn_W_base, L0_ffn_b_base, L0_ffn_Wd1, L0_ffn_bd1, L0_ffn_Wd2, L0_ffn_bd2, L0_ffn_Wa_down, L0_ffn_ba_down, L0_ffn_Wa_up, L0_ffn_ba_up):
    import jax
    import jax.numpy as jnp

    def _L0_attn_ref(x, Wq, bq, Wk, bk, Wv, bv):
        import jax, jax.numpy as jnp
        import numpy as np
        import math
        B, S, D_IN, D_KQ, D_OUT = (4, 1024, 512, 512, 512)
        Q = jnp.einsum('bsd,kd->bsk', x, Wq) + bq
        K = jnp.einsum('bsd,kd->bsk', x, Wk) + bk
        V = jnp.einsum('bsd,od->bso', x, Wv) + bv
        scale = 1.0 / math.sqrt(D_KQ)
        attn = jnp.einsum('bqk,bsk->bqs', Q, K) * scale
        s = attn.shape[-1]
        causal = jnp.tril(jnp.ones((s, s), dtype=bool))
        attn = jnp.where(causal[None, :, :], attn, -jnp.inf)
        attn = jax.nn.softmax(attn, axis=-1)
        Z = jnp.einsum('bqs,bso->bqo', attn, V)
        return Z

    def _L0_xattn_ref(query, key, value, key_padding_mask, Wq, bq, Wk, bk, Wv, bv, Wo, bo):
        import jax, jax.numpy as jnp
        import numpy as np
        D_MODEL = 512
        NUM_HEADS = 16
        STRIDE = 4
        HEAD_DIM = D_MODEL // NUM_HEADS
        SCALE = HEAD_DIM ** (-0.5)
        B, T, _ = query.shape
        S = key.shape[1]
        q = (query @ Wq + bq).reshape(B, T, NUM_HEADS, HEAD_DIM).transpose(0, 2, 1, 3)
        k = (key @ Wk + bk).reshape(B, S, NUM_HEADS, HEAD_DIM).transpose(0, 2, 1, 3)
        v = (value @ Wv + bv).reshape(B, S, NUM_HEADS, HEAD_DIM).transpose(0, 2, 1, 3)
        scores = jnp.einsum('bhtd,bhsd->bhts', q, k) * SCALE
        s_idx = jnp.arange(S)[None, None, None, :]
        h_idx = jnp.arange(NUM_HEADS)[None, :, None, None]
        hepos_mask = (s_idx - h_idx) % STRIDE != 0
        scores = jnp.where(hepos_mask, -jnp.inf, scores)
        scores = jnp.where(key_padding_mask[:, None, None, :], -jnp.inf, scores)
        attn = jax.nn.softmax(scores, axis=-1)
        context = jnp.einsum('bhts,bhsd->bhtd', attn, v)
        context = context.transpose(0, 2, 1, 3).reshape(B, T, D_MODEL)
        return context @ Wo + bo

    def _L0_ffn_ref(x, W_base, b_base, Wd1, bd1, Wd2, bd2, Wa_down, ba_down, Wa_up, ba_up):
        import jax, jax.numpy as jnp
        import numpy as np
        E = 8
        D = 512
        DO = 512
        R = 64
        H = 128
        B, T = (8, 1024)
        base = jnp.einsum('btd,do->bto', x, W_base) + b_base
        h = jax.nn.relu(jnp.einsum('btd,edh->ebth', x, Wd1) + bd1[:, None, None, :])
        recon = jnp.einsum('ebth,ehd->ebtd', h, Wd2) + bd2[:, None, None, :]
        losses = jnp.mean((recon - x[None]) ** 2, axis=(2, 3))
        idx = jnp.argmin(losses, axis=0)
        a = jax.nn.relu(jnp.einsum('btd,bdr->btr', x, Wa_down[idx]) + ba_down[idx][:, None, :])
        adapter_out = jnp.einsum('btr,bro->bto', a, Wa_up[idx]) + ba_up[idx][:, None, :]
        return base + adapter_out
    x = x + _L0_attn_ref(_layernorm(x, axis=-1), L0_attn_Wq, L0_attn_bq, L0_attn_Wk, L0_attn_bk, L0_attn_Wv, L0_attn_bv)
    x = x + _L0_xattn_ref(_layernorm(x, axis=-1), ctx_1024, ctx_1024, mask_BxS2_bf0, L0_xattn_Wq, L0_xattn_bq, L0_xattn_Wk, L0_xattn_bk, L0_xattn_Wv, L0_xattn_bv, L0_xattn_Wo, L0_xattn_bo)
    x = x + _L0_ffn_ref(_layernorm(x, axis=-1), L0_ffn_W_base, L0_ffn_b_base, L0_ffn_Wd1, L0_ffn_bd1, L0_ffn_Wd2, L0_ffn_bd2, L0_ffn_Wa_down, L0_ffn_ba_down, L0_ffn_Wa_up, L0_ffn_ba_up)
    return x

_drawn_inputs = setup_inputs


def setup_inputs(seed=0):
    import zlib

    import numpy as np

    out = dict(_drawn_inputs(seed))
    spreads = {'L0_xattn_bq': (0.0, 0.1),
     'L0_xattn_bk': (0.0, 0.8),
     'L0_xattn_bv': (0.0, 0.1),
     'L0_xattn_bo': (0.0, 0.1),
     'L0_ffn_b_base': (0.0, 0.1),
     'L0_ffn_bd1': (0.0, 0.1),
     'L0_ffn_bd2': (0.0, 0.1),
     'L0_ffn_ba_down': (0.0, 0.1),
     'L0_ffn_ba_up': (0.0, 0.1)}
    factors = {'L0_attn_Wq': 7.525, 'L0_attn_bq': 8.0, 'L0_attn_Wk': 7.337, 'L0_attn_bk': 8.0}
    for name, (base, spread) in spreads.items():
        noise = np.random.default_rng([zlib.crc32(name.encode()), seed]).standard_normal(out[name].shape)
        drawn = base * np.exp(spread * noise) if base else spread * noise
        out[name] = jnp.asarray(drawn.astype(out[name].dtype))
    for name, factor in factors.items():
        out[name] = (out[name] * factor).astype(out[name].dtype)
    return out
```

```python
import math
from contextlib import ExitStack

import numpy as np
import concourse.bass as bass
from concourse import mybir

FP32 = mybir.dt.float32
FP32R = mybir.dt.float32r
U8 = mybir.dt.uint8
U32 = mybir.dt.uint32
ALU = mybir.AluOpType
ACT = mybir.ActivationFunctionType
AX = mybir.AxisListType

P = 128
B, S, D = 4, 1024, 512
TT = S // P
KC = D // P
NBLK = S // 512
EPS = 1e-5
HI, LO = 0, 1
PARTS = ((HI, HI), (HI, LO), (LO, HI))
STRIDE = 4
HD = 32
GH = P // HD
KEYS = S // STRIDE
KT = KEYS // P
E, H, R = 8, 128, 64


def ahead(b):
    return isinstance(b, int) and b < 0


def self_attention(nc, x, wqT, wkT, wvT, bq, bk, bv, ident_in, causal_in, x1):
    scale = 1.0 / math.sqrt(D)
    RING = 3
    PT_UNITS = [-(-(i + 1) // 4) for i in range(TT)]
    K0, V0 = 0, KC * NBLK
    Q0 = V0 + TT

    def plan(prefetch):
        at, k = {("q", 0): Q0}, Q0 + KC
        for i in range(TT):
            if i == TT // 2 - 1:
                at["q", 1] = k
                k += KC
            at["pt", i] = k
            k += PT_UNITS[i]
            if prefetch and i >= TT // 2:
                at["ln", 2 * (i - TT // 2)] = k
                at["ln", 2 * (i - TT // 2) + 1] = k + 1
                k += 2
        return at, k

    LOOPED, PER = plan(True)
    LAST, _ = plan(False)
    assert PER % RING == TT % RING

    def order(b, *what):
        return (LAST if isinstance(b, int) and b == B - 1 else LOOPED)[what]

    ctx = ExitStack()
    with ctx:
        def sb(name, shape, dt=FP32):
            return ctx.enter_context(nc.sbuf_tensor("a_" + name, shape, dt))

        def sem(name):
            return ctx.enter_context(nc.semaphore("a_" + name))

        wq = sb("wq", [P, 2, KC, D], FP32R)
        wk = sb("wk", [P, 2, KC, D], FP32R)
        wv = sb("wv", [P, 2, KC, D], FP32R)
        zT = sb("zT", [P, 2, KC, S], FP32R)
        kT = sb("kT", [P, 2, KC, S], FP32R)
        v = sb("v", [P, 2, TT, D], FP32R)
        qT = sb("qT", [P, 2, KC, 512], FP32R)
        probs = sb("probs", [P, 2, S])
        stage = probs[:, :, :].rearrange("p a s -> p (a s)").rearrange("p (c n) -> p c n", c=KC)
        pT = sb("pT", [P, 2, 2, TT, P], FP32R)
        xln = sb("xln", [P, 2, D])
        z = sb("z", [P, 2, D])
        xres = sb("xres", [P, 2, D])
        xout = xres
        bv_rep = sb("bv_rep", [P, D])
        ident = sb("ident", [P, P])
        causal = sb("causal", [P, P])
        bqk = sb("bqk", [P, 2, KC])
        stats = sb("stats", [P, 2, 6])
        mv = sb("mv", [P, 2, 2])
        rstd = sb("rstd", [P, 2, 2])
        half = sb("half", [P, 1])
        mx = sb("mx", [P, TT])
        nbias = sb("nbias", [P, TT])
        rowsum = sb("rowsum", [P, TT])
        rinv = sb("rinv", [P, TT])

        ring = ctx.enter_context(nc.psum_tensor("a_ring", [P, RING, 512], FP32))
        zacc = ctx.enter_context(nc.psum_tensor("a_zacc", [P, 512], FP32))
        scores = ctx.enter_context(nc.psum_tensor("a_scores", [P, 2, S], FP32))

        waited = sem("waited")
        consts = sem("consts")
        w_loaded = sem("w_loaded")
        w_hi = sem("w_hi")
        w_lo = sem("w_lo")
        half_set = sem("half_set")
        xln_in = [sem(f"xln_in{j}") for j in range(2)]
        xres_in = [sem(f"xres_in{j}") for j in range(2)]
        stored = [sem(f"stored{j}") for j in range(2)]
        stats_done = sem("stats_done")
        mv_done = sem("mv_done")
        var_eps = sem("var_eps")
        rstd_done = sem("rstd_done")
        z_done = sem("z_done")
        unit_full = sem("unit_full")
        hi_done = sem("hi_done")
        lo_done = sem("lo_done")
        s_full = sem("s_full")
        masked = sem("masked")
        max_done = sem("max_done")
        nbias_done = sem("nbias_done")
        p_done = sem("p_done")
        rinv_done = sem("rinv_done")
        zacc_full = sem("zacc_full")
        combined = sem("combined")
        xb_done = sem("xb_done")
        block = ctx.enter_context(nc.Block())

        def G(b, k):
            return k if ahead(b) else TT + b * PER + k

        def lag(k):
            return RING if k >= RING else k + 1 + (TT - 1 - k) % RING

        def carry(engine):
            engine.sem_inc(waited, 1)

        @block.sync
        def _(sp):
            for j in range(2):
                sp.sem_inc(stored[j], 16)
            sp.dma_start(ident[:, :], ident_in).then_inc(consts, 16)
            sp.dma_start(causal[:, :], causal_in).then_inc(consts, 16)
            sp.dma_start(bqk[:, 0, :], bq).then_inc(consts, 16)
            sp.dma_start(bqk[:, 1, :], bk).then_inc(consts, 16)
            sp.dma_start(bv_rep[:, :], bv.partition_broadcast(P)).then_inc(consts, 16)

            def load_ln(b, t):
                if not ahead(b) or t >= 2:
                    sp.wait_ge(z_done, (b + 1) * TT + t - 1)
                sp.dma_start(xln[:, t % 2, :], x[bass.ds((b + 1) * TT + t, 1), :, :].rearrange("o p d -> (o p) d")
                             ).then_inc(xln_in[t % 2], 16)

            load_ln(-1, 0)
            load_ln(-1, 1)
            for w, src in enumerate((wkT, wvT, wqT)):
                if w:
                    sp.wait_ge(w_lo, w)
                sp.dma_start(stage, src).then_inc(w_loaded, 16)
            for t in range(2, TT):
                load_ln(-1, t)

            def store(b, i):
                sp.wait_ge(combined, 1 + b * TT + i + 1)
                sp.dma_start(x1[bass.ds(b * TT + i, 1), :, :].rearrange("o p d -> (o p) d"),
                             xout[:, i % 2, :]).then_inc(stored[i % 2], 16)

            def batch(b, prefetch):
                for i in range(TT):
                    sp.wait_ge(stored[i % 2], 16 + 16 * (b * (TT // 2) + i // 2))
                    sp.dma_start(xres[:, i % 2, :], x[bass.ds(b * TT + i, 1), :, :].rearrange("o p d -> (o p) d")
                                 ).then_inc(xres_in[i % 2], 16)
                    if prefetch and i >= TT // 2:
                        load_ln(b, 2 * (i - TT // 2))
                        load_ln(b, 2 * (i - TT // 2) + 1)
                    if i >= 1:
                        store(b, i - 1)
                store(b, TT - 1)

            with sp.Fori(0, B - 1) as b:
                batch(b, True)
            batch(B - 1, False)
            for j in range(2):
                sp.wait_ge(stored[j], 16 + 16 * B * TT // 2)

        @block.gpsimd
        def _(pool):
            nc.gpsimd.memset(half[:, :], -0.5).then_inc(half_set, 1)
            pool.wait_ge(half_set, 1)
            pool.wait_ge(consts, 16 * 5)

            def ln_rstd(b, t):
                n = (b + 1) * TT + t
                pool.wait_ge(mv_done, n + 1)
                carry(pool)
                nc.gpsimd.tensor_scalar(rstd[:, t % 2, 0:1], mv[:, t % 2, 1:2], EPS, None, ALU.add
                                        ).then_inc(var_eps, 1)
                pool.wait_ge(var_eps, n + 1)
                nc.gpsimd.tensor_tensor(rstd[:, t % 2, 1:2], rstd[:, t % 2, 0:1], half[:, :], ALU.pow
                                        ).then_inc(rstd_done, 1)

            def add_bv(b, i):
                pool.wait_ge(xres_in[i % 2], 16 * (b * (TT // 2) + i // 2 + 1))
                nc.gpsimd.tensor_tensor(xres[:, i % 2, :], xres[:, i % 2, :], bv_rep[:, :], ALU.add
                                        ).then_inc(xb_done, 1)

            def batch(b, prefetch):
                for i in range(TT):
                    add_bv(b, i)
                    if prefetch and i >= TT // 2:
                        ln_rstd(b, 2 * (i - TT // 2))
                        ln_rstd(b, 2 * (i - TT // 2) + 1)

            for t in range(TT):
                ln_rstd(-1, t)
            with pool.Fori(0, B - 1) as b:
                batch(b, True)
            batch(B - 1, False)

        @block.scalar
        def _(act):
            act.sem_inc(p_done, 1)
            act.wait_ge(consts, 16 * 5)

            def evacuate(b, k, out, bias=None):
                act.wait_ge(unit_full, G(b, k) + 1)
                src = ring[:, k % RING, :]
                if len(out.shape) == 3:
                    src = src.rearrange("p (c n) -> p c n", n=P)[:, 0:out.shape[1], :]
                if bias is None:
                    nc.scalar.copy(out, src).then_inc(hi_done, 1)
                else:
                    nc.scalar.activation(out, src, ACT.Identity, bias=bias).then_inc(hi_done, 1)

            def split_w(w, dst):
                act.wait_ge(w_loaded, 16 * (w + 1))
                nc.scalar.copy(dst[:, HI, :, :], stage).then_inc(w_hi, 1)

            def ln_unit(b, t):
                evacuate(b, t if ahead(b) else order(b, "ln", t), zT[:, HI, :, t * P:(t + 1) * P])

            def softmax_exp(b, i):
                n = (i + 1) * P
                act.wait_ge(nbias_done, b * TT + i + 1)
                nc.scalar.activation(probs[:, i % 2, 0:n], scores[:, i % 2, 0:n], ACT.Exp, scale=scale,
                                     bias=nbias[:, i:i + 1], accum_out=rowsum[:, i:i + 1]).then_inc(p_done, 1)

            def pt_units(b, i):
                act.wait_ge(zacc_full, 1 + (b * TT + i - 1 if i >= 2 else b * TT))
                for u in range(PT_UNITS[i]):
                    m = min(4, i + 1 - 4 * u)
                    evacuate(b, order(b, "pt", i) + u, pT[:, i % 2, HI, 4 * u:4 * u + m, :])

            def batch(b, prefetch):
                act.wait_ge(s_full, 1 + b * TT)
                for c in range(KC):
                    for n in range(NBLK):
                        evacuate(b, K0 + c * NBLK + n, kT[:, HI, c, n * 512:(n + 1) * 512], bqk[:, 1, c:c + 1])
                act.wait_ge(zacc_full, 1 + b * TT)
                for t in range(TT):
                    evacuate(b, V0 + t, v[:, HI, t, :])
                for c in range(KC):
                    evacuate(b, order(b, "q", 0) + c, qT[:, HI, c, :], bqk[:, 0, c:c + 1])
                softmax_exp(b, 0)
                for i in range(TT):
                    if i == TT // 2 - 1:
                        act.wait_ge(s_full, 1 + b * TT + TT // 2)
                        for c in range(KC):
                            evacuate(b, order(b, "q", 1) + c, qT[:, HI, c, :], bqk[:, 0, c:c + 1])
                    pt_units(b, i)
                    if prefetch and i >= TT // 2:
                        ln_unit(b, 2 * (i - TT // 2))
                        ln_unit(b, 2 * (i - TT // 2) + 1)
                    if i + 1 < TT:
                        softmax_exp(b, i + 1)

            split_w(0, wk)
            split_w(1, wv)
            split_w(2, wq)
            for t in range(TT):
                ln_unit(-1, t)
            with act.Fori(0, B - 1) as b:
                batch(b, True)
            batch(B - 1, False)

        @block.vector
        def _(dve):
            dve.sem_inc(combined, 1)
            dve.wait_ge(consts, 16 * 5)

            def remainder(b, k, out, hi, bias=None):
                dve.wait_ge(hi_done, G(b, k) + 1)
                src = ring[:, k % RING, :]
                if len(out.shape) == 3:
                    src = src.rearrange("p (c n) -> p c n", n=P)[:, 0:out.shape[1], :]
                hi = hi.bitcast(FP32)
                if bias is None:
                    nc.vector.tensor_tensor(out, src, hi, ALU.subtract).then_inc(lo_done, 1)
                else:
                    nc.vector.scalar_tensor_tensor(out, src, bias, hi, ALU.add, ALU.subtract).then_inc(lo_done, 1)

            def split_w(w, dst):
                dve.wait_ge(w_hi, w + 1)
                nc.vector.tensor_tensor(dst[:, LO, :, :], stage, dst[:, HI, :, :].bitcast(FP32), ALU.subtract
                                        ).then_inc(w_lo, 1)

            def ln_stats(b, t):
                n = (b + 1) * TT + t
                dve.wait_ge(xln_in[t % 2], 16 * ((b + 1) * (TT // 2) + t // 2 + 1))
                nc.vector.bn_stats(stats[:, t % 2, :], xln[:, t % 2, :]).then_inc(stats_done, 1)
                dve.wait_ge(stats_done, n + 1)
                carry(dve)
                nc.vector.bn_aggr(mv[:, t % 2, :], stats[:, t % 2, :]).then_inc(mv_done, 1)

            def ln_apply(b, t):
                n = (b + 1) * TT + t
                dve.wait_ge(rstd_done, n + 1)
                nc.vector.tensor_scalar(z[:, t % 2, :], xln[:, t % 2, :], mv[:, t % 2, 0:1], rstd[:, t % 2, 1:2],
                                        ALU.subtract, ALU.mult).then_inc(z_done, 1)

            def ln_unit(b, t):
                k = t if ahead(b) else order(b, "ln", t)
                at = slice(t * P, (t + 1) * P)
                remainder(b, k, zT[:, LO, :, at], zT[:, HI, :, at])

            def row_max(b, i):
                n = (i + 1) * P
                dve.wait_ge(s_full, 1 + b * TT + i + 1)
                nc.vector.tensor_tensor(scores[:, i % 2, n - P:n], scores[:, i % 2, n - P:n], causal[:, :], ALU.add
                                        ).then_inc(masked, 1)
                dve.wait_ge(masked, b * TT + i + 1)
                nc.vector.tensor_reduce(mx[:, i:i + 1], scores[:, i % 2, 0:n], AX.X, ALU.max).then_inc(max_done, 1)
                dve.wait_ge(max_done, b * TT + i + 1)
                nc.vector.tensor_scalar(nbias[:, i:i + 1], mx[:, i:i + 1], -scale, None, ALU.mult
                                        ).then_inc(nbias_done, 1)

            def pt_units(b, i):
                for u in range(PT_UNITS[i]):
                    m = min(4, i + 1 - 4 * u)
                    at = slice(4 * u, 4 * u + m)
                    remainder(b, order(b, "pt", i) + u, pT[:, i % 2, LO, at, :], pT[:, i % 2, HI, at, :])

            def combine(b, i):
                dve.wait_ge(p_done, 1 + b * TT + i + 1)
                nc.vector.reciprocal(rinv[:, i:i + 1], rowsum[:, i:i + 1]).then_inc(rinv_done, 1)
                dve.wait_ge(rinv_done, b * TT + i + 1)
                dve.wait_ge(xb_done, b * TT + i + 1)
                dve.wait_ge(zacc_full, 1 + b * TT + i + 1)
                nc.vector.scalar_tensor_tensor(xout[:, i % 2, :], zacc[:, :], rinv[:, i:i + 1], xres[:, i % 2, :],
                                               ALU.mult, ALU.add).then_inc(combined, 1)

            def batch(b, prefetch):
                for c in range(KC):
                    for n in range(NBLK):
                        at = slice(n * 512, (n + 1) * 512)
                        remainder(b, K0 + c * NBLK + n, kT[:, LO, c, at], kT[:, HI, c, at], bqk[:, 1, c:c + 1])
                for t in range(TT):
                    remainder(b, V0 + t, v[:, LO, t, :], v[:, HI, t, :])
                for c in range(KC):
                    remainder(b, order(b, "q", 0) + c, qT[:, LO, c, :], qT[:, HI, c, :], bqk[:, 0, c:c + 1])
                row_max(b, 0)
                for i in range(TT):
                    if i == TT // 2 - 1:
                        for c in range(KC):
                            remainder(b, order(b, "q", 1) + c, qT[:, LO, c, :], qT[:, HI, c, :], bqk[:, 0, c:c + 1])
                    if i + 1 < TT:
                        row_max(b, i + 1)
                    if prefetch and i >= TT // 2:
                        t = 2 * (i - TT // 2)
                        ln_stats(b, t)
                        ln_stats(b, t + 1)
                        ln_apply(b, t)
                        ln_apply(b, t + 1)
                    pt_units(b, i)
                    if prefetch and i >= TT // 2:
                        ln_unit(b, t)
                        ln_unit(b, t + 1)
                    if i >= 1:
                        combine(b, i - 1)
                combine(b, TT - 1)

            split_w(0, wk)
            split_w(1, wv)
            split_w(2, wq)
            ln_stats(-1, 0)
            for t in range(TT):
                if t + 1 < TT:
                    ln_stats(-1, t + 1)
                ln_apply(-1, t)
                ln_unit(-1, t)
            with dve.Fori(0, B - 1) as b:
                batch(b, True)
            batch(B - 1, False)

        @block.tensor
        def _(pe):
            pe.sem_inc(zacc_full, 1)
            pe.sem_inc(s_full, 1)
            pe.wait_ge(consts, 16 * 5)

            def bank(b, k):
                if not (ahead(b) and k < RING):
                    pe.wait_ge(lo_done, G(b, k) - lag(k) + 1)
                return ring[:, k % RING, :]

            def product(out, lhs, rhs):
                for c in range(KC):
                    for n, (a, r) in enumerate(PARTS):
                        last = nc.tensor.matmul(out, lhs(a, c), rhs(r, c), start=(c == 0 and n == 0),
                                                stop=(c == KC - 1 and n == len(PARTS) - 1))
                return last

            def transpose_z(b, t):
                out = bank(b, t if ahead(b) else order(b, "ln", t))
                pe.wait_ge(z_done, (b + 1) * TT + t + 1)
                for c in range(KC):
                    last = nc.tensor.transpose(out[:, c * P:(c + 1) * P], z[:, t % 2, c * P:(c + 1) * P], ident[:, :])
                last.then_inc(unit_full, 1)

            def score(b, i):
                if i == 0:
                    pe.wait_ge(lo_done, G(b, order(b, "q", 0) + KC - 1) + 1)
                if i == TT // 2:
                    pe.wait_ge(lo_done, G(b, order(b, "q", 1) + KC - 1) + 1)
                pe.wait_ge(p_done, 1 + (b * TT + i - 1 if i >= 2 else b * TT))
                q = slice((i % 4) * P, (i % 4 + 1) * P)
                for at in range(0, (i + 1) * P, 512):
                    n = at + min(512, max(256, (i + 1) * P - at))
                    last = product(scores[:, i % 2, at:n], lambda a, c: qT[:, a, c, q],
                                   lambda r, c: kT[:, r, c, at:n])
                last.then_inc(s_full, 1)

            def transpose_p(b, i):
                pe.wait_ge(p_done, 1 + b * TT + i + 1)
                for u in range(PT_UNITS[i]):
                    out = bank(b, order(b, "pt", i) + u)
                    for j in range(4 * u, min(4 * u + 4, i + 1)):
                        last = nc.tensor.transpose(out[:, (j % 4) * P:(j % 4 + 1) * P],
                                                   probs[:, i % 2, j * P:(j + 1) * P], ident[:, :])
                    last.then_inc(unit_full, 1)

            def times_v(b, i):
                pe.wait_ge(lo_done, G(b, order(b, "pt", i) + PT_UNITS[i]))
                pe.wait_ge(combined, 1 + b * TT + i)
                for j in range(i + 1):
                    for n, (a, r) in enumerate(PARTS):
                        last = nc.tensor.matmul(zacc[:, :], pT[:, i % 2, a, j, :], v[:, r, j, :],
                                                start=(j == 0 and n == 0), stop=(j == i and n == len(PARTS) - 1))
                last.then_inc(zacc_full, 1)

            def q_units(b, blk):
                for c in range(KC):
                    out = bank(b, order(b, "q", blk) + c)
                    product(out, lambda a, d: wq[:, a, d, c * P:(c + 1) * P],
                            lambda r, d: zT[:, r, d, blk * 512:(blk + 1) * 512]).then_inc(unit_full, 1)

            def batch(b, prefetch):
                pe.wait_ge(lo_done, G(b, 0))
                for c in range(KC):
                    for n in range(NBLK):
                        out = bank(b, K0 + c * NBLK + n)
                        product(out, lambda a, d: wk[:, a, d, c * P:(c + 1) * P],
                                lambda r, d: zT[:, r, d, n * 512:(n + 1) * 512]).then_inc(unit_full, 1)
                for t in range(TT):
                    out = bank(b, V0 + t)
                    product(out, lambda a, d: zT[:, a, d, t * P:(t + 1) * P],
                            lambda r, d: wv[:, r, d, :]).then_inc(unit_full, 1)
                q_units(b, 0)
                score(b, 0)
                for i in range(TT):
                    if i == TT // 2 - 1:
                        q_units(b, 1)
                    if i + 1 < TT:
                        score(b, i + 1)
                    transpose_p(b, i)
                    if prefetch and i >= TT // 2:
                        transpose_z(b, 2 * (i - TT // 2))
                        transpose_z(b, 2 * (i - TT // 2) + 1)
                    if i >= 1:
                        times_v(b, i - 1)
                times_v(b, TT - 1)

            for t in range(TT):
                transpose_z(-1, t)
            pe.wait_ge(w_lo, 3)
            with pe.Fori(0, B - 1) as b:
                batch(b, True)
            batch(B - 1, False)


def cross_keys_values(nc, ctxT, wkT, wvT, bk, bv, ident_in, k_out, v_out):
    ctx = ExitStack()
    with ctx:
        def sb(name, shape, dt=FP32):
            return ctx.enter_context(nc.sbuf_tensor("kv_" + name, shape, dt))

        def sem(name):
            return ctx.enter_context(nc.semaphore("kv_" + name))

        wk = sb("wk", [P, 2, KC, D], FP32R)
        wv = sb("wv", [P, 2, KC, D], FP32R)
        raw = sb("raw", [P, 2, KC, STRIDE * KEYS])
        c_hl = sb("c_hl", [P, 2, KC, STRIDE * KEYS], FP32R)
        k_hl = sb("k_hl", [P, 2, 2, KEYS], FP32R)
        vT = sb("vT", [P, 2, KEYS])
        v_sb = sb("v_sb", [P, 2, KT, P])
        bkv = sb("bkv", [P, 2, STRIDE])
        ident = sb("ident", [P, P])
        k_ps = [ctx.enter_context(nc.psum_tensor(f"kv_k{i}", [P, KEYS], FP32)) for i in range(2)]
        vT_ps = [ctx.enter_context(nc.psum_tensor(f"kv_vT{i}", [P, KEYS], FP32)) for i in range(2)]
        v_ps = [ctx.enter_context(nc.psum_tensor(f"kv_v{i}", [P, KT * P], FP32)) for i in range(2)]

        consts = sem("consts")
        w_loaded = sem("w_loaded")
        w_hi = sem("w_hi")
        w_lo = sem("w_lo")
        raw_in = sem("raw_in")
        c_hi = sem("c_hi")
        c_lo = sem("c_lo")
        k_full = sem("k_full")
        k_hi = sem("k_hi")
        k_lo = sem("k_lo")
        vT_full = sem("vT_full")
        vT_done = sem("vT_done")
        v_full = sem("v_full")
        v_done = sem("v_done")
        k_stored = [sem(f"k_stored{i}") for i in range(2)]
        v_stored = [sem(f"v_stored{i}") for i in range(2)]
        block = ctx.enter_context(nc.Block())
        R = STRIDE

        @block.sync
        def _(sp):
            for j in range(2):
                sp.sem_inc(k_stored[j], 16)
            for j in range(2):
                sp.sem_inc(v_stored[j], 16)
            sp.dma_start(ident[:, :], ident_in).then_inc(consts, 16)
            sp.dma_start(bkv[:, 0, :], bk).then_inc(consts, 16)
            sp.dma_start(bkv[:, 1, :], bv).then_inc(consts, 16)
            for w, src in enumerate((wkT, wvT)):
                sp.dma_start(raw[:, w, :, 0:D], src).then_inc(w_loaded, 16)
            sp.wait_ge(w_lo, 2)
            sp.dma_start(raw[:, 0, :, :], ctxT[0]).then_inc(raw_in, 16)

            def batch(b, prefetch):
                if prefetch:
                    sp.wait_ge(c_lo, b + 1)
                    sp.dma_start(raw[:, 0, :, :], ctxT[bass.ds(b + 1, 1), :, :, :].rearrange("o p c s -> p (o c) s")
                                 ).then_inc(raw_in, 16)
                for r in range(R):
                    n = b * R + r
                    sp.wait_ge(k_lo, 1 + n + 1)
                    sp.dma_start(k_out[bass.ds(n, 1), :, :, :].rearrange("o p h s -> p (o h) s"),
                                 k_hl[:, r % 2, :, :].bitcast(FP32)).then_inc(k_stored[r % 2], 16)
                    sp.wait_ge(v_done, 1 + n + 1)
                    sp.dma_start(v_out[bass.ds(n, 1), :, :, :].rearrange("o p c d -> p (o c) d"),
                                 v_sb[:, r % 2, :, :]).then_inc(v_stored[r % 2], 16)

            with sp.Fori(0, B - 1) as b:
                batch(b, True)
            batch(B - 1, False)
            for i in range(2):
                sp.wait_ge(k_stored[i], 16 + 16 * B * R // 2)
                sp.wait_ge(v_stored[i], 16 + 16 * B * R // 2)

        @block.scalar
        def _(act):
            act.sem_inc(vT_done, 1)
            act.wait_ge(consts, 48)
            for w, dst in enumerate((wk, wv)):
                act.wait_ge(w_loaded, 32)
                nc.scalar.copy(dst[:, HI, :, :], raw[:, w, :, 0:D]).then_inc(w_hi, 1)
            with act.Fori(0, B) as b:
                act.wait_ge(raw_in, 16 * b + 16)
                act.wait_ge(vT_full, 1 + b * R)
                nc.scalar.copy(c_hl[:, HI, :, :], raw[:, 0, :, :]).then_inc(c_hi, 1)
                for r in range(R):
                    n = b * R + r
                    act.wait_ge(k_full, n + 1)
                    act.wait_ge(k_stored[r % 2], 16 + 16 * (b * (R // 2) + r // 2))
                    nc.scalar.activation(k_hl[:, r % 2, HI, :], k_ps[r % 2][:, :], ACT.Identity,
                                         bias=bkv[:, 0, r:r + 1]).then_inc(k_hi, 1)
                    act.wait_ge(vT_full, 1 + n + 1)
                    act.wait_ge(v_full, 1 + (n - 1 if r >= 2 else b * R))
                    nc.scalar.activation(vT[:, r % 2, :], vT_ps[r % 2][:, :], ACT.Identity,
                                         bias=bkv[:, 1, r:r + 1]).then_inc(vT_done, 1)

        @block.vector
        def _(dve):
            dve.sem_inc(k_lo, 1)
            dve.sem_inc(v_done, 1)
            dve.wait_ge(consts, 48)
            for w, dst in enumerate((wk, wv)):
                dve.wait_ge(w_hi, w + 1)
                nc.vector.tensor_tensor(dst[:, LO, :, :], raw[:, w, :, 0:D], dst[:, HI, :, :].bitcast(FP32),
                                        ALU.subtract).then_inc(w_lo, 1)
            with dve.Fori(0, B) as b:
                dve.wait_ge(c_hi, b + 1)
                nc.vector.tensor_tensor(c_hl[:, LO, :, :], raw[:, 0, :, :], c_hl[:, HI, :, :].bitcast(FP32),
                                        ALU.subtract).then_inc(c_lo, 1)
                for r in range(R):
                    n = b * R + r
                    dve.wait_ge(k_hi, n + 1)
                    nc.vector.scalar_tensor_tensor(k_hl[:, r % 2, LO, :], k_ps[r % 2][:, :], bkv[:, 0, r:r + 1],
                                                   k_hl[:, r % 2, HI, :].bitcast(FP32), ALU.add, ALU.subtract
                                                   ).then_inc(k_lo, 1)
                    dve.wait_ge(v_full, 1 + n + 1)
                    dve.wait_ge(v_stored[r % 2], 16 + 16 * (b * (R // 2) + r // 2))
                    nc.vector.tensor_copy(v_sb[:, r % 2, :, :], v_ps[r % 2][:, :].rearrange("p (c d) -> p c d", d=P)
                                          ).then_inc(v_done, 1)

        @block.tensor
        def _(pe):
            pe.sem_inc(vT_full, 1)
            pe.sem_inc(v_full, 1)
            pe.wait_ge(consts, 48)

            def project(out, w, r):
                for c in range(KC):
                    for n, (a, h) in enumerate(PARTS):
                        last = nc.tensor.matmul(out, w[:, a, c, r * P:(r + 1) * P],
                                                c_hl[:, h, c, r * KEYS:(r + 1) * KEYS],
                                                start=(c == 0 and n == 0), stop=(c == KC - 1 and n == 2))
                return last

            with pe.Fori(0, B) as b:
                pe.wait_ge(c_lo, b + 1)
                for r in range(R):
                    n = b * R + r
                    pe.wait_ge(k_lo, 1 + (n - 1 if r >= 2 else b * R))
                    project(k_ps[r % 2][:, :], wk, r).then_inc(k_full, 1)
                    pe.wait_ge(vT_done, 1 + (n - 1 if r >= 2 else b * R))
                    project(vT_ps[r % 2][:, :], wv, r).then_inc(vT_full, 1)
                    pe.wait_ge(vT_done, 1 + n + 1)
                    pe.wait_ge(v_done, 1 + (n - 1 if r >= 2 else b * R))
                    for c in range(KT):
                        last = nc.tensor.transpose(v_ps[r % 2][:, c * P:(c + 1) * P],
                                                   vT[:, r % 2, c * P:(c + 1) * P], ident[:, :])
                    last.then_inc(v_full, 1)


def cross_attention(nc, x1, wqT, woT, bq, bo, mask, k_in, v_in, ident_in, x2):
    scale = float(HD) ** -0.5
    QT = 4
    NG = NBLK * STRIDE
    NH = NG * GH
    RING = 3
    SRING = 4
    PBUF = 4
    STACKED = 16 * 4 * GH
    SPH = QT // 2
    ACT_PT = ((1, 1), (3, 1))

    def plan(prefetch, first=False):
        units = []

        def ln(blk):
            return [(("z", blk, t), "dve") for t in range(QT)]

        if first:
            units += ln(0) + [(("q", 0), "dve"), (("q", 1), "dve")]
        else:
            for n in range(NG):
                for j in range(GH):
                    if n % 4 == 2 and (n < 4 or prefetch):
                        blk = n // 4 + 1
                        units += ln(blk)[j:j + 1] if j < 2 else ln(blk)[2:4] if j == 2 else []
                    if j == 1 and n >= 1:
                        units += [(("r", n - 1), "act")]
                    for c in range(KT):
                        units += [(("pt", n, j, c), "act" if (j, c) in ACT_PT else "dve")]
                    if j == GH - 1 and (n + 2 < NG or prefetch):
                        units += [(("q", n + 2), "dve")]
                    if n == STRIDE and j == GH - 1:
                        units += [(("o", 0, t), "dve") for t in range(QT)]
            units += [(("r", NG - 1), "act")] + [(("o", 1, t), "dve") for t in range(QT)]
        table, acts, dves, hist = {}, 0, 0, []
        for i, (what, eng) in enumerate(units):
            hi = what[0] in "zq"
            acts += hi or eng == "act"
            dves += eng == "dve"
            freed = hist[i - RING] if i >= RING else None
            hist.append((eng, acts if eng == "act" else dves))
            table[what] = dict(i=i, bank=i % RING, act=acts, dve=dves, eng=eng, freed=freed)
        return table, len(units), acts, dves

    FIRST, LOOPED, LAST = plan(False, True), plan(True), plan(False)

    def of(b):
        return FIRST if ahead(b) else LAST if isinstance(b, int) and b == B - 1 else LOOPED

    def base(b, which):
        return 0 if ahead(b) else FIRST[which] + b * LOOPED[which]

    ctx = ExitStack()
    with ctx:
        def sb(name, shape, dt=FP32):
            return ctx.enter_context(nc.sbuf_tensor("x_" + name, shape, dt))

        def sem(name):
            return ctx.enter_context(nc.semaphore("x_" + name))

        wq = sb("wq", [P, 2, KC, D], FP32R)
        wo = sb("wo", [P, 2, KC, D], FP32R)
        k_st = sb("k_st", [P, STRIDE, GH, KEYS], FP32R)
        v_sb = sb("v_sb", [P, STRIDE, KT, P])
        q_hl = sb("q_hl", [P, 2, 2, 512], FP32R)
        q_st = sb("q_st", [P, 2, GH, 512], FP32R)
        zT = sb("zT", [P, 2, KC, 512], FP32R)
        probs = sb("probs", [P, PBUF, QT, KEYS])
        pT = sb("pT", [P, 2, GH, KT, 512])
        ctxn = sb("ctxn", [P, 2, 512])
        r_sb = sb("r_sb", [P, 2, 512])
        cT = sb("cT", [P, 2, STRIDE, 512], FP32R)
        xln = sb("xln", [P, 2, D])
        z = sb("z", [P, 2, D])
        xres = sb("xres", [P, QT, D])
        bo_rep = sb("bo_rep", [P, D])
        ident = sb("ident", [P, P])
        bq_sb = sb("bq_sb", [P, STRIDE])
        mask_u8 = sb("mask_u8", [P, STRIDE, KEYS], U8)
        mask_add = sb("mask_add", [P, STRIDE, KEYS])
        stats = sb("stats", [P, 2, 6])
        mv = sb("mv", [P, 2, 2])
        rstd = sb("rstd", [P, 2, 2])
        half = sb("half", [P, 1])
        mx = sb("mx", [P, PBUF, QT])
        nbias = sb("nbias", [P, PBUF, QT])
        rowsum = sb("rowsum", [P, 2, QT, GH])
        rinv = sb("rinv", [P, 2, QT, GH])
        rinv_rep = sb("rinv_rep", [P, 2, QT, GH, HD])
        w_stage = pT[:, 0, :, :, :].rearrange("p j c q -> p (j c) q")

        ring = ctx.enter_context(nc.psum_tensor("x_ring", [P, RING, 512], FP32))
        sps = ctx.enter_context(nc.psum_tensor("x_sps", [P, SRING, 512], FP32))
        cacc = ctx.enter_context(nc.psum_tensor("x_cacc", [P, 512], FP32))

        waited = sem("waited")
        consts = sem("consts")
        w_loaded = sem("w_loaded")
        w_hi = sem("w_hi")
        w_lo = sem("w_lo")
        half_set = sem("half_set")
        xln_in = [sem(f"xln_in{j}") for j in range(2)]
        xres_in = [sem(f"xres_in{j}") for j in range(QT)]
        stored = [sem(f"stored{j}") for j in range(QT)]
        k_loaded = [sem(f"k_loaded{r}") for r in range(STRIDE)]
        v_loaded = [sem(f"v_loaded{r}") for r in range(STRIDE)]
        mask_in = sem("mask_in")
        mask_done = sem("mask_done")
        q_stacked = [sem(f"q_stacked{j}") for j in range(2)]
        stats_done = sem("stats_done")
        mv_done = sem("mv_done")
        var_eps = sem("var_eps")
        rstd_done = sem("rstd_done")
        z_done = sem("z_done")
        unit_full = sem("unit_full")
        act_done = sem("act_done")
        dve_done = sem("dve_done")
        s_full = sem("s_full")
        max_done = sem("max_done")
        nbias_done = sem("nbias_done")
        p_done = sem("p_done")
        rinv_done = sem("rinv_done")
        rinv_spread = sem("rinv_spread")
        cacc_full = sem("cacc_full")
        ctxn_done = sem("ctxn_done")
        cT_hi = sem("cT_hi")
        cT_lo = sem("cT_lo")
        xb_done = sem("xb_done")
        block = ctx.enter_context(nc.Block())
        NCONST = 4

        def carry(engine):
            engine.sem_inc(waited, 1)

        @block.sync
        def _(sp):
            for j in range(4):
                sp.sem_inc(stored[j], 16)
            sp.dma_start(ident[:, :], ident_in).then_inc(consts, 16)
            sp.dma_start(bq_sb[:, :], bq).then_inc(consts, 16)
            sp.dma_start(bo_rep[:, :], bo.partition_broadcast(P)).then_inc(consts, 16)

            def tile_of(b, blk, t):
                return b * TT + blk * QT + t

            def load_ln(b, blk, t):
                n = tile_of(b, blk, t)
                if not (isinstance(n, int) and n < 2):
                    sp.wait_ge(z_done, n - 1)
                sp.dma_start(xln[:, t % 2, :], x1[bass.ds(n, 1), :, :].rearrange("o p d -> (o p) d")
                             ).then_inc(xln_in[t % 2], 16)

            def load_res(b, blk):
                for t in range(QT):
                    sp.wait_ge(stored[t], 16 + 16 * (b * NBLK + blk))
                    sp.dma_start(xres[:, t, :], x1[bass.ds(tile_of(b, blk, t), 1), :, :].rearrange("o p d -> (o p) d")
                                 ).then_inc(xres_in[t], 16)

            def store(b, blk):
                for t in range(QT):
                    sp.wait_ge(dve_done, base(b, 3) + of(b)[0]["o", blk, t]["dve"])
                    sp.dma_start(x2[bass.ds(tile_of(b, blk, t), 1), :, :].rearrange("o p d -> (o p) d"),
                                 xres[:, t, :]).then_inc(stored[t], 16)

            def load_k(b, r):
                if not (isinstance(b, int) and b == 0):
                    sp.wait_ge(s_full, ((b - 1) * NH + (STRIDE + r + 1) * GH) * SPH)
                for part in range(4):
                    sp.dma_start(k_st[part * HD:(part + 1) * HD, r, :, :].bitcast(FP32),
                                 k_in[bass.ds(b * STRIDE + r, 1), :, part % 2, :].rearrange(
                                     "o (j d) s -> d (o j) s", d=HD)).then_inc(k_loaded[r], 16)

            def load_v(b, r):
                if not (isinstance(b, int) and b == 0):
                    sp.wait_ge(cacc_full, 1 + (b - 1) * NG + STRIDE + r + 1)
                sp.dma_start(v_sb[:, r, :, :], v_in[bass.ds(b * STRIDE + r, 1), :, :, :].rearrange(
                    "o p c d -> p (o c) d")).then_inc(v_loaded[r], 16)

            def load_mask(b):
                sp.dma_start(mask_u8[:, :, :].rearrange("p r s -> p (r s)"), mask[bass.ds(b, 1), :].rearrange(
                    "o s -> (o s)").partition_broadcast(P)).then_inc(mask_in, 16)

            def stack_q(b, n):
                what = of(b)[0]["q", n]
                sp.wait_ge(dve_done, base(b, 3) + what["dve"])
                for part in range(4):
                    for j in range(GH):
                        sp.dma_start(q_st[part * HD:(part + 1) * HD, n % 2, j, :].bitcast(FP32),
                                     q_hl[j * HD:(j + 1) * HD, n % 2, part // 2, :].bitcast(FP32)
                                     ).then_inc(q_stacked[n % 2], 16)

            load_ln(0, 0, 0)
            load_ln(0, 0, 1)
            sp.dma_start(w_stage[:, 0:KC, :], wqT).then_inc(w_loaded, 16)
            sp.dma_start(w_stage[:, KC:2 * KC, :], woT).then_inc(w_loaded, 16)
            load_mask(0)
            for r in range(STRIDE):
                load_k(0, r)
                load_v(0, r)
            load_ln(0, 0, 2)
            load_ln(0, 0, 3)
            stack_q(-1, 0)
            stack_q(-1, 1)

            def batch(b, prefetch):
                stack_q(b, 2)
                load_ln(b, 1, 0)
                load_ln(b, 1, 1)
                stack_q(b, 3)
                load_ln(b, 1, 2)
                load_ln(b, 1, 3)
                stack_q(b, 4)
                load_res(b, 0)
                stack_q(b, 5)
                if prefetch:
                    sp.wait_ge(mask_done, (b + 1) * STRIDE)
                    carry(sp)
                    load_mask(b + 1)
                    load_k(b + 1, 0)
                stack_q(b, 6)
                store(b, 0)
                if prefetch:
                    load_k(b + 1, 1)
                    load_v(b + 1, 0)
                    load_ln(b + 1, 0, 0)
                    load_ln(b + 1, 0, 1)
                stack_q(b, 7)
                load_res(b, 1)
                if prefetch:
                    load_ln(b + 1, 0, 2)
                    load_ln(b + 1, 0, 3)
                    load_k(b + 1, 2)
                    load_v(b + 1, 1)
                    stack_q(b, 8)
                    load_k(b + 1, 3)
                    load_v(b + 1, 2)
                    stack_q(b, 9)
                    load_v(b + 1, 3)
                store(b, 1)

            with sp.Fori(0, B - 1) as b:
                batch(b, True)
            batch(B - 1, False)
            for j in range(QT):
                sp.wait_ge(stored[j], 16 + 16 * B * NBLK)

        def ln_tiles(b, n, j):
            blk = n // 4 + 1
            ts = [j] if j < 2 else [2, 3] if j == 2 else []
            return [(blk, t, b * TT + blk * QT + t) for t in ts]

        @block.gpsimd
        def _(pool):
            pool.sem_inc(cT_lo, 1)
            nc.gpsimd.memset(half[:, :], -0.5).then_inc(half_set, 1)
            pool.wait_ge(half_set, 1)
            pool.wait_ge(consts, 16 * 3)

            def ln_rstd(t, n):
                pool.wait_ge(mv_done, n + 1)
                carry(pool)
                nc.gpsimd.tensor_scalar(rstd[:, t % 2, 0:1], mv[:, t % 2, 1:2], EPS, None, ALU.add
                                        ).then_inc(var_eps, 1)
                pool.wait_ge(var_eps, n + 1)
                nc.gpsimd.tensor_tensor(rstd[:, t % 2, 1:2], rstd[:, t % 2, 0:1], half[:, :], ALU.pow
                                        ).then_inc(rstd_done, 1)

            def add_bo(b, blk):
                for t in range(QT):
                    pool.wait_ge(xres_in[t], 16 * (b * NBLK + blk + 1))
                    nc.gpsimd.tensor_tensor(xres[:, t, :], xres[:, t, :], bo_rep[:, :], ALU.add).then_inc(xb_done, 1)

            def ctx_lo(b, n):
                g = b * NG + n
                pool.wait_ge(cT_hi, g + 1)
                nc.gpsimd.tensor_tensor(cT[:, LO, n % 4, :], ctxn[:, n % 2, :], cT[:, HI, n % 4, :].bitcast(FP32),
                                        ALU.subtract).then_inc(cT_lo, 1)

            def spread(b, n):
                pool.wait_ge(rinv_done, b * NG + n + 1)
                pool.wait_ge(ctxn_done, 1 + b * NG + max(n - 1, 0))
                carry(pool)
                nc.gpsimd.tensor_copy(rinv_rep[:, n % 2, :, :, :].rearrange("p q j d -> p (q j) d"),
                                      rinv[:, n % 2, :, :].rearrange("p q j -> p (q j)")[:, :, None].broadcast_to(
                                          (P, QT * GH, HD))).then_inc(rinv_spread, 1)

            def batch(b, prefetch):
                for n in range(NG):
                    layernorm = n % 4 == 2 and (n < 4 or prefetch)
                    for j in range(GH):
                        if layernorm:
                            for blk, t, m in ln_tiles(b, n, j):
                                ln_rstd(t, m)
                        if j == 0 and n >= 1:
                            spread(b, n - 1)
                        if j == 2 and n >= 1:
                            ctx_lo(b, n - 1)
                    if n == 3:
                        add_bo(b, 0)
                    if n == 7:
                        add_bo(b, 1)
                spread(b, NG - 1)
                ctx_lo(b, NG - 1)

            for t in range(QT):
                ln_rstd(t, t)
            with pool.Fori(0, B - 1) as b:
                batch(b, True)
            batch(B - 1, False)

        @block.scalar
        def _(act):
            act.wait_ge(consts, 16 * 3)

            def unit(b, *what):
                u = of(b)[0][what]
                act.wait_ge(unit_full, base(b, 1) + u["i"] + 1)
                return ring[:, u["bank"], :]

            def z_hi(b, blk, t):
                src = unit(b, "z", blk, t).rearrange("p (c n) -> p c n", n=P)
                nc.scalar.copy(zT[:, HI, :, t * P:(t + 1) * P], src).then_inc(act_done, 1)

            def q_hi(b, n):
                if not ahead(b):
                    act.wait_ge(q_stacked[n % 2], STACKED * (b * (NG // 2) + n // 2))
                nc.scalar.activation(q_hl[:, n % 2, HI, :], unit(b, "q", n), ACT.Identity,
                                     bias=bq_sb[:, n % 4:n % 4 + 1]).then_inc(act_done, 1)

            def exps(b, k):
                act.wait_ge(nbias_done, b * NH + k + 1)
                for q in range(QT):
                    nc.scalar.activation(probs[:, k % PBUF, q, :], probs[:, k % PBUF, q, :], ACT.Exp, scale=scale,
                                         bias=nbias[:, k % PBUF, q:q + 1],
                                         accum_out=rowsum[:, k // GH % 2, q, k % GH:k % GH + 1]).then_inc(p_done, 1)

            def p_copy(b, n, j, c):
                if (j, c) in ACT_PT:
                    src = unit(b, "pt", n, j, c)
                    act.wait_ge(cacc_full, 1 + b * NG + max(n - 1, 0))
                    nc.scalar.copy(pT[:, n % 2, j, c, :], src).then_inc(act_done, 1)

            def r_copy(b, n):
                act.wait_ge(ctxn_done, 1 + b * NG + max(n - 1, 0))
                nc.scalar.copy(r_sb[:, n % 2, :], unit(b, "r", n)).then_inc(act_done, 1)

            def ctx_hi(b, n):
                act.wait_ge(ctxn_done, 1 + b * NG + n + 1)
                nc.scalar.copy(cT[:, HI, n % 4, :], ctxn[:, n % 2, :]).then_inc(cT_hi, 1)

            def batch(b, prefetch):
                for n in range(NG):
                    for j in range(GH):
                        k = n * GH + j
                        if n % 4 == 2 and (n < 4 or prefetch):
                            for blk, t, m in ln_tiles(b, n, j):
                                z_hi(b, blk, t)
                        if j == 1 and n >= 1:
                            r_copy(b, n - 1)
                        for c in range(KT):
                            p_copy(b, n, j, c)
                        if j == 2 and n >= 1:
                            ctx_hi(b, n - 1)
                        if j == GH - 1 and (n + 2 < NG or prefetch):
                            q_hi(b, n + 2)
                        if k + 2 < NH or prefetch:
                            exps(b, k + 2)
                r_copy(b, NG - 1)
                ctx_hi(b, NG - 1)

            for w, dst in enumerate((wq, wo)):
                act.wait_ge(w_loaded, 32)
                nc.scalar.copy(dst[:, HI, :, :], w_stage[:, w * KC:(w + 1) * KC, :]).then_inc(w_hi, 1)
            for t in range(QT):
                z_hi(-1, 0, t)
            q_hi(-1, 0)
            q_hi(-1, 1)
            exps(0, 0)
            exps(0, 1)
            with act.Fori(0, B - 1) as b:
                batch(b, True)
            batch(B - 1, False)

        @block.vector
        def _(dve):
            dve.sem_inc(ctxn_done, 1)
            dve.wait_ge(consts, 16 * 3)

            def unit(b, *what):
                u = of(b)[0][what]
                if what[0] in "zq":
                    dve.wait_ge(act_done, base(b, 2) + u["act"])
                else:
                    dve.wait_ge(unit_full, base(b, 1) + u["i"] + 1)
                return ring[:, u["bank"], :]

            def ln_stats(t, n):
                dve.wait_ge(xln_in[t % 2], 8 * (n - t % 2) + 16)
                nc.vector.bn_stats(stats[:, t % 2, :], xln[:, t % 2, :]).then_inc(stats_done, 1)
                dve.wait_ge(stats_done, n + 1)
                carry(dve)
                nc.vector.bn_aggr(mv[:, t % 2, :], stats[:, t % 2, :]).then_inc(mv_done, 1)

            def ln_apply(t, n):
                dve.wait_ge(rstd_done, n + 1)
                nc.vector.tensor_scalar(z[:, t % 2, :], xln[:, t % 2, :], mv[:, t % 2, 0:1], rstd[:, t % 2, 1:2],
                                        ALU.subtract, ALU.mult).then_inc(z_done, 1)

            def z_lo(b, blk, t):
                src = unit(b, "z", blk, t).rearrange("p (c n) -> p c n", n=P)
                at = slice(t * P, (t + 1) * P)
                nc.vector.tensor_tensor(zT[:, LO, :, at], src, zT[:, HI, :, at].bitcast(FP32), ALU.subtract
                                        ).then_inc(dve_done, 1)

            def q_lo(b, n):
                nc.vector.scalar_tensor_tensor(q_hl[:, n % 2, LO, :], unit(b, "q", n), bq_sb[:, n % 4:n % 4 + 1],
                                               q_hl[:, n % 2, HI, :].bitcast(FP32), ALU.add, ALU.subtract
                                               ).then_inc(dve_done, 1)

            def mask_to_add(b, r):
                dve.wait_ge(mask_in, 16 * (b + 1))
                nc.vector.tensor_scalar(mask_add[:, r, :], mask_u8[:, r, :], -1e30, None, ALU.mult
                                        ).then_inc(mask_done, 1)

            def maxima(b, k):
                r = k // GH % STRIDE
                for q in range(QT):
                    u = k * SPH + q // 2
                    if q % 2 == 0:
                        dve.wait_ge(s_full, b * NH * SPH + u + 1)
                        carry(dve)
                    nc.vector.tensor_tensor_reduce(
                        out=probs[:, k % PBUF, q, :], in0=sps[:, u % SRING, q % 2 * KEYS:(q % 2 + 1) * KEYS],
                        in1=mask_add[:, r, :], scale=1.0, scalar=-3.4e38, op0=ALU.add, op1=ALU.max,
                        accum_out=mx[:, k % PBUF, q:q + 1]).then_inc(max_done, 1)
                dve.wait_ge(max_done, b * NH * QT + (k + 1) * QT)
                nc.vector.tensor_scalar(nbias[:, k % PBUF, :], mx[:, k % PBUF, :], -scale, None, ALU.mult
                                        ).then_inc(nbias_done, 1)

            def p_copy(b, n, j, c):
                if (j, c) not in ACT_PT:
                    src = unit(b, "pt", n, j, c)
                    dve.wait_ge(cacc_full, 1 + b * NG + max(n - 1, 0))
                    nc.vector.tensor_copy(pT[:, n % 2, j, c, :], src).then_inc(dve_done, 1)

            def invert(b, n):
                dve.wait_ge(p_done, (b * NH + (n + 1) * GH) * QT)
                nc.vector.reciprocal(rinv[:, n % 2, :, :], rowsum[:, n % 2, :, :]).then_inc(rinv_done, 1)

            def normalise(b, n):
                dve.wait_ge(act_done, base(b, 2) + of(b)[0]["r", n]["act"])
                dve.wait_ge(cacc_full, 1 + b * NG + n + 1)
                dve.wait_ge(cT_lo, 1 + b * NG + max(n - 1, 0))
                nc.vector.tensor_tensor(ctxn[:, n % 2, :], cacc[:, :], r_sb[:, n % 2, :], ALU.mult
                                        ).then_inc(ctxn_done, 1)

            def output(b, blk, t):
                src = unit(b, "o", blk, t)
                dve.wait_ge(xb_done, (b * NBLK + blk) * QT + t + 1)
                nc.vector.tensor_tensor(xres[:, t, :], src, xres[:, t, :], ALU.add).then_inc(dve_done, 1)

            def batch(b, prefetch):
                for n in range(NG):
                    for j in range(GH):
                        k = n * GH + j
                        if k + 2 < NH or prefetch:
                            if j == 2 and n >= 4 and prefetch:
                                mask_to_add(b + 1, n - 4)
                            maxima(b, k + 2)
                        if n % 4 == 2 and (n < 4 or prefetch):
                            tiles = ln_tiles(b, n, j)
                            for blk, t, m in tiles:
                                ln_stats(t, m)
                            for blk, t, m in tiles:
                                ln_apply(t, m)
                            for blk, t, m in tiles:
                                z_lo(b, blk, t)
                        if j == 0 and n >= 1:
                            invert(b, n - 1)
                        for c in range(KT):
                            p_copy(b, n, j, c)
                        if j == 1 and n >= 1:
                            normalise(b, n - 1)
                        if j == GH - 1 and (n + 2 < NG or prefetch):
                            q_lo(b, n + 2)
                        if n == STRIDE and j == GH - 1:
                            for t in range(QT):
                                output(b, 0, t)
                invert(b, NG - 1)
                normalise(b, NG - 1)
                for t in range(QT):
                    output(b, 1, t)

            for w, dst in enumerate((wq, wo)):
                dve.wait_ge(w_hi, w + 1)
                nc.vector.tensor_tensor(dst[:, LO, :, :], w_stage[:, w * KC:(w + 1) * KC, :],
                                        dst[:, HI, :, :].bitcast(FP32), ALU.subtract).then_inc(w_lo, 1)
            for r in range(STRIDE):
                mask_to_add(0, r)
            for t in range(QT):
                ln_stats(t, t)
                ln_apply(t, t)
                z_lo(-1, 0, t)
            q_lo(-1, 0)
            q_lo(-1, 1)
            maxima(0, 0)
            maxima(0, 1)
            with dve.Fori(0, B - 1) as b:
                batch(b, True)
            batch(B - 1, False)

        @block.tensor
        def _(pe):
            pe.sem_inc(cacc_full, 1)
            pe.wait_ge(consts, 16 * 3)

            def bank(b, *what):
                u = of(b)[0][what]
                if u["freed"]:
                    eng, count = u["freed"]
                    if eng == "act":
                        pe.wait_ge(act_done, base(b, 2) + count)
                    else:
                        pe.wait_ge(dve_done, base(b, 3) + count)
                return ring[:, u["bank"], :]

            def product(out, lhs, rhs):
                for c in range(KC):
                    for n, (a, r) in enumerate(PARTS):
                        last = nc.tensor.matmul(out, lhs(a, c), rhs(r, c), start=(c == 0 and n == 0),
                                                stop=(c == KC - 1 and n == len(PARTS) - 1))
                return last

            def transpose_z(b, blk, t, m):
                out = bank(b, "z", blk, t)
                pe.wait_ge(z_done, m + 1)
                for c in range(KC):
                    last = nc.tensor.transpose(out[:, c * P:(c + 1) * P], z[:, t % 2, c * P:(c + 1) * P], ident[:, :])
                last.then_inc(unit_full, 1)

            def queries(b, n):
                if ahead(b):
                    pe.wait_ge(dve_done, QT)
                elif n % 4 == 0:
                    pe.wait_ge(dve_done, base(b, 3) + of(b)[0]["z", n // 4, QT - 1]["dve"])
                r = n % 4
                out = bank(b, "q", n)
                product(out, lambda a, c: wq[:, a, c, r * P:(r + 1) * P], lambda h, c: zT[:, h, c, :]
                        ).then_inc(unit_full, 1)

            def scores(b, k):
                n, j = k // GH, k % GH
                r, nb = n % 4, n // NG
                if j == 0:
                    pe.wait_ge(q_stacked[n % 2], STACKED * (b * (NG // 2) + n // 2 + 1))
                    pe.wait_ge(k_loaded[r], 64 * (b + nb + 1))
                for s in range(SPH):
                    u = k * SPH + s
                    if not (isinstance(b, int) and b == 0 and u < SRING):
                        pe.wait_ge(max_done, (b * NH * SPH + u - SRING + 1) * 2)
                    for q in (2 * s, 2 * s + 1):
                        last = nc.tensor.matmul(sps[:, u % SRING, q % 2 * KEYS:(q % 2 + 1) * KEYS],
                                                q_st[:, n % 2, j, q * P:(q + 1) * P], k_st[:, r, j, :],
                                                start=True, stop=True)
                    last.then_inc(s_full, 1)

            def transpose_p(b, n, j):
                k = n * GH + j
                pe.wait_ge(p_done, (b * NH + k + 1) * QT)
                for c in range(KT):
                    out = bank(b, "pt", n, j, c)
                    for q in range(QT):
                        last = nc.tensor.transpose(out[:, q * P:(q + 1) * P],
                                                   probs[:, k % PBUF, q, c * P:(c + 1) * P], ident[:, :])
                    last.then_inc(unit_full, 1)

            def times_v(b, n):
                u = of(b)[0]
                last_dve = max(u["pt", n, j, c]["dve"] for j in range(GH) for c in range(KT) if (j, c) not in ACT_PT)
                last_act = max(u["pt", n, j, c]["act"] for j, c in ACT_PT)
                pe.wait_ge(dve_done, base(b, 3) + last_dve)
                pe.wait_ge(act_done, base(b, 2) + last_act)
                if n < STRIDE:
                    pe.wait_ge(v_loaded[n], 16 * (b + 1))
                pe.wait_ge(ctxn_done, 1 + b * NG + n)
                for c in range(KT):
                    for j in range(GH):
                        last = nc.tensor.matmul(cacc[j * HD:(j + 1) * HD, :], v_sb[:, n % 4, c, j * HD:(j + 1) * HD],
                                                pT[:, n % 2, j, c, :], start=(c == 0), stop=(c == KT - 1))
                last.then_inc(cacc_full, 1)

            def inverse_rows(b, n):
                out = bank(b, "r", n)
                pe.wait_ge(rinv_spread, b * NG + n + 1)
                for q in range(QT):
                    last = nc.tensor.transpose(out[:, q * P:(q + 1) * P],
                                               rinv_rep[:, n % 2, q, :, :].rearrange("p j d -> p (j d)"), ident[:, :])
                last.then_inc(unit_full, 1)

            def outputs(b, blk, ts):
                pe.wait_ge(cT_lo, 1 + b * NG + (blk + 1) * STRIDE)
                for t in ts:
                    out = bank(b, "o", blk, t)
                    product(out, lambda a, c: cT[:, a, c, t * P:(t + 1) * P], lambda h, c: wo[:, h, c, :]
                            ).then_inc(unit_full, 1)

            def batch(b, prefetch):
                pe.wait_ge(act_done, base(b, 2))
                pe.wait_ge(dve_done, base(b, 3))
                for n in range(NG):
                    for j in range(GH):
                        k = n * GH + j
                        if k + 2 < NH or prefetch:
                            scores(b, k + 2)
                        if n % 4 == 2 and (n < 4 or prefetch):
                            for blk, t, m in ln_tiles(b, n, j):
                                transpose_z(b, blk, t, m)
                        if j == 1 and n >= 1:
                            inverse_rows(b, n - 1)
                        transpose_p(b, n, j)
                        if j == 0 and n >= 1:
                            times_v(b, n - 1)
                        if j == GH - 1 and (n + 2 < NG or prefetch):
                            queries(b, n + 2)
                        if n == STRIDE and j == GH - 1:
                            outputs(b, 0, range(QT))
                times_v(b, NG - 1)
                inverse_rows(b, NG - 1)
                outputs(b, 1, range(QT))

            for t in range(QT):
                transpose_z(-1, 0, t, t)
            pe.wait_ge(w_lo, 2)
            queries(-1, 0)
            queries(-1, 1)
            scores(0, 0)
            scores(0, 1)
            with pe.Fori(0, B - 1) as b:
                batch(b, True)
            batch(B - 1, False)


def adapters(nc, x2, wd1, wd2, wb, bd1, bd2, b_base, wa_down, ba_down, wa_up, ba_up, ident_in, out):
    RING = 8
    NU = NBLK * E

    def plan(prefetch, first=False):
        if first:
            alloc = [("z", t) for t in range(TT)]
            read = list(alloc)
        else:
            alloc = [("h", 0), ("h", 1)]
            for u in range(NU):
                alloc += [("h", u + 2)] * (u + 2 < NU) + [("rec", u, c) for c in range(KC)]
            read = list(alloc)
            alloc += [("loss",), ("o", 0), ("o", 1), ("o", 2), ("a", 0), ("a", 1)]
            read += [("loss",), ("a", 0), ("a", 1), ("o", 0), ("o", 1), ("o", 2)]
            for t in range(3, TT):
                both = [("o", t)] + [("z", t - 3)] * prefetch
                alloc += both
                read += both
            if prefetch:
                alloc += [("z", t) for t in range(TT - 3, TT)]
                read += [("z", t) for t in range(TT - 3, TT)]
        acts = dves = 0
        table = {}
        for what in read:
            acts += what[0] in ("z", "h", "a")
            dves += what[0] in ("z", "rec", "loss", "o")
            table[what] = dict(full=len(table) + 1, act=acts, dve=dves, eng="act" if what[0] in ("h", "a") else "dve")
        for i, what in enumerate(alloc):
            table[what].update(i=i, bank=i % RING, freed=table[alloc[i - RING]] if i >= RING else None)
        return table, len(alloc), acts, dves

    FIRST, LOOPED, LAST = plan(False, True), plan(True), plan(False)

    def of(b):
        return FIRST if ahead(b) else LAST if isinstance(b, int) and b == B - 1 else LOOPED

    def base(b, which):
        return 0 if ahead(b) else FIRST[which] + b * LOOPED[which]

    ctx = ExitStack()
    with ctx:
        def sb(name, shape, dt=FP32):
            return ctx.enter_context(nc.sbuf_tensor("f_" + name, shape, dt))

        def sem(name):
            return ctx.enter_context(nc.semaphore("f_" + name))

        w1 = sb("w1", [P, 2, KC, E * H], FP32R)
        w2 = sb("w2", [H, 2, E, D], FP32R)
        wbase = sb("wbase", [P, 2, KC, D], FP32R)
        zT = sb("zT", [P, 2, KC, S], FP32R)
        zf = sb("zf", [P, KC, S])
        hf = sb("hf", [P, 2, 512])
        h = sb("h", [P, 3, 2, 512], FP32R)
        diff = sb("diff", [P, 2, KC, 512])
        dn_raw = sb("dn_raw", [P, KC, R])
        dn = sb("dn", [P, 2, KC, 2, R], FP32R)
        up_raw = sb("up_raw", [P, D])
        up = sb("up", [P, 2, D], FP32R)
        ba_dn = sb("ba_dn", [P, 1])
        ba_up_rep = sb("ba_up_rep", [P, D])
        af = sb("af", [P, 2, 512])
        a_hl = sb("a_hl", [P, 2, 512], FP32R)
        bb_rep = sb("bb_rep", [P, D])
        bsum = sb("bsum", [P, D])
        xln = sb("xln", [P, 2, D])
        z = sb("z", [P, 2, D])
        xres = sb("xres", [P, 4, D])
        ident = sb("ident", [P, P])
        b1 = sb("b1", [P, E])
        b2 = sb("b2", [P, E, KC])
        ones = sb("ones", [P, 1])
        sq = sb("sq", [P, NBLK, E])
        l8 = sb("l8", [1, E])
        neg = sb("neg", [1, E])
        best = sb("best", [1, 8])
        idx = sb("idx", [1, 8], U32)
        stats = sb("stats", [P, 2, 6])
        mv = sb("mv", [P, 2, 2])
        rstd = sb("rstd", [P, 2, 2])
        half = sb("half", [P, 1])
        stage = [diff[:, 0, :, :], diff[:, 1, :, :]]
        ring = ctx.enter_context(nc.psum_tensor("f_ring", [P, RING, 512], FP32))

        waited = sem("waited")
        consts = sem("consts")
        w_loaded = [sem(f"w_loaded{i}") for i in range(2)]
        w_hi = sem("w_hi")
        w_lo = sem("w_lo")
        half_set = sem("half_set")
        ones_set = sem("ones_set")
        xln_in = [sem(f"xln_in{j}") for j in range(2)]
        xres_in = [sem(f"xres_in{j}") for j in range(4)]
        stored = [sem(f"stored{j}") for j in range(4)]
        stats_done = sem("stats_done")
        mv_done = sem("mv_done")
        var_eps = sem("var_eps")
        rstd_done = sem("rstd_done")
        z_done = sem("z_done")
        zf_done = sem("zf_done")
        unit_full = sem("unit_full")
        act_done = sem("act_done")
        dve_done = sem("dve_done")
        h_hi = sem("h_hi")
        h_lo = sem("h_lo")
        sq_done = sem("sq_done")
        argmin_step = sem("argmin_step")
        expert_in = sem("expert_in")
        dn_step = sem("dn_step")
        a_hi = sem("a_hi")
        a_lo = sem("a_lo")
        bsum_done = sem("bsum_done")
        xb_done = sem("xb_done")
        block = ctx.enter_context(nc.Block())
        NEXP = 6
        PIECES = [(wd1[:, :, 0:512], lambda a: w1[:, a, :, 0:512]), (wd1[:, :, 512:1024], lambda a: w1[:, a, :, 512:1024]),
                  (wd2[:, 0:4, :], lambda a: w2[:, a, 0:4, :]), (wd2[:, 4:8, :], lambda a: w2[:, a, 4:8, :]),
                  (wb, lambda a: wbase[:, a, :, :])]

        def carry(engine):
            engine.sem_inc(waited, 1)

        @block.sync
        def _(sp):
            for j in range(4):
                sp.sem_inc(stored[j], 16)
            def load_ln(b, t):
                n = (b + 1) * TT + t
                if not (ahead(b) and t < 2):
                    sp.wait_ge(z_done, n - 1)
                sp.dma_start(xln[:, t % 2, :], x2[bass.ds(n, 1), :, :].rearrange("o p d -> (o p) d")
                             ).then_inc(xln_in[t % 2], 16)

            def load_res(b, t):
                sp.wait_ge(stored[t % 4], 16 + 16 * (b * 2 + t // 4))
                sp.dma_start(xres[:, t % 4, :], x2[bass.ds(b * TT + t, 1), :, :].rearrange("o p d -> (o p) d")
                             ).then_inc(xres_in[t % 4], 16)

            def store(b, t):
                sp.wait_ge(dve_done, base(b, 3) + of(b)[0]["o", t]["dve"])
                sp.dma_start(out[bass.ds(b * TT + t, 1), :, :].rearrange("o p d -> (o p) d"),
                             xres[:, t % 4, :]).then_inc(stored[t % 4], 16)

            sp.dma_start(ident[:, :], ident_in).then_inc(consts, 16)
            sp.dma_start(b1[:, :], bd1).then_inc(consts, 16)
            sp.dma_start(b2[:, :, :], bd2).then_inc(consts, 16)
            sp.dma_start(bb_rep[:, :], b_base.partition_broadcast(P)).then_inc(consts, 16)
            load_ln(-1, 0)
            load_ln(-1, 1)
            for i, (src, _) in enumerate(PIECES):
                if i >= 2:
                    sp.wait_ge(w_lo, i - 1)
                sp.dma_start(stage[i % 2], src).then_inc(w_loaded[i % 2], 16)
            for t in range(2, TT):
                load_ln(-1, t)

            def batch(b, prefetch):
                for t in range(4):
                    load_res(b, t)
                if prefetch:
                    load_ln(b, 0)
                    load_ln(b, 1)
                sp.wait_ge(argmin_step, 4 * (b + 1))
                carry(sp)
                e = sp.value_load(idx[0:1, 0:1], min_val=0, max_val=E - 1)
                sp.dma_start(dn_raw[:, :, :], wa_down[bass.ds(e, 1), :, :, :].rearrange("o p c r -> p (o c) r")
                             ).then_inc(expert_in, 16)
                for half_at in (0, R):
                    sp.dma_start(ba_dn[half_at:half_at + R, :], ba_down[bass.ds(e, 1), :].rearrange("o r -> r o")
                                 ).then_inc(expert_in, 16)
                    sp.dma_start(up_raw[half_at:half_at + R, :], wa_up[bass.ds(e, 1), :, :].rearrange("o r d -> (o r) d")
                                 ).then_inc(expert_in, 16)
                sp.dma_start(ba_up_rep[:, :], ba_up[bass.ds(e, 1), :].rearrange("o d -> (o d)").partition_broadcast(P)
                             ).then_inc(expert_in, 16)
                for t in range(TT):
                    if prefetch and t + 2 < TT:
                        load_ln(b, t + 2)
                    store(b, t)
                    if 1 <= t <= TT - 4:
                        load_res(b, t + 3)
                    
            with sp.Fori(0, B - 1) as b:
                batch(b, True)
            batch(B - 1, False)
            for j in range(4):
                sp.wait_ge(stored[j], 16 + 16 * B * 2)

        @block.gpsimd
        def _(pool):
            nc.gpsimd.memset(half[:, :], -0.5).then_inc(half_set, 1)
            nc.gpsimd.memset(ones[:, :], 1.0).then_inc(ones_set, 1)
            pool.wait_ge(half_set, 1)
            pool.wait_ge(consts, 16 * 4)

            def ln_rstd(b, t):
                n = (b + 1) * TT + t
                pool.wait_ge(mv_done, n + 1)
                carry(pool)
                nc.gpsimd.tensor_scalar(rstd[:, t % 2, 0:1], mv[:, t % 2, 1:2], EPS, None, ALU.add
                                        ).then_inc(var_eps, 1)
                pool.wait_ge(var_eps, n + 1)
                nc.gpsimd.tensor_tensor(rstd[:, t % 2, 1:2], rstd[:, t % 2, 0:1], half[:, :], ALU.pow
                                        ).then_inc(rstd_done, 1)

            def z_whole(b, t):
                pool.wait_ge(dve_done, base(b, 3) + of(b)[0]["z", t]["dve"])
                at = slice(t * P, (t + 1) * P)
                nc.gpsimd.tensor_tensor(zf[:, :, at], zT[:, HI, :, at].bitcast(FP32), zT[:, LO, :, at].bitcast(FP32),
                                        ALU.add).then_inc(zf_done, 1)

            def add_bias(b, t):
                pool.wait_ge(xres_in[t % 4], 16 * (b * 2 + t // 4 + 1))
                nc.gpsimd.tensor_tensor(xres[:, t % 4, :], xres[:, t % 4, :], bsum[:, :], ALU.add).then_inc(xb_done, 1)

            def batch(b, prefetch):
                if prefetch:
                    ln_rstd(b, 0)
                    ln_rstd(b, 1)
                pool.wait_ge(expert_in, 16 * NEXP * (b + 1))
                nc.gpsimd.tensor_tensor(bsum[:, :], bb_rep[:, :], ba_up_rep[:, :], ALU.add).then_inc(bsum_done, 1)
                pool.wait_ge(bsum_done, b + 1)
                for t in range(4):
                    add_bias(b, t)
                for t in range(3, TT):
                    if prefetch:
                        z_whole(b, t - 3)
                        if t > 3 or True:
                            ln_rstd(b, t - 1)
                    if t + 1 < TT:
                        add_bias(b, t + 1)
                if prefetch:
                    z_whole(b, TT - 3)
                    ln_rstd(b, TT - 1)
                    z_whole(b, TT - 2)
                    z_whole(b, TT - 1)

            for t in range(TT):
                ln_rstd(-1, t)
                z_whole(-1, t)
            with pool.Fori(0, B - 1) as b:
                batch(b, True)
            batch(B - 1, False)

        @block.scalar
        def _(act):
            act.sem_inc(sq_done, 1)
            act.wait_ge(consts, 16 * 4)

            def unit(b, *what):
                u = of(b)[0][what]
                act.wait_ge(unit_full, base(b, 1) + u["full"])
                return ring[:, u["bank"], :]

            def z_hi(b, t):
                src = unit(b, "z", t).rearrange("p (c n) -> p c n", n=P)
                nc.scalar.copy(zT[:, HI, :, t * P:(t + 1) * P], src).then_inc(act_done, 1)

            def hidden(b, u):
                e = u % E
                src = unit(b, "h", u)
                act.wait_ge(h_lo, 1 + b * NU + max(u - 1, 0))
                nc.scalar.activation(hf[:, u % 2, :], src, ACT.Relu, bias=b1[:, e:e + 1]).then_inc(act_done, 1)

            def squares(b, u):
                act.wait_ge(dve_done, base(b, 3) + of(b)[0]["rec", u, KC - 1]["dve"])
                nc.scalar.activation(diff[:, u % 2, :, :], diff[:, u % 2, :, :], ACT.Square,
                                     accum_out=sq[:, u // E, u % E:u % E + 1]).then_inc(sq_done, 1)

            def batch(b, prefetch):
                hidden(b, 0)
                hidden(b, 1)
                for u in range(NU):
                    if u + 2 < NU:
                        hidden(b, u + 2)
                    if u >= 1:
                        squares(b, u - 1)
                squares(b, NU - 1)
                act.wait_ge(expert_in, 16 * NEXP * (b + 1))
                for blk in range(NBLK):
                    src = unit(b, "a", blk)
                    nc.scalar.activation(af[:, blk, :], src, ACT.Relu, bias=ba_dn[:, 0:1]).then_inc(act_done, 1)
                if prefetch:
                    for t in range(TT):
                        z_hi(b, t)

            for i, (_, dst) in enumerate(PIECES):
                act.wait_ge(w_loaded[i % 2], 16 * (i // 2 + 1))
                nc.scalar.copy(dst(HI), stage[i % 2]).then_inc(w_hi, 1)
            for t in range(TT):
                z_hi(-1, t)
            with act.Fori(0, B - 1) as b:
                batch(b, True)
            batch(B - 1, False)

        @block.vector
        def _(dve):
            dve.sem_inc(h_lo, 1)
            dve.wait_ge(consts, 16 * 4)

            def unit(b, *what):
                u = of(b)[0][what]
                if what[0] == "z":
                    dve.wait_ge(act_done, base(b, 2) + u["act"])
                else:
                    dve.wait_ge(unit_full, base(b, 1) + u["full"])
                return ring[:, u["bank"], :]

            def ln_stats(b, t):
                n = (b + 1) * TT + t
                dve.wait_ge(xln_in[t % 2], 16 * ((b + 1) * (TT // 2) + t // 2 + 1))
                nc.vector.bn_stats(stats[:, t % 2, :], xln[:, t % 2, :]).then_inc(stats_done, 1)
                dve.wait_ge(stats_done, n + 1)
                carry(dve)
                nc.vector.bn_aggr(mv[:, t % 2, :], stats[:, t % 2, :]).then_inc(mv_done, 1)

            def ln_apply(b, t):
                n = (b + 1) * TT + t
                dve.wait_ge(rstd_done, n + 1)
                nc.vector.tensor_scalar(z[:, t % 2, :], xln[:, t % 2, :], mv[:, t % 2, 0:1], rstd[:, t % 2, 1:2],
                                        ALU.subtract, ALU.mult).then_inc(z_done, 1)

            def z_lo(b, t):
                src = unit(b, "z", t).rearrange("p (c n) -> p c n", n=P)
                at = slice(t * P, (t + 1) * P)
                nc.vector.tensor_tensor(zT[:, LO, :, at], src, zT[:, HI, :, at].bitcast(FP32), ALU.subtract
                                        ).then_inc(dve_done, 1)

            def split_h(b, u):
                dve.wait_ge(act_done, base(b, 2) + of(b)[0]["h", u]["act"])
                nc.vector.tensor_copy(h[:, u % 3, HI, :], hf[:, u % 2, :]).then_inc(h_hi, 1)
                dve.wait_ge(h_hi, b * NU + u + 1)
                nc.vector.tensor_tensor(h[:, u % 3, LO, :], hf[:, u % 2, :], h[:, u % 3, HI, :].bitcast(FP32),
                                        ALU.subtract).then_inc(h_lo, 1)

            def error(b, u):
                blk, e = u // E, u % E
                dve.wait_ge(sq_done, 1 + b * NU + max(u - 1, 0))
                for c in range(KC):
                    nc.vector.scalar_tensor_tensor(diff[:, u % 2, c, :], unit(b, "rec", u, c), b2[:, e, c:c + 1],
                                                   zf[:, c, blk * 512:(blk + 1) * 512], ALU.add, ALU.subtract
                                                   ).then_inc(dve_done, 1)

            def argmin(b):
                src = unit(b, "loss")[0:1, 0:NU]
                nc.vector.tensor_reduce(l8[:, :], src.rearrange("p (k e) -> p e k", e=E), AX.X, ALU.add
                                        ).then_inc(dve_done, 1)
                dve.wait_ge(dve_done, base(b, 3) + of(b)[0]["loss",]["dve"])
                nc.vector.tensor_scalar(neg[:, :], l8[:, :], -1.0 / (S * D), None, ALU.mult).then_inc(argmin_step, 1)
                dve.wait_ge(argmin_step, 4 * b + 1)
                carry(dve)
                nc.vector.max(best[:, :], neg[:, :]).then_inc(argmin_step, 1)
                dve.wait_ge(argmin_step, 4 * b + 2)
                carry(dve)
                nc.vector.max_index(idx[:, :], best[:, :], neg[:, :]).then_inc(argmin_step, 2)

            def split_expert(b):
                dve.wait_ge(expert_in, 16 * NEXP * (b + 1))
                raw = dn_raw[:, :, None, :].broadcast_to((P, KC, 2, R))
                nc.vector.tensor_copy(dn[:, HI, :, :, :], raw).then_inc(dn_step, 1)
                nc.vector.tensor_copy(up[:, HI, :], up_raw[:, :]).then_inc(dn_step, 1)
                dve.wait_ge(dn_step, 4 * b + 2)
                nc.vector.tensor_tensor(dn[:, LO, :, :, :], raw, dn[:, HI, :, :, :].bitcast(FP32), ALU.subtract
                                        ).then_inc(dn_step, 1)
                nc.vector.tensor_tensor(up[:, LO, :], up_raw[:, :], up[:, HI, :].bitcast(FP32), ALU.subtract
                                        ).then_inc(dn_step, 1)

            def split_a(b, blk):
                dve.wait_ge(act_done, base(b, 2) + of(b)[0]["a", blk]["act"])
                nc.vector.tensor_copy(a_hl[:, blk, :], af[:, blk, :]).then_inc(a_hi, 1)
                dve.wait_ge(a_hi, b * NBLK + blk + 1)
                nc.vector.tensor_tensor(a_hl[R:P, blk, :], af[R:P, blk, :], a_hl[R:P, blk, :].bitcast(FP32),
                                        ALU.subtract).then_inc(a_lo, 1)

            def output(b, t):
                src = unit(b, "o", t)
                dve.wait_ge(xb_done, b * TT + t + 1)
                nc.vector.tensor_tensor(xres[:, t % 4, :], src, xres[:, t % 4, :], ALU.add).then_inc(dve_done, 1)

            def batch(b, prefetch):
                split_h(b, 0)
                split_h(b, 1)
                dve.wait_ge(zf_done, (b + 1) * TT)
                for u in range(NU):
                    if u + 2 < NU:
                        split_h(b, u + 2)
                    error(b, u)
                argmin(b)
                if prefetch:
                    ln_stats(b, 0)
                    ln_stats(b, 1)
                    ln_apply(b, 0)
                    ln_apply(b, 1)
                split_expert(b)
                for blk in range(NBLK):
                    split_a(b, blk)
                for t in range(3):
                    output(b, t)
                for t in range(3, TT):
                    output(b, t)
                    if prefetch:
                        z_lo(b, t - 3)
                        ln_stats(b, t - 1)
                        ln_apply(b, t - 1)
                if prefetch:
                    z_lo(b, TT - 3)
                    ln_stats(b, TT - 1)
                    ln_apply(b, TT - 1)
                    z_lo(b, TT - 2)
                    z_lo(b, TT - 1)

            for i, (_, dst) in enumerate(PIECES):
                dve.wait_ge(w_hi, i + 1)
                nc.vector.tensor_tensor(dst(LO), stage[i % 2], dst(HI).bitcast(FP32), ALU.subtract).then_inc(w_lo, 1)
            ln_stats(-1, 0)
            for t in range(TT):
                if t + 1 < TT:
                    ln_stats(-1, t + 1)
                ln_apply(-1, t)
                z_lo(-1, t)
            with dve.Fori(0, B - 1) as b:
                batch(b, True)
            batch(B - 1, False)

        @block.tensor
        def _(pe):
            pe.wait_ge(consts, 16 * 4)
            pe.wait_ge(ones_set, 1)

            def bank(b, *what):
                u = of(b)[0][what]
                if u["freed"]:
                    f = u["freed"]
                    if f["eng"] == "act":
                        pe.wait_ge(act_done, base(b, 2) + f["act"])
                    else:
                        pe.wait_ge(dve_done, base(b, 3) + f["dve"])
                return ring[:, u["bank"], :]

            def product(out, lhs, rhs, stop=True):
                for c in range(KC):
                    for n, (a, r) in enumerate(PARTS):
                        last = nc.tensor.matmul(out, lhs(a, c), rhs(r, c), start=(c == 0 and n == 0),
                                                stop=(stop and c == KC - 1 and n == len(PARTS) - 1))
                return last

            def transpose_z(b, t):
                out = bank(b, "z", t)
                pe.wait_ge(z_done, (b + 1) * TT + t + 1)
                for c in range(KC):
                    last = nc.tensor.transpose(out[:, c * P:(c + 1) * P], z[:, t % 2, c * P:(c + 1) * P], ident[:, :])
                last.then_inc(unit_full, 1)

            def encode(b, u):
                blk, e = u // E, u % E
                product(bank(b, "h", u), lambda a, c: w1[:, a, c, e * H:(e + 1) * H],
                        lambda r, c: zT[:, r, c, blk * 512:(blk + 1) * 512]).then_inc(unit_full, 1)

            def rebuild(b, u):
                e = u % E
                pe.wait_ge(h_lo, 1 + b * NU + u + 1)
                for c in range(KC):
                    out = bank(b, "rec", u, c)
                    for n, (a, r) in enumerate(PARTS):
                        last = nc.tensor.matmul(out, w2[:, a, e, c * P:(c + 1) * P], h[:, u % 3, r, :],
                                                start=(n == 0), stop=(n == len(PARTS) - 1))
                    last.then_inc(unit_full, 1)

            def loss(b):
                out = bank(b, "loss")
                pe.wait_ge(sq_done, 1 + (b + 1) * NU)
                nc.tensor.matmul(out[0:1, 0:NU], ones[:, :], sq[:, :, :].rearrange("p k e -> p (k e)"),
                                 start=True, stop=True).then_inc(unit_full, 1)

            def base_part(b, t):
                out = bank(b, "o", t)
                product(out, lambda a, c: zT[:, a, c, t * P:(t + 1) * P], lambda r, c: wbase[:, r, c, :], stop=False)
                return out

            def adapter_part(b, t, out):
                pe.wait_ge(a_lo, b * NBLK + t // 4 + 1)
                for r in (HI, LO):
                    last = nc.tensor.matmul(out, a_hl[:, t // 4, t % 4 * P:(t % 4 + 1) * P], up[:, r, :],
                                            start=False, stop=(r == LO))
                last.then_inc(unit_full, 1)

            def down(b, blk):
                out = bank(b, "a", blk)
                product(out, lambda a, c: dn[:, a, c, :, :].rearrange("p k r -> p (k r)"),
                        lambda r, c: zT[:, r, c, blk * 512:(blk + 1) * 512]).then_inc(unit_full, 1)

            def batch(b, prefetch):
                pe.wait_ge(act_done, base(b, 2))
                pe.wait_ge(dve_done, base(b, 3))
                encode(b, 0)
                encode(b, 1)
                for u in range(NU):
                    if u + 2 < NU:
                        encode(b, u + 2)
                    rebuild(b, u)
                loss(b)
                open_tiles = [base_part(b, t) for t in range(3)]
                pe.wait_ge(dn_step, 4 * (b + 1))
                down(b, 0)
                down(b, 1)
                for t in range(3):
                    adapter_part(b, t, open_tiles[t])
                for t in range(3, TT):
                    adapter_part(b, t, base_part(b, t))
                    if prefetch:
                        transpose_z(b, t - 3)
                if prefetch:
                    for t in range(TT - 3, TT):
                        transpose_z(b, t)

            for t in range(TT):
                transpose_z(-1, t)
            pe.wait_ge(w_lo, len(PIECES))
            with pe.Fori(0, B - 1) as b:
                batch(b, True)
            batch(B - 1, False)


def decoder_layer(nc, t):
    x1 = nc.dram_tensor("x_after_self_attention", (B * TT, P, D), FP32, kind="Internal").ap()
    x2 = nc.dram_tensor("x_after_cross_attention", (B * TT, P, D), FP32, kind="Internal").ap()
    keys = nc.dram_tensor("cross_keys", (B * STRIDE, P, 2, KEYS), FP32, kind="Internal").ap()
    values = nc.dram_tensor("cross_values", (B * STRIDE, P, KT, P), FP32, kind="Internal").ap()
    self_attention(nc, t["x"], t["s_wqT"], t["s_wkT"], t["s_wvT"], t["s_bq"], t["s_bk"], t["s_bv"],
                   t["ident"], t["causal"], x1)
    cross_keys_values(nc, t["ctxT"], t["c_wk"], t["c_wv"], t["c_bk"], t["c_bv"], t["ident"], keys, values)
    cross_attention(nc, x1, t["c_wq"], t["c_wo"], t["c_bq"], t["c_bo"], t["mask"], keys, values, t["ident"], x2)
    adapters(nc, x2, t["wd1"], t["wd2"], t["w_base"], t["bd1"], t["bd2"], t["b_base"], t["wa_down"], t["ba_down"],
             t["wa_up"], t["ba_up"], t["ident"], t["out"])


def kernel(**inputs):
    import concourse.bacc as bacc
    from concourse.bass_utils import run_bass_kernel_spmd

    a = {name: np.asarray(v) for name, v in inputs.items()}

    def rows(w):
        return w.reshape(KC, P, -1).transpose(1, 0, 2)

    def by_group(w):
        return w.reshape(D, GH, STRIDE, HD).transpose(0, 2, 1, 3).reshape(D, D)

    def group_bias(v):
        return v.reshape(GH, STRIDE, HD).transpose(0, 2, 1).reshape(P, STRIDE)

    arrays = {
        "x": a["x"].reshape(B * TT, P, D),
        "s_wqT": rows(a["L0_attn_Wq"].T), "s_wkT": rows(a["L0_attn_Wk"].T), "s_wvT": rows(a["L0_attn_Wv"].T),
        "s_bq": a["L0_attn_bq"].reshape(KC, P).T, "s_bk": a["L0_attn_bk"].reshape(KC, P).T, "s_bv": a["L0_attn_bv"],
        "ctxT": a["ctx_1024"].transpose(0, 2, 1).reshape(B, KC, P, KEYS, STRIDE).transpose(0, 2, 1, 4, 3).reshape(
            B, P, KC, S),
        "mask": a["mask_BxS2_bf0"].reshape(B, KEYS, STRIDE).transpose(0, 2, 1).reshape(B, S),
        "c_wq": rows(by_group(a["L0_xattn_Wq"])), "c_wk": rows(by_group(a["L0_xattn_Wk"])),
        "c_wv": rows(by_group(a["L0_xattn_Wv"])), "c_wo": rows(by_group(a["L0_xattn_Wo"].T).T),
        "c_bq": group_bias(a["L0_xattn_bq"]), "c_bk": group_bias(a["L0_xattn_bk"]),
        "c_bv": group_bias(a["L0_xattn_bv"]), "c_bo": a["L0_xattn_bo"],
        "wd1": rows(a["L0_ffn_Wd1"].transpose(1, 0, 2).reshape(D, E * H)), "wd2": a["L0_ffn_Wd2"].transpose(1, 0, 2),
        "w_base": rows(a["L0_ffn_W_base"]), "b_base": a["L0_ffn_b_base"],
        "bd1": a["L0_ffn_bd1"].T, "bd2": a["L0_ffn_bd2"].reshape(E, KC, P).transpose(2, 0, 1),
        "wa_down": a["L0_ffn_Wa_down"].reshape(E, KC, P, R).transpose(0, 2, 1, 3), "ba_down": a["L0_ffn_ba_down"],
        "wa_up": a["L0_ffn_Wa_up"], "ba_up": a["L0_ffn_ba_up"],
        "ident": np.eye(P, dtype=np.float32),
        "causal": np.triu(np.full((P, P), -1e30, np.float32), 1),
    }
    nc = bacc.Bacc("TRN2", target_bir_lowering=False, num_devices=1)
    arrays = {f"in_{name}": np.ascontiguousarray(v) for name, v in arrays.items()}
    tensors = {name[3:]: nc.dram_tensor(name, v.shape, mybir.dt.from_np(v.dtype), kind="ExternalInput").ap()
               for name, v in arrays.items()}
    tensors["out"] = nc.dram_tensor("out", (B * TT, P, D), FP32, kind="ExternalOutput").ap()
    decoder_layer(nc, tensors)
    got = run_bass_kernel_spmd(nc, [arrays], core_ids=[0])
    return got.results[0]["out"].reshape(B, S, D)
```

```python
import math
from contextlib import ExitStack

import numpy as np
import concourse.bass as bass
from concourse import mybir

FP32 = mybir.dt.float32
FP32R = mybir.dt.float32r
U8 = mybir.dt.uint8
U32 = mybir.dt.uint32
ALU = mybir.AluOpType
ACT = mybir.ActivationFunctionType
AX = mybir.AxisListType

P = 128
B, S, D = 4, 1024, 512
TT = S // P
KC = D // P
NBLK = S // 512
EPS = 1e-5
HI, LO = 0, 1
PARTS = ((HI, HI), (HI, LO), (LO, HI))
STRIDE = 4
HD = 32
GH = P // HD
KEYS = S // STRIDE
KT = KEYS // P
E, H, R = 8, 128, 64


def ahead(b):
    return isinstance(b, int) and b < 0


def self_attention(nc, x, wqT, wkT, wvT, bq, bk, bv, ident_in, causal_in, x1):
    scale = 1.0 / math.sqrt(D)
    RING = 3
    PT_UNITS = [-(-(i + 1) // 4) for i in range(TT)]
    K0, V0 = 0, KC * NBLK
    Q0 = V0 + TT

    def plan(prefetch):
        at, k = {("q", 0): Q0}, Q0 + KC
        for i in range(TT):
            if i == TT // 2 - 1:
                at["q", 1] = k
                k += KC
            at["pt", i] = k
            k += PT_UNITS[i]
            if prefetch and i >= TT // 2:
                at["ln", 2 * (i - TT // 2)] = k
                at["ln", 2 * (i - TT // 2) + 1] = k + 1
                k += 2
        return at, k

    LOOPED, PER = plan(True)
    LAST, _ = plan(False)
    assert PER % RING == TT % RING

    def order(b, *what):
        return (LAST if isinstance(b, int) and b == B - 1 else LOOPED)[what]

    ctx = ExitStack()
    with ctx:
        def sb(name, shape, dt=FP32):
            return ctx.enter_context(nc.sbuf_tensor("a_" + name, shape, dt))

        def sem(name):
            return ctx.enter_context(nc.semaphore("a_" + name))

        wq = sb("wq", [P, 2, KC, D], FP32R)
        wk = sb("wk", [P, 2, KC, D], FP32R)
        wv = sb("wv", [P, 2, KC, D], FP32R)
        zT = sb("zT", [P, 2, KC, S], FP32R)
        kT = sb("kT", [P, 2, KC, S], FP32R)
        v = sb("v", [P, 2, TT, D], FP32R)
        qT = sb("qT", [P, 2, KC, 512], FP32R)
        probs = sb("probs", [P, 2, S])
        stage = probs[:, :, :].rearrange("p a s -> p (a s)").rearrange("p (c n) -> p c n", c=KC)
        pT = sb("pT", [P, 2, 2, TT, P], FP32R)
        xln = sb("xln", [P, 2, D])
        z = sb("z", [P, 2, D])
        xres = sb("xres", [P, 2, D])
        xout = xres
        bv_rep = sb("bv_rep", [P, D])
        ident = sb("ident", [P, P])
        causal = sb("causal", [P, P])
        bqk = sb("bqk", [P, 2, KC])
        stats = sb("stats", [P, 2, 6])
        mv = sb("mv", [P, 2, 2])
        rstd = sb("rstd", [P, 2, 2])
        half = sb("half", [P, 1])
        mx = sb("mx", [P, TT])
        nbias = sb("nbias", [P, TT])
        rowsum = sb("rowsum", [P, TT])
        rinv = sb("rinv", [P, TT])

        ring = ctx.enter_context(nc.psum_tensor("a_ring", [P, RING, 512], FP32))
        zacc = ctx.enter_context(nc.psum_tensor("a_zacc", [P, 512], FP32))
        scores = ctx.enter_context(nc.psum_tensor("a_scores", [P, 2, S], FP32))

        waited = sem("waited")
        consts = sem("consts")
        w_loaded = sem("w_loaded")
        w_hi = sem("w_hi")
        w_lo = sem("w_lo")
        half_set = sem("half_set")
        xln_in = [sem(f"xln_in{j}") for j in range(2)]
        xres_in = [sem(f"xres_in{j}") for j in range(2)]
        stored = [sem(f"stored{j}") for j in range(2)]
        stats_done = sem("stats_done")
        mv_done = sem("mv_done")
        var_eps = sem("var_eps")
        rstd_done = sem("rstd_done")
        z_done = sem("z_done")
        unit_full = sem("unit_full")
        hi_done = sem("hi_done")
        lo_done = sem("lo_done")
        s_full = sem("s_full")
        masked = sem("masked")
        max_done = sem("max_done")
        nbias_done = sem("nbias_done")
        p_done = sem("p_done")
        rinv_done = sem("rinv_done")
        zacc_full = sem("zacc_full")
        combined = sem("combined")
        xb_done = sem("xb_done")
        block = ctx.enter_context(nc.Block())

        def G(b, k):
            return k if ahead(b) else TT + b * PER + k

        def lag(k):
            return RING if k >= RING else k + 1 + (TT - 1 - k) % RING

        def carry(engine):
            engine.sem_inc(waited, 1)

        @block.sync
        def _(sp):
            for j in range(2):
                sp.sem_inc(stored[j], 16)
            sp.dma_start(ident[:, :], ident_in).then_inc(consts, 16)
            sp.dma_start(causal[:, :], causal_in).then_inc(consts, 16)
            sp.dma_start(bqk[:, 0, :], bq).then_inc(consts, 16)
            sp.dma_start(bqk[:, 1, :], bk).then_inc(consts, 16)
            sp.dma_start(bv_rep[:, :], bv.partition_broadcast(P)).then_inc(consts, 16)

            def load_ln(b, t):
                if not ahead(b) or t >= 2:
                    sp.wait_ge(z_done, (b + 1) * TT + t - 1)
                sp.dma_start(xln[:, t % 2, :], x[bass.ds((b + 1) * TT + t, 1), :, :].rearrange("o p d -> (o p) d")
                             ).then_inc(xln_in[t % 2], 16)

            load_ln(-1, 0)
            load_ln(-1, 1)
            for w, src in enumerate((wkT, wvT, wqT)):
                if w:
                    sp.wait_ge(w_lo, w)
                sp.dma_start(stage, src).then_inc(w_loaded, 16)
            for t in range(2, TT):
                load_ln(-1, t)

            def store(b, i):
                sp.wait_ge(combined, 1 + b * TT + i + 1)
                sp.dma_start(x1[bass.ds(b * TT + i, 1), :, :].rearrange("o p d -> (o p) d"),
                             xout[:, i % 2, :]).then_inc(stored[i % 2], 16)

            def batch(b, prefetch):
                for i in range(TT):
                    sp.wait_ge(stored[i % 2], 16 + 16 * (b * (TT // 2) + i // 2))
                    sp.dma_start(xres[:, i % 2, :], x[bass.ds(b * TT + i, 1), :, :].rearrange("o p d -> (o p) d")
                                 ).then_inc(xres_in[i % 2], 16)
                    if prefetch and i >= TT // 2:
                        load_ln(b, 2 * (i - TT // 2))
                        load_ln(b, 2 * (i - TT // 2) + 1)
                    if i >= 1:
                        store(b, i - 1)
                store(b, TT - 1)

            with sp.Fori(0, B - 1) as b:
                batch(b, True)
            batch(B - 1, False)
            for j in range(2):
                sp.wait_ge(stored[j], 16 + 16 * B * TT // 2)

        @block.gpsimd
        def _(pool):
            nc.gpsimd.memset(half[:, :], -0.5).then_inc(half_set, 1)
            pool.wait_ge(half_set, 1)
            pool.wait_ge(consts, 16 * 5)

            def ln_rstd(b, t):
                n = (b + 1) * TT + t
                pool.wait_ge(mv_done, n + 1)
                carry(pool)
                nc.gpsimd.tensor_scalar(rstd[:, t % 2, 0:1], mv[:, t % 2, 1:2], EPS, None, ALU.add
                                        ).then_inc(var_eps, 1)
                pool.wait_ge(var_eps, n + 1)
                nc.gpsimd.tensor_tensor(rstd[:, t % 2, 1:2], rstd[:, t % 2, 0:1], half[:, :], ALU.pow
                                        ).then_inc(rstd_done, 1)

            def add_bv(b, i):
                pool.wait_ge(xres_in[i % 2], 16 * (b * (TT // 2) + i // 2 + 1))
                nc.gpsimd.tensor_tensor(xres[:, i % 2, :], xres[:, i % 2, :], bv_rep[:, :], ALU.add
                                        ).then_inc(xb_done, 1)

            def batch(b, prefetch):
                for i in range(TT):
                    add_bv(b, i)
                    if prefetch and i >= TT // 2:
                        ln_rstd(b, 2 * (i - TT // 2))
                        ln_rstd(b, 2 * (i - TT // 2) + 1)

            for t in range(TT):
                ln_rstd(-1, t)
            with pool.Fori(0, B - 1) as b:
                batch(b, True)
            batch(B - 1, False)

        @block.scalar
        def _(act):
            act.sem_inc(p_done, 1)
            act.wait_ge(consts, 16 * 5)

            def evacuate(b, k, out, bias=None):
                act.wait_ge(unit_full, G(b, k) + 1)
                src = ring[:, k % RING, :]
                if len(out.shape) == 3:
                    src = src.rearrange("p (c n) -> p c n", n=P)[:, 0:out.shape[1], :]
                if bias is None:
                    nc.scalar.copy(out, src).then_inc(hi_done, 1)
                else:
                    nc.scalar.activation(out, src, ACT.Identity, bias=bias).then_inc(hi_done, 1)

            def split_w(w, dst):
                act.wait_ge(w_loaded, 16 * (w + 1))
                nc.scalar.copy(dst[:, HI, :, :], stage).then_inc(w_hi, 1)

            def ln_unit(b, t):
                evacuate(b, t if ahead(b) else order(b, "ln", t), zT[:, HI, :, t * P:(t + 1) * P])

            def softmax_exp(b, i):
                n = (i + 1) * P
                act.wait_ge(nbias_done, b * TT + i + 1)
                nc.scalar.activation(probs[:, i % 2, 0:n], scores[:, i % 2, 0:n], ACT.Exp, scale=scale,
                                     bias=nbias[:, i:i + 1], accum_out=rowsum[:, i:i + 1]).then_inc(p_done, 1)

            def pt_units(b, i):
                act.wait_ge(zacc_full, 1 + (b * TT + i - 1 if i >= 2 else b * TT))
                for u in range(PT_UNITS[i]):
                    m = min(4, i + 1 - 4 * u)
                    evacuate(b, order(b, "pt", i) + u, pT[:, i % 2, HI, 4 * u:4 * u + m, :])

            def batch(b, prefetch):
                act.wait_ge(s_full, 1 + b * TT)
                for c in range(KC):
                    for n in range(NBLK):
                        evacuate(b, K0 + c * NBLK + n, kT[:, HI, c, n * 512:(n + 1) * 512], bqk[:, 1, c:c + 1])
                act.wait_ge(zacc_full, 1 + b * TT)
                for t in range(TT):
                    evacuate(b, V0 + t, v[:, HI, t, :])
                for c in range(KC):
                    evacuate(b, order(b, "q", 0) + c, qT[:, HI, c, :], bqk[:, 0, c:c + 1])
                softmax_exp(b, 0)
                for i in range(TT):
                    if i == TT // 2 - 1:
                        act.wait_ge(s_full, 1 + b * TT + TT // 2)
                        for c in range(KC):
                            evacuate(b, order(b, "q", 1) + c, qT[:, HI, c, :], bqk[:, 0, c:c + 1])
                    pt_units(b, i)
                    if prefetch and i >= TT // 2:
                        ln_unit(b, 2 * (i - TT // 2))
                        ln_unit(b, 2 * (i - TT // 2) + 1)
                    if i + 1 < TT:
                        softmax_exp(b, i + 1)

            split_w(0, wk)
            split_w(1, wv)
            split_w(2, wq)
            for t in range(TT):
                ln_unit(-1, t)
            with act.Fori(0, B - 1) as b:
                batch(b, True)
            batch(B - 1, False)

        @block.vector
        def _(dve):
            dve.sem_inc(combined, 1)
            dve.wait_ge(consts, 16 * 5)

            def remainder(b, k, out, hi, bias=None):
                dve.wait_ge(hi_done, G(b, k) + 1)
                src = ring[:, k % RING, :]
                if len(out.shape) == 3:
                    src = src.rearrange("p (c n) -> p c n", n=P)[:, 0:out.shape[1], :]
                hi = hi.bitcast(FP32)
                if bias is None:
                    nc.vector.tensor_tensor(out, src, hi, ALU.subtract).then_inc(lo_done, 1)
                else:
                    nc.vector.scalar_tensor_tensor(out, src, bias, hi, ALU.add, ALU.subtract).then_inc(lo_done, 1)

            def split_w(w, dst):
                dve.wait_ge(w_hi, w + 1)
                nc.vector.tensor_tensor(dst[:, LO, :, :], stage, dst[:, HI, :, :].bitcast(FP32), ALU.subtract
                                        ).then_inc(w_lo, 1)

            def ln_stats(b, t):
                n = (b + 1) * TT + t
                dve.wait_ge(xln_in[t % 2], 16 * ((b + 1) * (TT // 2) + t // 2 + 1))
                nc.vector.bn_stats(stats[:, t % 2, :], xln[:, t % 2, :]).then_inc(stats_done, 1)
                dve.wait_ge(stats_done, n + 1)
                carry(dve)
                nc.vector.bn_aggr(mv[:, t % 2, :], stats[:, t % 2, :]).then_inc(mv_done, 1)

            def ln_apply(b, t):
                n = (b + 1) * TT + t
                dve.wait_ge(rstd_done, n + 1)
                nc.vector.tensor_scalar(z[:, t % 2, :], xln[:, t % 2, :], mv[:, t % 2, 0:1], rstd[:, t % 2, 1:2],
                                        ALU.subtract, ALU.mult).then_inc(z_done, 1)

            def ln_unit(b, t):
                k = t if ahead(b) else order(b, "ln", t)
                at = slice(t * P, (t + 1) * P)
                remainder(b, k, zT[:, LO, :, at], zT[:, HI, :, at])

            def row_max(b, i):
                n = (i + 1) * P
                dve.wait_ge(s_full, 1 + b * TT + i + 1)
                nc.vector.tensor_tensor(scores[:, i % 2, n - P:n], scores[:, i % 2, n - P:n], causal[:, :], ALU.add
                                        ).then_inc(masked, 1)
                dve.wait_ge(masked, b * TT + i + 1)
                nc.vector.tensor_reduce(mx[:, i:i + 1], scores[:, i % 2, 0:n], AX.X, ALU.max).then_inc(max_done, 1)
                dve.wait_ge(max_done, b * TT + i + 1)
                nc.vector.tensor_scalar(nbias[:, i:i + 1], mx[:, i:i + 1], -scale, None, ALU.mult
                                        ).then_inc(nbias_done, 1)

            def pt_units(b, i):
                for u in range(PT_UNITS[i]):
                    m = min(4, i + 1 - 4 * u)
                    at = slice(4 * u, 4 * u + m)
                    remainder(b, order(b, "pt", i) + u, pT[:, i % 2, LO, at, :], pT[:, i % 2, HI, at, :])

            def combine(b, i):
                dve.wait_ge(p_done, 1 + b * TT + i + 1)
                nc.vector.reciprocal(rinv[:, i:i + 1], rowsum[:, i:i + 1]).then_inc(rinv_done, 1)
                dve.wait_ge(rinv_done, b * TT + i + 1)
                dve.wait_ge(xb_done, b * TT + i + 1)
                dve.wait_ge(zacc_full, 1 + b * TT + i + 1)
                nc.vector.scalar_tensor_tensor(xout[:, i % 2, :], zacc[:, :], rinv[:, i:i + 1], xres[:, i % 2, :],
                                               ALU.mult, ALU.add).then_inc(combined, 1)

            def batch(b, prefetch):
                for c in range(KC):
                    for n in range(NBLK):
                        at = slice(n * 512, (n + 1) * 512)
                        remainder(b, K0 + c * NBLK + n, kT[:, LO, c, at], kT[:, HI, c, at], bqk[:, 1, c:c + 1])
                for t in range(TT):
                    remainder(b, V0 + t, v[:, LO, t, :], v[:, HI, t, :])
                for c in range(KC):
                    remainder(b, order(b, "q", 0) + c, qT[:, LO, c, :], qT[:, HI, c, :], bqk[:, 0, c:c + 1])
                row_max(b, 0)
                for i in range(TT):
                    if i == TT // 2 - 1:
                        for c in range(KC):
                            remainder(b, order(b, "q", 1) + c, qT[:, LO, c, :], qT[:, HI, c, :], bqk[:, 0, c:c + 1])
                    if i + 1 < TT:
                        row_max(b, i + 1)
                    if prefetch and i >= TT // 2:
                        t = 2 * (i - TT // 2)
                        ln_stats(b, t)
                        ln_stats(b, t + 1)
                        ln_apply(b, t)
                        ln_apply(b, t + 1)
                    pt_units(b, i)
                    if prefetch and i >= TT // 2:
                        ln_unit(b, t)
                        ln_unit(b, t + 1)
                    if i >= 1:
                        combine(b, i - 1)
                combine(b, TT - 1)

            split_w(0, wk)
            split_w(1, wv)
            split_w(2, wq)
            ln_stats(-1, 0)
            for t in range(TT):
                if t + 1 < TT:
                    ln_stats(-1, t + 1)
                ln_apply(-1, t)
                ln_unit(-1, t)
            with dve.Fori(0, B - 1) as b:
                batch(b, True)
            batch(B - 1, False)

        @block.tensor
        def _(pe):
            pe.sem_inc(zacc_full, 1)
            pe.sem_inc(s_full, 1)
            pe.wait_ge(consts, 16 * 5)

            def bank(b, k):
                if not (ahead(b) and k < RING):
                    pe.wait_ge(lo_done, G(b, k) - lag(k) + 1)
                return ring[:, k % RING, :]

            def product(out, lhs, rhs):
                for c in range(KC):
                    for n, (a, r) in enumerate(PARTS):
                        last = nc.tensor.matmul(out, lhs(a, c), rhs(r, c), start=(c == 0 and n == 0),
                                                stop=(c == KC - 1 and n == len(PARTS) - 1))
                return last

            def transpose_z(b, t):
                out = bank(b, t if ahead(b) else order(b, "ln", t))
                pe.wait_ge(z_done, (b + 1) * TT + t + 1)
                for c in range(KC):
                    last = nc.tensor.transpose(out[:, c * P:(c + 1) * P], z[:, t % 2, c * P:(c + 1) * P], ident[:, :])
                last.then_inc(unit_full, 1)

            def score(b, i):
                if i == 0:
                    pe.wait_ge(lo_done, G(b, order(b, "q", 0) + KC - 1) + 1)
                if i == TT // 2:
                    pe.wait_ge(lo_done, G(b, order(b, "q", 1) + KC - 1) + 1)
                pe.wait_ge(p_done, 1 + (b * TT + i - 1 if i >= 2 else b * TT))
                q = slice((i % 4) * P, (i % 4 + 1) * P)
                for at in range(0, (i + 1) * P, 512):
                    n = at + min(512, max(256, (i + 1) * P - at))
                    last = product(scores[:, i % 2, at:n], lambda a, c: qT[:, a, c, q],
                                   lambda r, c: kT[:, r, c, at:n])
                last.then_inc(s_full, 1)

            def transpose_p(b, i):
                pe.wait_ge(p_done, 1 + b * TT + i + 1)
                for u in range(PT_UNITS[i]):
                    out = bank(b, order(b, "pt", i) + u)
                    for j in range(4 * u, min(4 * u + 4, i + 1)):
                        last = nc.tensor.transpose(out[:, (j % 4) * P:(j % 4 + 1) * P],
                                                   probs[:, i % 2, j * P:(j + 1) * P], ident[:, :])
                    last.then_inc(unit_full, 1)

            def times_v(b, i):
                pe.wait_ge(lo_done, G(b, order(b, "pt", i) + PT_UNITS[i]))
                pe.wait_ge(combined, 1 + b * TT + i)
                for j in range(i + 1):
                    for n, (a, r) in enumerate(PARTS):
                        last = nc.tensor.matmul(zacc[:, :], pT[:, i % 2, a, j, :], v[:, r, j, :],
                                                start=(j == 0 and n == 0), stop=(j == i and n == len(PARTS) - 1))
                last.then_inc(zacc_full, 1)

            def q_units(b, blk):
                for c in range(KC):
                    out = bank(b, order(b, "q", blk) + c)
                    product(out, lambda a, d: wq[:, a, d, c * P:(c + 1) * P],
                            lambda r, d: zT[:, r, d, blk * 512:(blk + 1) * 512]).then_inc(unit_full, 1)

            def batch(b, prefetch):
                pe.wait_ge(lo_done, G(b, 0))
                for c in range(KC):
                    for n in range(NBLK):
                        out = bank(b, K0 + c * NBLK + n)
                        product(out, lambda a, d: wk[:, a, d, c * P:(c + 1) * P],
                                lambda r, d: zT[:, r, d, n * 512:(n + 1) * 512]).then_inc(unit_full, 1)
                for t in range(TT):
                    out = bank(b, V0 + t)
                    product(out, lambda a, d: zT[:, a, d, t * P:(t + 1) * P],
                            lambda r, d: wv[:, r, d, :]).then_inc(unit_full, 1)
                q_units(b, 0)
                score(b, 0)
                for i in range(TT):
                    if i == TT // 2 - 1:
                        q_units(b, 1)
                    if i + 1 < TT:
                        score(b, i + 1)
                    transpose_p(b, i)
                    if prefetch and i >= TT // 2:
                        transpose_z(b, 2 * (i - TT // 2))
                        transpose_z(b, 2 * (i - TT // 2) + 1)
                    if i >= 1:
                        times_v(b, i - 1)
                times_v(b, TT - 1)

            for t in range(TT):
                transpose_z(-1, t)
            pe.wait_ge(w_lo, 3)
            with pe.Fori(0, B - 1) as b:
                batch(b, True)
            batch(B - 1, False)


def cross_keys_values(nc, ctxT, wkT, wvT, bk, bv, ident_in, k_out, v_out):
    ctx = ExitStack()
    with ctx:
        def sb(name, shape, dt=FP32):
            return ctx.enter_context(nc.sbuf_tensor("kv_" + name, shape, dt))

        def sem(name):
            return ctx.enter_context(nc.semaphore("kv_" + name))

        wk = sb("wk", [P, 2, KC, D], FP32R)
        wv = sb("wv", [P, 2, KC, D], FP32R)
        raw = sb("raw", [P, 2, KC, STRIDE * KEYS])
        c_hl = sb("c_hl", [P, 2, KC, STRIDE * KEYS], FP32R)
        k_hl = sb("k_hl", [P, 2, 2, KEYS], FP32R)
        vT = sb("vT", [P, 2, KEYS])
        v_sb = sb("v_sb", [P, 2, KT, P])
        bkv = sb("bkv", [P, 2, STRIDE])
        ident = sb("ident", [P, P])
        k_ps = [ctx.enter_context(nc.psum_tensor(f"kv_k{i}", [P, KEYS], FP32)) for i in range(2)]
        vT_ps = [ctx.enter_context(nc.psum_tensor(f"kv_vT{i}", [P, KEYS], FP32)) for i in range(2)]
        v_ps = [ctx.enter_context(nc.psum_tensor(f"kv_v{i}", [P, KT * P], FP32)) for i in range(2)]

        consts = sem("consts")
        w_loaded = sem("w_loaded")
        w_hi = sem("w_hi")
        w_lo = sem("w_lo")
        raw_in = sem("raw_in")
        c_hi = sem("c_hi")
        c_lo = sem("c_lo")
        k_full = sem("k_full")
        k_hi = sem("k_hi")
        k_lo = sem("k_lo")
        vT_full = sem("vT_full")
        vT_done = sem("vT_done")
        v_full = sem("v_full")
        v_done = sem("v_done")
        k_stored = [sem(f"k_stored{i}") for i in range(2)]
        v_stored = [sem(f"v_stored{i}") for i in range(2)]
        block = ctx.enter_context(nc.Block())
        R = STRIDE

        @block.sync
        def _(sp):
            for j in range(2):
                sp.sem_inc(k_stored[j], 16)
            for j in range(2):
                sp.sem_inc(v_stored[j], 16)
            sp.dma_start(ident[:, :], ident_in).then_inc(consts, 16)
            sp.dma_start(bkv[:, 0, :], bk).then_inc(consts, 16)
            sp.dma_start(bkv[:, 1, :], bv).then_inc(consts, 16)
            for w, src in enumerate((wkT, wvT)):
                sp.dma_start(raw[:, w, :, 0:D], src).then_inc(w_loaded, 16)
            sp.wait_ge(w_lo, 2)
            sp.dma_start(raw[:, 0, :, :], ctxT[0]).then_inc(raw_in, 16)

            def batch(b, prefetch):
                if prefetch:
                    sp.wait_ge(c_lo, b + 1)
                    sp.dma_start(raw[:, 0, :, :], ctxT[bass.ds(b + 1, 1), :, :, :].rearrange("o p c s -> p (o c) s")
                                 ).then_inc(raw_in, 16)
                for r in range(R):
                    n = b * R + r
                    sp.wait_ge(k_lo, 1 + n + 1)
                    sp.dma_start(k_out[bass.ds(n, 1), :, :, :].rearrange("o p h s -> p (o h) s"),
                                 k_hl[:, r % 2, :, :].bitcast(FP32)).then_inc(k_stored[r % 2], 16)
                    sp.wait_ge(v_done, 1 + n + 1)
                    sp.dma_start(v_out[bass.ds(n, 1), :, :, :].rearrange("o p c d -> p (o c) d"),
                                 v_sb[:, r % 2, :, :]).then_inc(v_stored[r % 2], 16)

            with sp.Fori(0, B - 1) as b:
                batch(b, True)
            batch(B - 1, False)
            for i in range(2):
                sp.wait_ge(k_stored[i], 16 + 16 * B * R // 2)
                sp.wait_ge(v_stored[i], 16 + 16 * B * R // 2)

        @block.scalar
        def _(act):
            act.sem_inc(vT_done, 1)
            act.wait_ge(consts, 48)
            for w, dst in enumerate((wk, wv)):
                act.wait_ge(w_loaded, 32)
                nc.scalar.copy(dst[:, HI, :, :], raw[:, w, :, 0:D]).then_inc(w_hi, 1)
            with act.Fori(0, B) as b:
                act.wait_ge(raw_in, 16 * b + 16)
                act.wait_ge(vT_full, 1 + b * R)
                nc.scalar.copy(c_hl[:, HI, :, :], raw[:, 0, :, :]).then_inc(c_hi, 1)
                for r in range(R):
                    n = b * R + r
                    act.wait_ge(k_full, n + 1)
                    act.wait_ge(k_stored[r % 2], 16 + 16 * (b * (R // 2) + r // 2))
                    nc.scalar.activation(k_hl[:, r % 2, HI, :], k_ps[r % 2][:, :], ACT.Identity,
                                         bias=bkv[:, 0, r:r + 1]).then_inc(k_hi, 1)
                    act.wait_ge(vT_full, 1 + n + 1)
                    act.wait_ge(v_full, 1 + (n - 1 if r >= 2 else b * R))
                    nc.scalar.activation(vT[:, r % 2, :], vT_ps[r % 2][:, :], ACT.Identity,
                                         bias=bkv[:, 1, r:r + 1]).then_inc(vT_done, 1)

        @block.vector
        def _(dve):
            dve.sem_inc(k_lo, 1)
            dve.sem_inc(v_done, 1)
            dve.wait_ge(consts, 48)
            for w, dst in enumerate((wk, wv)):
                dve.wait_ge(w_hi, w + 1)
                nc.vector.tensor_tensor(dst[:, LO, :, :], raw[:, w, :, 0:D], dst[:, HI, :, :].bitcast(FP32),
                                        ALU.subtract).then_inc(w_lo, 1)
            with dve.Fori(0, B) as b:
                dve.wait_ge(c_hi, b + 1)
                nc.vector.tensor_tensor(c_hl[:, LO, :, :], raw[:, 0, :, :], c_hl[:, HI, :, :].bitcast(FP32),
                                        ALU.subtract).then_inc(c_lo, 1)
                for r in range(R):
                    n = b * R + r
                    dve.wait_ge(k_hi, n + 1)
                    nc.vector.scalar_tensor_tensor(k_hl[:, r % 2, LO, :], k_ps[r % 2][:, :], bkv[:, 0, r:r + 1],
                                                   k_hl[:, r % 2, HI, :].bitcast(FP32), ALU.add, ALU.subtract
                                                   ).then_inc(k_lo, 1)
                    dve.wait_ge(v_full, 1 + n + 1)
                    dve.wait_ge(v_stored[r % 2], 16 + 16 * (b * (R // 2) + r // 2))
                    nc.vector.tensor_copy(v_sb[:, r % 2, :, :], v_ps[r % 2][:, :].rearrange("p (c d) -> p c d", d=P)
                                          ).then_inc(v_done, 1)

        @block.tensor
        def _(pe):
            pe.sem_inc(vT_full, 1)
            pe.sem_inc(v_full, 1)
            pe.wait_ge(consts, 48)

            def project(out, w, r):
                for c in range(KC):
                    for n, (a, h) in enumerate(PARTS):
                        last = nc.tensor.matmul(out, w[:, a, c, r * P:(r + 1) * P],
                                                c_hl[:, h, c, r * KEYS:(r + 1) * KEYS],
                                                start=(c == 0 and n == 0), stop=(c == KC - 1 and n == 2))
                return last

            with pe.Fori(0, B) as b:
                pe.wait_ge(c_lo, b + 1)
                for r in range(R):
                    n = b * R + r
                    pe.wait_ge(k_lo, 1 + (n - 1 if r >= 2 else b * R))
                    project(k_ps[r % 2][:, :], wk, r).then_inc(k_full, 1)
                    pe.wait_ge(vT_done, 1 + (n - 1 if r >= 2 else b * R))
                    project(vT_ps[r % 2][:, :], wv, r).then_inc(vT_full, 1)
                    pe.wait_ge(vT_done, 1 + n + 1)
                    pe.wait_ge(v_done, 1 + (n - 1 if r >= 2 else b * R))
                    for c in range(KT):
                        last = nc.tensor.transpose(v_ps[r % 2][:, c * P:(c + 1) * P],
                                                   vT[:, r % 2, c * P:(c + 1) * P], ident[:, :])
                    last.then_inc(v_full, 1)


def cross_attention(nc, x1, wqT, woT, bq, bo, mask, mask_keys, k_in, v_in, ident_in, x2):
    scale = float(HD) ** -0.5
    QT = 4
    NG = NBLK * STRIDE
    NH = NG * GH
    RING = 4
    MBUF = 4
    STACKED = 16 * 4
    SPH = QT // 2
    OUT_TILES = {(1, j): (j,) for j in range(GH)}
    LN_TILES = ((), (0, 1), (2, 3), ())

    def plan(prefetch, first=False):
        units = [("z", 2, t) for t in range(QT)] + [("q", NG), ("q", NG + 1)] if first else []
        for n in range(NG if first else 2, NG + 2 if prefetch else NG):
            for j in range(GH):
                if n % 4 == 1 and prefetch:
                    units += [("z", n // 4 + 1, t) for t in LN_TILES[j - 1]]
                if j == 0 and (n + 2 < NG or prefetch):
                    units += [("q", n + 2)]
                if not (first and n == NG):
                    units += {1: [("r", n - 1)], 2: [("c", n - 1)]}.get(j, [])
                if not first:
                    units += [("o", n // 4 - 1, t) for t in OUT_TILES.get((n % 4, j), ())]
        if not prefetch:
            units += [("r", NG - 1), ("c", NG - 1)] + [("o", 1, t) for t in range(QT)]
        table, acts = {}, 0
        for i, what in enumerate(units):
            acts += what[0] in "zq"
            table[what] = dict(full=i + 1, act=acts, bank=(i - (len(units) if first else 0)) % RING)
        assert first or not prefetch or len(units) % RING == 0
        return table, len(units), acts

    FIRST, LOOPED, LAST = plan(True, True), plan(True), plan(False)

    def of(b):
        return FIRST if ahead(b) else LAST if isinstance(b, int) and b == B - 1 else LOOPED

    def base(b, which):
        return 0 if ahead(b) else FIRST[which] + b * LOOPED[which]

    def behind(b, n):
        return not (ahead(b) and n == NG)

    def ctx_groups(b, n, j):
        if ahead(b) and n == NG or n % 4 == 1:
            return []
        return [n - 2] if n % 4 == 2 and j == 0 else [n - 1] if j == GH - 1 else []

    def out_tiles(b, n, j):
        return [] if ahead(b) else [(n // 4 - 1, t) for t in OUT_TILES.get((n % 4, j), ())]

    def steps(b, prefetch):
        return [(n, j, n * GH + j) for n in range(NG if ahead(b) else 2, NG + 2 if prefetch else NG)
                for j in range(GH)]

    ctx = ExitStack()
    with ctx:
        def sb(name, shape, dt=FP32):
            return ctx.enter_context(nc.sbuf_tensor("x_" + name, shape, dt))

        def sem(name):
            return ctx.enter_context(nc.semaphore("x_" + name))

        wq = sb("wq", [P, 2, KC, D], FP32R)
        wo = sb("wo", [P, 2, KC, D], FP32R)
        k_st = sb("k_st", [P, STRIDE, GH, KEYS], FP32R)
        v_sb = sb("v_sb", [P, STRIDE, KT, P])
        q_hl = sb("q_hl", [P, 2, 2, 512], FP32R)
        q_st = sb("q_st", [P, 2, GH, 512], FP32R)
        zT = sb("zT", [P, 2, KC, 512], FP32R)
        masked = sb("masked", [P, 2, QT, KEYS])
        diag = sb("diag", [P, 2, QT, P], FP32R)
        neg_ones = sb("neg_ones", [P, P], FP32R)
        ones = sb("ones", [P, HD])
        pT = sb("pT", [P, 2, GH, KT, 512])
        ctxn = sb("ctxn", [P, 2, 512])
        r_sb = sb("r_sb", [P, 2, 512])
        cT = sb("cT", [P, 2, STRIDE, 512], FP32R)
        xln = sb("xln", [P, QT, D])
        z = sb("z", [P, 2, D])
        xres = sb("xres", [P, QT, D])
        bo_rep = sb("bo_rep", [P, D])
        ident = sb("ident", [P, P])
        bq_sb = sb("bq_sb", [P, STRIDE])
        mask_u8 = sb("mask_u8", [P, STRIDE, KEYS], U8)
        mask_add = sb("mask_add", [P, STRIDE, KEYS])
        mask_keys_u8 = sb("mask_keys_u8", [P, STRIDE, KT], U8)
        mask_bias = sb("mask_bias", [P, STRIDE, KT])
        stats = sb("stats", [P, 2, 6])
        mv = sb("mv", [P, 2, 2])
        rstd = sb("rstd", [P, 2, 2])
        half = sb("half", [P, 1])
        mx = sb("mx", [P, MBUF, QT])
        w_stage = pT[:, 0, :, :, :].rearrange("p j c q -> p (j c) q")

        ring = ctx.enter_context(nc.psum_tensor("x_ring", [P, RING, 512], FP32))
        sps = ctx.enter_context(nc.psum_tensor("x_sps", [P, SPH, 512], FP32))
        stps = ctx.enter_context(nc.psum_tensor("x_stps", [P, KT, 512], FP32))

        waited = sem("waited")
        consts = sem("consts")
        wq_loaded = sem("wq_loaded")
        wo_loaded = sem("wo_loaded")
        w_hi = sem("w_hi")
        w_lo = sem("w_lo")
        half_set = sem("half_set")
        xln_in = [sem(f"xln_in{j}") for j in range(QT)]
        xres_in = [sem(f"xres_in{j}") for j in range(QT)]
        stored = [sem(f"stored{j}") for j in range(QT)]
        k_loaded = [sem(f"k_loaded{r}") for r in range(STRIDE)]
        v_loaded = [sem(f"v_loaded{r}") for r in range(STRIDE)]
        mask_in = sem("mask_in")
        mask_done = sem("mask_done")
        q_stacked = [[sem(f"q_stacked{p}{j}") for j in range(GH)] for p in range(2)]
        stats_done = sem("stats_done")
        mv_done = sem("mv_done")
        var_eps = sem("var_eps")
        rstd_done = sem("rstd_done")
        z_done = sem("z_done")
        unit_full = sem("unit_full")
        act_done = sem("act_done")
        s_full = sem("s_full")
        max_done = sem("max_done")
        diag_done = sem("diag_done")
        st_full = sem("st_full")
        p_done = sem("p_done")
        dve_done = sem("dve_done")
        ones_set = sem("ones_set")
        cT_hi = sem("cT_hi")
        cT_lo = sem("cT_lo")
        xb_done = sem("xb_done")
        block = ctx.enter_context(nc.Block())

        def carry(engine):
            engine.sem_inc(waited, 1)

        @block.sync
        def _(sp):
            for j in range(4):
                sp.sem_inc(stored[j], 16)
            sp.dma_start(ident[:, :], ident_in).then_inc(consts, 16)
            sp.dma_start(bq_sb[:, :], bq).then_inc(consts, 16)
            sp.dma_start(bo_rep[:, :], bo.partition_broadcast(P)).then_inc(consts, 16)

            def tile_of(b, blk, t):
                return b * TT + blk * QT + t

            def load_ln(b, blk, t):
                n = tile_of(b, blk, t)
                if not (isinstance(n, int) and n < QT):
                    sp.wait_ge(z_done, n - QT + 1)
                sp.dma_start(xln[:, t, :], x1[bass.ds(n, 1), :, :].rearrange("o p d -> (o p) d")
                             ).then_inc(xln_in[t], 16)

            def load_res(b, blk):
                for t in range(QT):
                    sp.wait_ge(stored[t], 16 + 16 * (b * NBLK + blk))
                    sp.dma_start(xres[:, t, :], x1[bass.ds(tile_of(b, blk, t), 1), :, :].rearrange("o p d -> (o p) d")
                                 ).then_inc(xres_in[t], 16)

            def store(b, blk):
                for t in range(QT):
                    sp.wait_ge(dve_done, base(b, 1) + of(b)[0]["o", blk, t]["full"])
                    sp.dma_start(x2[bass.ds(tile_of(b, blk, t), 1), :, :].rearrange("o p d -> (o p) d"),
                                 xres[:, t, :]).then_inc(stored[t], 16)

            def load_k(b, r):
                if not (isinstance(b, int) and b == 0):
                    sp.wait_ge(st_full, ((b - 1) * NH + (STRIDE + r + 1) * GH) * KT)
                for part in range(4):
                    sp.dma_start(k_st[part * HD:(part + 1) * HD, r, :, :].bitcast(FP32),
                                 k_in[bass.ds(b * STRIDE + r, 1), :, part % 2, :].rearrange(
                                     "o (j d) s -> d (o j) s", d=HD)).then_inc(k_loaded[r], 16)

            def load_v(b, r):
                if not (isinstance(b, int) and b == 0):
                    sp.wait_ge(unit_full, base(b - 1, 1) + LOOPED[0]["c", STRIDE + r]["full"])
                sp.dma_start(v_sb[:, r, :, :], v_in[bass.ds(b * STRIDE + r, 1), :, :, :].rearrange(
                    "o p c d -> p (o c) d")).then_inc(v_loaded[r], 16)

            def load_mask(b):
                sp.dma_start(mask_u8[:, :, :].rearrange("p r s -> p (r s)"), mask[bass.ds(b, 1), :].rearrange(
                    "o s -> (o s)").partition_broadcast(P)).then_inc(mask_in, 16)
                sp.dma_start(mask_keys_u8[:, :, :], mask_keys[bass.ds(b, 1), :, :, :].rearrange(
                    "o p r c -> (o p) r c")).then_inc(mask_in, 16)

            def stack_q(b, n):
                sp.wait_ge(dve_done, base(b, 1) + of(b)[0]["q", n]["full"])
                for j in range(GH):
                    if not ahead(b) or n >= NG + 2:
                        sp.wait_ge(st_full, (b * NH + (n - 2) * GH + j + 1) * KT)
                    for part in range(4):
                        sp.dma_start(q_st[part * HD:(part + 1) * HD, n % 2, j, :].bitcast(FP32),
                                     q_hl[j * HD:(j + 1) * HD, n % 2, part // 2, :].bitcast(FP32)
                                     ).then_inc(q_stacked[n % 2][j], 16)

            for t in range(QT):
                load_ln(-1, 2, t)
            sp.dma_start(w_stage[:, 0:KC, :], wqT).then_inc(wq_loaded, 16)
            sp.dma_start(w_stage[:, KC:2 * KC, :], woT).then_inc(wo_loaded, 16)
            load_mask(0)
            for r in range(STRIDE):
                load_k(0, r)
                load_v(0, r)
            for t in range(QT):
                load_ln(-1, 3, t)
            stack_q(-1, NG)
            stack_q(-1, NG + 1)
            stack_q(-1, NG + 2)
            stack_q(-1, NG + 3)

            def batch(b, prefetch):
                stack_q(b, 4)
                load_res(b, 0)
                stack_q(b, 5)
                if prefetch:
                    sp.wait_ge(mask_done, (b + 1) * STRIDE * 2)
                    carry(sp)
                    load_mask(b + 1)
                stack_q(b, 6)
                if prefetch:
                    load_k(b + 1, 0)
                    for t in range(QT):
                        load_ln(b, 2, t)
                stack_q(b, 7)
                store(b, 0)
                if prefetch:
                    load_k(b + 1, 1)
                    load_v(b + 1, 0)
                    stack_q(b, 8)
                    load_k(b + 1, 2)
                    load_v(b + 1, 1)
                load_res(b, 1)
                if prefetch:
                    stack_q(b, 9)
                    load_k(b + 1, 3)
                    load_v(b + 1, 2)
                    for t in range(QT):
                        load_ln(b, 3, t)
                    stack_q(b, 10)
                    load_v(b + 1, 3)
                    stack_q(b, 11)
                store(b, 1)

            with sp.Fori(0, B - 1) as b:
                batch(b, True)
            batch(B - 1, False)
            for j in range(QT):
                sp.wait_ge(stored[j], 16 + 16 * B * NBLK)

        def ln_tiles(b, n, j, late=0):
            blk, j = n // 4 + 1, j - late
            if n % 4 != 1 or not 0 <= j < GH:
                return []
            return [(blk, t, b * TT + blk * QT + t) for t in LN_TILES[j]]

        @block.gpsimd
        def _(pool):
            pool.sem_inc(cT_lo, 1)
            nc.gpsimd.memset(half[:, :], -0.5).then_inc(half_set, 1)
            nc.gpsimd.memset(ones[:, :], 1.0).then_inc(ones_set, 1)
            pool.wait_ge(half_set, 1)
            pool.wait_ge(consts, 16 * 3)

            def ln_rstd(t, n):
                pool.wait_ge(mv_done, n + 1)
                carry(pool)
                nc.gpsimd.tensor_scalar(rstd[:, t % 2, 0:1], mv[:, t % 2, 1:2], EPS, None, ALU.add
                                        ).then_inc(var_eps, 1)
                pool.wait_ge(var_eps, n + 1)
                nc.gpsimd.tensor_tensor(rstd[:, t % 2, 1:2], rstd[:, t % 2, 0:1], half[:, :], ALU.pow
                                        ).then_inc(rstd_done, 1)

            def add_bo(b, blk):
                for t in range(QT):
                    pool.wait_ge(xres_in[t], 16 * (b * NBLK + blk + 1))
                    nc.gpsimd.tensor_tensor(xres[:, t, :], xres[:, t, :], bo_rep[:, :], ALU.add).then_inc(xb_done, 1)

            def ctx_lo(b, n):
                g = b * NG + n
                pool.wait_ge(cT_hi, g + 1)
                nc.gpsimd.tensor_tensor(cT[:, LO, n % 4, :], ctxn[:, n % 2, :], cT[:, HI, n % 4, :].bitcast(FP32),
                                        ALU.subtract).then_inc(cT_lo, 1)

            def diagonal(b, k):
                pool.wait_ge(max_done, (b * NH + k + 1) * QT)
                if not (ahead(b) and k < NH + 2):
                    pool.wait_ge(st_full, (b * NH + k - 1) * KT)
                nc.gpsimd.tensor_tensor(diag[:, k % 2, :, :], ident[:, None, :].broadcast_to((P, QT, P)),
                                        mx[:, k % MBUF, :][:, :, None].broadcast_to((P, QT, P)), ALU.mult
                                        ).then_inc(diag_done, 1)

            def batch(b, prefetch):
                for n, j, k in steps(b, prefetch):
                    if k + 2 < NH or prefetch:
                        diagonal(b, k + 2)
                    if prefetch:
                        for blk, t, m in ln_tiles(b, n, j):
                            ln_rstd(t, m)
                    for g in ctx_groups(b, n, j):
                        ctx_lo(b, g)
                    if j == GH - 1 and n % 4 == 3 and not ahead(b):
                        add_bo(b, n // 4)
                if not prefetch:
                    ctx_lo(b, NG - 1)

            for t in range(QT):
                ln_rstd(t, t)
            diagonal(-1, NH)
            diagonal(-1, NH + 1)
            batch(-1, True)
            with pool.Fori(0, B - 1) as b:
                batch(b, True)
            batch(B - 1, False)

        @block.scalar
        def _(act):
            act.wait_ge(consts, 16 * 3)

            def unit(b, *what):
                u = of(b)[0][what]
                act.wait_ge(unit_full, base(b, 1) + u["full"])
                return ring[:, u["bank"], :]

            def z_hi(b, blk, t):
                src = unit(b, "z", blk, t).rearrange("p (c n) -> p c n", n=P)
                nc.scalar.copy(zT[:, HI, :, t * P:(t + 1) * P], src).then_inc(act_done, 1)

            def q_hi(b, n):
                src = unit(b, "q", n)
                if not (ahead(b) and n < NG + 2):
                    for j in range(GH):
                        act.wait_ge(q_stacked[n % 2][j], STACKED * (b * (NG // 2) + n // 2))
                nc.scalar.activation(q_hl[:, n % 2, HI, :], src, ACT.Identity,
                                     bias=bq_sb[:, n % 4:n % 4 + 1]).then_inc(act_done, 1)

            def exps(b, k):
                n, j = k // GH, k % GH
                for c in range(KT):
                    act.wait_ge(st_full, (b * NH + k) * KT + c + 1)
                    nc.scalar.activation(pT[:, n % 2, j, c, :], stps[:, c, :], ACT.Exp, scale=scale,
                                         bias=mask_bias[:, n % 4, c:c + 1]).then_inc(p_done, 1)

            def ctx_hi(b, n):
                act.wait_ge(dve_done, base(b, 1) + (of(b)[0]["c", n]["full"] if n > 0 else 0))
                nc.scalar.copy(cT[:, HI, n % 4, :], ctxn[:, n % 2, :]).then_inc(cT_hi, 1)

            def batch(b, prefetch):
                for n, j, k in steps(b, prefetch):
                    if prefetch:
                        for blk, t, m in ln_tiles(b, n, j, late=1):
                            z_hi(b, blk, t)
                    exps(b, k)
                    if j == 0 and (n + 2 < NG or prefetch):
                        q_hi(b, n + 2)
                    for g in ctx_groups(b, n, j):
                        ctx_hi(b, g)
                if not prefetch:
                    ctx_hi(b, NG - 1)

            act.wait_ge(wq_loaded, 16)
            nc.scalar.copy(wq[:, HI, :, :], w_stage[:, 0:KC, :]).then_inc(w_hi, 1)
            for t in range(QT):
                z_hi(-1, 2, t)
            act.wait_ge(wo_loaded, 16)
            nc.scalar.copy(wo[:, HI, :, :], w_stage[:, KC:2 * KC, :]).then_inc(w_hi, 1)
            q_hi(-1, NG)
            q_hi(-1, NG + 1)
            batch(-1, True)
            with act.Fori(0, B - 1) as b:
                batch(b, True)
            batch(B - 1, False)

        @block.vector
        def _(dve):
            dve.wait_ge(consts, 16 * 3)

            def unit(b, *what):
                u = of(b)[0][what]
                if what[0] in "zq":
                    dve.wait_ge(act_done, base(b, 2) + u["act"])
                else:
                    dve.wait_ge(unit_full, base(b, 1) + u["full"])
                return ring[:, u["bank"], :]

            def ln_stats(t, n):
                dve.wait_ge(xln_in[t], 4 * (n - t) + 16)
                nc.vector.bn_stats(stats[:, t % 2, :], xln[:, t, :]).then_inc(stats_done, 1)
                dve.wait_ge(stats_done, n + 1)
                carry(dve)
                nc.vector.bn_aggr(mv[:, t % 2, :], stats[:, t % 2, :]).then_inc(mv_done, 1)

            def ln_apply(t, n):
                dve.wait_ge(rstd_done, n + 1)
                nc.vector.tensor_scalar(z[:, t % 2, :], xln[:, t, :], mv[:, t % 2, 0:1], rstd[:, t % 2, 1:2],
                                        ALU.subtract, ALU.mult).then_inc(z_done, 1)

            def z_lo(b, blk, t):
                src = unit(b, "z", blk, t).rearrange("p (c n) -> p c n", n=P)
                at = slice(t * P, (t + 1) * P)
                nc.vector.tensor_tensor(zT[:, LO, :, at], src, zT[:, HI, :, at].bitcast(FP32), ALU.subtract
                                        ).then_inc(dve_done, 1)

            def q_lo(b, n):
                nc.vector.scalar_tensor_tensor(q_hl[:, n % 2, LO, :], unit(b, "q", n), bq_sb[:, n % 4:n % 4 + 1],
                                               q_hl[:, n % 2, HI, :].bitcast(FP32), ALU.add, ALU.subtract
                                               ).then_inc(dve_done, 1)

            def mask_to_add(b, r):
                dve.wait_ge(mask_in, 32 * (b + 1))
                if not (isinstance(b, int) and b == 0):
                    dve.wait_ge(p_done, ((b - 1) * NH + (STRIDE + r + 1) * GH) * KT)
                nc.vector.tensor_scalar(mask_bias[:, r, :], mask_keys_u8[:, r, :], -1e30, None, ALU.mult
                                        ).then_inc(mask_done, 1)
                nc.vector.tensor_scalar(mask_add[:, r, :], mask_u8[:, r, :], -1e30, None, ALU.mult
                                        ).then_inc(mask_done, 1)

            def maxima(b, k):
                r = k // GH % STRIDE
                if not (ahead(b) and k < NH + 2):
                    dve.wait_ge(max_done, (b * NH + k - 1) * QT)
                for q in range(QT):
                    u = k * SPH + q // 2
                    if q % 2 == 0:
                        dve.wait_ge(s_full, b * NH * SPH + u + 1)
                        carry(dve)
                    nc.vector.tensor_tensor_reduce(
                        out=masked[:, k % 2, q, :], in0=sps[:, u % SPH, q % 2 * KEYS:(q % 2 + 1) * KEYS],
                        in1=mask_add[:, r, :], scale=1.0, scalar=-3.4e38, op0=ALU.add, op1=ALU.max,
                        accum_out=mx[:, k % MBUF, q:q + 1]).then_inc(max_done, 1)

            def reciprocal(b, n):
                nc.vector.reciprocal(r_sb[:, n % 2, :], unit(b, "r", n)).then_inc(dve_done, 1)

            def normalise(b, n):
                src = unit(b, "c", n)
                dve.wait_ge(dve_done, base(b, 1) + of(b)[0]["r", n]["full"])
                if not ahead(b):
                    dve.wait_ge(cT_lo, 1 + b * NG + n - 1)
                nc.vector.tensor_tensor(ctxn[:, n % 2, :], src, r_sb[:, n % 2, :], ALU.mult).then_inc(dve_done, 1)

            def output(b, blk, t):
                src = unit(b, "o", blk, t)
                dve.wait_ge(xb_done, (b * NBLK + blk) * QT + t + 1)
                nc.vector.tensor_tensor(xres[:, t, :], src, xres[:, t, :], ALU.add).then_inc(dve_done, 1)

            def batch(b, prefetch):
                for n, j, k in steps(b, prefetch):
                    if k + 2 < NH or prefetch:
                        if j == 1 and 5 <= n <= NG and prefetch and not ahead(b):
                            mask_to_add(b + 1, n - 5)
                        maxima(b, k + 2)
                    if prefetch:
                        for blk, t, m in ln_tiles(b, n, j, late=1):
                            z_lo(b, blk, t)
                    if j == 0 and (n + 2 < NG or prefetch):
                        q_lo(b, n + 2)
                    if j == 1 and behind(b, n):
                        reciprocal(b, n - 1)
                    if j == 2 and behind(b, n):
                        normalise(b, n - 1)
                    for blk, t in out_tiles(b, n, j):
                        output(b, blk, t)
                    if prefetch:
                        for blk, t, m in ln_tiles(b, n, j):
                            ln_apply(t, m)
                        for blk, t, m in ln_tiles(b, n, j, late=-1):
                            ln_stats(t, m)
                if not prefetch:
                    reciprocal(b, NG - 1)
                    normalise(b, NG - 1)
                    for t in range(QT):
                        output(b, 1, t)

            nc.vector.tensor_scalar(neg_ones[:, :], ident[:, :], 0.0, -1.0, ALU.mult, ALU.add).then_inc(ones_set, 1)

            def split(w, dst):
                dve.wait_ge(w_hi, w + 1)
                nc.vector.tensor_tensor(dst[:, LO, :, :], w_stage[:, w * KC:(w + 1) * KC, :],
                                        dst[:, HI, :, :].bitcast(FP32), ALU.subtract).then_inc(w_lo, 1)

            for t in range(2):
                ln_stats(t, t)
                ln_apply(t, t)
            split(0, wq)
            for t in range(2):
                z_lo(-1, 2, t)
            for t in range(2, QT):
                ln_stats(t, t)
                ln_apply(t, t)
                z_lo(-1, 2, t)
            for r in range(STRIDE):
                mask_to_add(0, r)
            split(1, wo)
            q_lo(-1, NG)
            maxima(-1, NH)
            maxima(-1, NH + 1)
            q_lo(-1, NG + 1)
            batch(-1, True)
            with dve.Fori(0, B - 1) as b:
                batch(b, True)
            batch(B - 1, False)

        @block.tensor
        def _(pe):
            pe.wait_ge(consts, 16 * 3)

            def bank(b, *what):
                u = of(b)[0][what]
                if not (ahead(b) and u["full"] <= RING):
                    pe.wait_ge(dve_done, base(b, 1) + u["full"] - RING)
                return ring[:, u["bank"], :]

            def product(out, lhs, rhs):
                for c in range(KC):
                    for n, (a, r) in enumerate(PARTS):
                        last = nc.tensor.matmul(out, lhs(a, c), rhs(r, c), start=(c == 0 and n == 0),
                                                stop=(c == KC - 1 and n == len(PARTS) - 1))
                return last

            def transpose_z(b, blk, t, m):
                out = bank(b, "z", blk, t)
                pe.wait_ge(z_done, m + 1)
                for c in range(KC):
                    last = nc.tensor.transpose(out[:, c * P:(c + 1) * P], z[:, t % 2, c * P:(c + 1) * P], ident[:, :])
                last.then_inc(unit_full, 1)

            def queries(b, n):
                if n == 4:
                    pe.wait_ge(dve_done, base(b, 1))
                elif n % 4 == 0:
                    pe.wait_ge(dve_done, base(b, 1) + of(b)[0]["z", n // 4, QT - 1]["full"])
                r = n % 4
                out = bank(b, "q", n)
                product(out, lambda a, c: wq[:, a, c, r * P:(r + 1) * P], lambda h, c: zT[:, h, c, :]
                        ).then_inc(unit_full, 1)

            def scores(b, k):
                n, j = k // GH, k % GH
                r, nb = n % 4, n // NG
                pe.wait_ge(q_stacked[n % 2][j], STACKED * (b * (NG // 2) + n // 2 + 1))
                if j == 0:
                    pe.wait_ge(k_loaded[r], 64 * (b + nb + 1))
                for s in range(SPH):
                    u = k * SPH + s
                    if not (ahead(b) and u < (NH + 1) * SPH):
                        pe.wait_ge(max_done, (b * NH * SPH + u - SPH + 1) * 2)
                    for q in (2 * s, 2 * s + 1):
                        last = nc.tensor.matmul(sps[:, u % SPH, q % 2 * KEYS:(q % 2 + 1) * KEYS],
                                                q_st[:, n % 2, j, q * P:(q + 1) * P], k_st[:, r, j, :],
                                                start=True, stop=True)
                    last.then_inc(s_full, 1)

            def scores_by_key(b, n, j):
                k = n * GH + j
                for c in range(KT):
                    if not (ahead(b) and k == NH):
                        pe.wait_ge(p_done, (b * NH + k - 1) * KT + c + 1)
                    nc.tensor.matmul(stps[:, c, :], k_st[:, n % 4, j, c * P:(c + 1) * P], q_st[:, n % 2, j, :],
                                     start=True, stop=False)
                    if c == 0:
                        pe.wait_ge(diag_done, b * NH + k + 1)
                    nc.tensor.matmul(stps[:, c, :], neg_ones[:, :],
                                     diag[:, k % 2, :, :].rearrange("p q n -> p (q n)"), start=False, stop=True
                                     ).then_inc(st_full, 1)

            def sums(b, n):
                pe.wait_ge(p_done, (b * NH + (n + 1) * GH) * KT)
                out = bank(b, "r", n)
                for c in range(KT):
                    for j in range(GH):
                        last = nc.tensor.matmul(out[j * HD:(j + 1) * HD, :], ones[:, :], pT[:, n % 2, j, c, :],
                                                start=(c == 0), stop=(c == KT - 1))
                last.then_inc(unit_full, 1)

            def times_v(b, n):
                if n % NG < STRIDE:
                    pe.wait_ge(v_loaded[n % NG], 16 * (b + n // NG + 1))
                out = bank(b, "c", n)
                for c in range(KT):
                    for j in range(GH):
                        last = nc.tensor.matmul(out[j * HD:(j + 1) * HD, :], v_sb[:, n % 4, c, j * HD:(j + 1) * HD],
                                                pT[:, n % 2, j, c, :], start=(c == 0), stop=(c == KT - 1))
                last.then_inc(unit_full, 1)

            def outputs(b, tiles):
                for blk, t in tiles:
                    pe.wait_ge(cT_lo, 1 + b * NG + (blk + 1) * STRIDE)
                    out = bank(b, "o", blk, t)
                    product(out, lambda a, c: cT[:, a, c, t * P:(t + 1) * P], lambda h, c: wo[:, h, c, :]
                            ).then_inc(unit_full, 1)

            def batch(b, prefetch):
                for n, j, k in steps(b, prefetch):
                    if k + 2 < NH or prefetch:
                        scores(b, k + 2)
                    if prefetch:
                        for blk, t, m in ln_tiles(b, n, j, late=1):
                            transpose_z(b, blk, t, m)
                    scores_by_key(b, n, j)
                    if j == 0 and (n + 2 < NG or prefetch):
                        queries(b, n + 2)
                    if j == 1 and behind(b, n):
                        sums(b, n - 1)
                    if j == 2 and behind(b, n):
                        times_v(b, n - 1)
                    outputs(b, out_tiles(b, n, j))
                if not prefetch:
                    sums(b, NG - 1)
                    times_v(b, NG - 1)
                    outputs(b, [(1, t) for t in range(QT)])

            pe.wait_ge(ones_set, 2)
            for t in range(QT):
                transpose_z(-1, 2, t, t)
            pe.wait_ge(w_lo, 1)
            queries(-1, NG)
            scores(-1, NH)
            scores(-1, NH + 1)
            queries(-1, NG + 1)
            pe.wait_ge(w_lo, 2)
            batch(-1, True)
            with pe.Fori(0, B - 1) as b:
                batch(b, True)
            batch(B - 1, False)


def adapters(nc, x2, wd1, wd2, wb, bd1, bd2, b_base, wa_down, ba_down, wa_up, ba_up, ident_in, out):
    RING = 8
    NU = NBLK * E

    def plan(prefetch, first=False):
        if first:
            alloc = [("z", t) for t in range(TT)]
            read = list(alloc)
        else:
            alloc = [("h", 0), ("h", 1)]
            for u in range(NU):
                alloc += [("h", u + 2)] * (u + 2 < NU) + [("rec", u, c) for c in range(KC)]
            read = list(alloc)
            alloc += [("loss",), ("o", 0), ("o", 1), ("o", 2), ("a", 0), ("a", 1)]
            read += [("loss",), ("a", 0), ("a", 1), ("o", 0), ("o", 1), ("o", 2)]
            for t in range(3, TT):
                both = [("o", t)] + [("z", t - 3)] * prefetch
                alloc += both
                read += both
            if prefetch:
                alloc += [("z", t) for t in range(TT - 3, TT)]
                read += [("z", t) for t in range(TT - 3, TT)]
        acts = dves = 0
        table = {}
        for what in read:
            acts += what[0] in ("z", "h", "a")
            dves += what[0] in ("z", "rec", "loss", "o")
            table[what] = dict(full=len(table) + 1, act=acts, dve=dves, eng="act" if what[0] in ("h", "a") else "dve")
        for i, what in enumerate(alloc):
            table[what].update(i=i, bank=i % RING, freed=table[alloc[i - RING]] if i >= RING else None)
        return table, len(alloc), acts, dves

    FIRST, LOOPED, LAST = plan(False, True), plan(True), plan(False)

    def of(b):
        return FIRST if ahead(b) else LAST if isinstance(b, int) and b == B - 1 else LOOPED

    def base(b, which):
        return 0 if ahead(b) else FIRST[which] + b * LOOPED[which]

    ctx = ExitStack()
    with ctx:
        def sb(name, shape, dt=FP32):
            return ctx.enter_context(nc.sbuf_tensor("f_" + name, shape, dt))

        def sem(name):
            return ctx.enter_context(nc.semaphore("f_" + name))

        w1 = sb("w1", [P, 2, KC, E * H], FP32R)
        w2 = sb("w2", [H, 2, E, D], FP32R)
        wbase = sb("wbase", [P, 2, KC, D], FP32R)
        zT = sb("zT", [P, 2, KC, S], FP32R)
        zf = sb("zf", [P, KC, S])
        hf = sb("hf", [P, 2, 512])
        h = sb("h", [P, 3, 2, 512], FP32R)
        diff = sb("diff", [P, 2, KC, 512])
        dn_raw = sb("dn_raw", [P, KC, R])
        dn = sb("dn", [P, 2, KC, 2, R], FP32R)
        up_raw = sb("up_raw", [P, D])
        up = sb("up", [P, 2, D], FP32R)
        ba_dn = sb("ba_dn", [P, 1])
        ba_up_rep = sb("ba_up_rep", [P, D])
        af = sb("af", [P, 2, 512])
        a_hl = sb("a_hl", [P, 2, 512], FP32R)
        bb_rep = sb("bb_rep", [P, D])
        bsum = sb("bsum", [P, D])
        xln = sb("xln", [P, 2, D])
        z = sb("z", [P, 2, D])
        xres = sb("xres", [P, 4, D])
        ident = sb("ident", [P, P])
        b1 = sb("b1", [P, E])
        b2 = sb("b2", [P, E, KC])
        ones = sb("ones", [P, 1])
        sq = sb("sq", [P, NBLK, E])
        l8 = sb("l8", [1, E])
        neg = sb("neg", [1, E])
        best = sb("best", [1, 8])
        idx = sb("idx", [1, 8], U32)
        stats = sb("stats", [P, 2, 6])
        mv = sb("mv", [P, 2, 2])
        rstd = sb("rstd", [P, 2, 2])
        half = sb("half", [P, 1])
        stage = [diff[:, 0, :, :], diff[:, 1, :, :]]
        ring = ctx.enter_context(nc.psum_tensor("f_ring", [P, RING, 512], FP32))

        waited = sem("waited")
        consts = sem("consts")
        w_loaded = [sem(f"w_loaded{i}") for i in range(2)]
        w_hi = sem("w_hi")
        w_lo = sem("w_lo")
        half_set = sem("half_set")
        ones_set = sem("ones_set")
        xln_in = [sem(f"xln_in{j}") for j in range(2)]
        xres_in = [sem(f"xres_in{j}") for j in range(4)]
        stored = [sem(f"stored{j}") for j in range(4)]
        stats_done = sem("stats_done")
        mv_done = sem("mv_done")
        var_eps = sem("var_eps")
        rstd_done = sem("rstd_done")
        z_done = sem("z_done")
        zf_done = sem("zf_done")
        unit_full = sem("unit_full")
        act_done = sem("act_done")
        dve_done = sem("dve_done")
        h_hi = sem("h_hi")
        h_lo = sem("h_lo")
        sq_done = sem("sq_done")
        argmin_step = sem("argmin_step")
        expert_in = sem("expert_in")
        dn_step = sem("dn_step")
        a_hi = sem("a_hi")
        a_lo = sem("a_lo")
        bsum_done = sem("bsum_done")
        xb_done = sem("xb_done")
        block = ctx.enter_context(nc.Block())
        NEXP = 6
        PIECES = [(wd1[:, :, 0:512], lambda a: w1[:, a, :, 0:512]), (wd1[:, :, 512:1024], lambda a: w1[:, a, :, 512:1024]),
                  (wd2[:, 0:4, :], lambda a: w2[:, a, 0:4, :]), (wd2[:, 4:8, :], lambda a: w2[:, a, 4:8, :]),
                  (wb, lambda a: wbase[:, a, :, :])]

        def carry(engine):
            engine.sem_inc(waited, 1)

        @block.sync
        def _(sp):
            for j in range(4):
                sp.sem_inc(stored[j], 16)
            def load_ln(b, t):
                n = (b + 1) * TT + t
                if not (ahead(b) and t < 2):
                    sp.wait_ge(z_done, n - 1)
                sp.dma_start(xln[:, t % 2, :], x2[bass.ds(n, 1), :, :].rearrange("o p d -> (o p) d")
                             ).then_inc(xln_in[t % 2], 16)

            def load_res(b, t):
                sp.wait_ge(stored[t % 4], 16 + 16 * (b * 2 + t // 4))
                sp.dma_start(xres[:, t % 4, :], x2[bass.ds(b * TT + t, 1), :, :].rearrange("o p d -> (o p) d")
                             ).then_inc(xres_in[t % 4], 16)

            def store(b, t):
                sp.wait_ge(dve_done, base(b, 3) + of(b)[0]["o", t]["dve"])
                sp.dma_start(out[bass.ds(b * TT + t, 1), :, :].rearrange("o p d -> (o p) d"),
                             xres[:, t % 4, :]).then_inc(stored[t % 4], 16)

            sp.dma_start(ident[:, :], ident_in).then_inc(consts, 16)
            sp.dma_start(b1[:, :], bd1).then_inc(consts, 16)
            sp.dma_start(b2[:, :, :], bd2).then_inc(consts, 16)
            sp.dma_start(bb_rep[:, :], b_base.partition_broadcast(P)).then_inc(consts, 16)
            load_ln(-1, 0)
            load_ln(-1, 1)
            for i, (src, _) in enumerate(PIECES):
                if i >= 2:
                    sp.wait_ge(w_lo, i - 1)
                sp.dma_start(stage[i % 2], src).then_inc(w_loaded[i % 2], 16)
            for t in range(2, TT):
                load_ln(-1, t)

            def batch(b, prefetch):
                for t in range(4):
                    load_res(b, t)
                if prefetch:
                    load_ln(b, 0)
                    load_ln(b, 1)
                sp.wait_ge(argmin_step, 4 * (b + 1))
                carry(sp)
                e = sp.value_load(idx[0:1, 0:1], min_val=0, max_val=E - 1)
                sp.dma_start(dn_raw[:, :, :], wa_down[bass.ds(e, 1), :, :, :].rearrange("o p c r -> p (o c) r")
                             ).then_inc(expert_in, 16)
                for half_at in (0, R):
                    sp.dma_start(ba_dn[half_at:half_at + R, :], ba_down[bass.ds(e, 1), :].rearrange("o r -> r o")
                                 ).then_inc(expert_in, 16)
                    sp.dma_start(up_raw[half_at:half_at + R, :], wa_up[bass.ds(e, 1), :, :].rearrange("o r d -> (o r) d")
                                 ).then_inc(expert_in, 16)
                sp.dma_start(ba_up_rep[:, :], ba_up[bass.ds(e, 1), :].rearrange("o d -> (o d)").partition_broadcast(P)
                             ).then_inc(expert_in, 16)
                for t in range(TT):
                    if prefetch and t + 2 < TT:
                        load_ln(b, t + 2)
                    store(b, t)
                    if 1 <= t <= TT - 4:
                        load_res(b, t + 3)
                    
            with sp.Fori(0, B - 1) as b:
                batch(b, True)
            batch(B - 1, False)
            for j in range(4):
                sp.wait_ge(stored[j], 16 + 16 * B * 2)

        @block.gpsimd
        def _(pool):
            nc.gpsimd.memset(half[:, :], -0.5).then_inc(half_set, 1)
            nc.gpsimd.memset(ones[:, :], 1.0).then_inc(ones_set, 1)
            pool.wait_ge(half_set, 1)
            pool.wait_ge(consts, 16 * 4)

            def ln_rstd(b, t):
                n = (b + 1) * TT + t
                pool.wait_ge(mv_done, n + 1)
                carry(pool)
                nc.gpsimd.tensor_scalar(rstd[:, t % 2, 0:1], mv[:, t % 2, 1:2], EPS, None, ALU.add
                                        ).then_inc(var_eps, 1)
                pool.wait_ge(var_eps, n + 1)
                nc.gpsimd.tensor_tensor(rstd[:, t % 2, 1:2], rstd[:, t % 2, 0:1], half[:, :], ALU.pow
                                        ).then_inc(rstd_done, 1)

            def z_whole(b, t):
                pool.wait_ge(dve_done, base(b, 3) + of(b)[0]["z", t]["dve"])
                at = slice(t * P, (t + 1) * P)
                nc.gpsimd.tensor_tensor(zf[:, :, at], zT[:, HI, :, at].bitcast(FP32), zT[:, LO, :, at].bitcast(FP32),
                                        ALU.add).then_inc(zf_done, 1)

            def add_bias(b, t):
                pool.wait_ge(xres_in[t % 4], 16 * (b * 2 + t // 4 + 1))
                nc.gpsimd.tensor_tensor(xres[:, t % 4, :], xres[:, t % 4, :], bsum[:, :], ALU.add).then_inc(xb_done, 1)

            def batch(b, prefetch):
                if prefetch:
                    ln_rstd(b, 0)
                    ln_rstd(b, 1)
                pool.wait_ge(expert_in, 16 * NEXP * (b + 1))
                nc.gpsimd.tensor_tensor(bsum[:, :], bb_rep[:, :], ba_up_rep[:, :], ALU.add).then_inc(bsum_done, 1)
                pool.wait_ge(bsum_done, b + 1)
                for t in range(4):
                    add_bias(b, t)
                for t in range(3, TT):
                    if prefetch:
                        z_whole(b, t - 3)
                        if t > 3 or True:
                            ln_rstd(b, t - 1)
                    if t + 1 < TT:
                        add_bias(b, t + 1)
                if prefetch:
                    z_whole(b, TT - 3)
                    ln_rstd(b, TT - 1)
                    z_whole(b, TT - 2)
                    z_whole(b, TT - 1)

            for t in range(TT):
                ln_rstd(-1, t)
                z_whole(-1, t)
            with pool.Fori(0, B - 1) as b:
                batch(b, True)
            batch(B - 1, False)

        @block.scalar
        def _(act):
            act.sem_inc(sq_done, 1)
            act.wait_ge(consts, 16 * 4)

            def unit(b, *what):
                u = of(b)[0][what]
                act.wait_ge(unit_full, base(b, 1) + u["full"])
                return ring[:, u["bank"], :]

            def z_hi(b, t):
                src = unit(b, "z", t).rearrange("p (c n) -> p c n", n=P)
                nc.scalar.copy(zT[:, HI, :, t * P:(t + 1) * P], src).then_inc(act_done, 1)

            def hidden(b, u):
                e = u % E
                src = unit(b, "h", u)
                act.wait_ge(h_lo, 1 + b * NU + max(u - 1, 0))
                nc.scalar.activation(hf[:, u % 2, :], src, ACT.Relu, bias=b1[:, e:e + 1]).then_inc(act_done, 1)

            def squares(b, u):
                act.wait_ge(dve_done, base(b, 3) + of(b)[0]["rec", u, KC - 1]["dve"])
                nc.scalar.activation(diff[:, u % 2, :, :], diff[:, u % 2, :, :], ACT.Square,
                                     accum_out=sq[:, u // E, u % E:u % E + 1]).then_inc(sq_done, 1)

            def batch(b, prefetch):
                hidden(b, 0)
                hidden(b, 1)
                for u in range(NU):
                    if u + 2 < NU:
                        hidden(b, u + 2)
                    if u >= 1:
                        squares(b, u - 1)
                squares(b, NU - 1)
                act.wait_ge(expert_in, 16 * NEXP * (b + 1))
                for blk in range(NBLK):
                    src = unit(b, "a", blk)
                    nc.scalar.activation(af[:, blk, :], src, ACT.Relu, bias=ba_dn[:, 0:1]).then_inc(act_done, 1)
                if prefetch:
                    for t in range(TT):
                        z_hi(b, t)

            for i, (_, dst) in enumerate(PIECES):
                act.wait_ge(w_loaded[i % 2], 16 * (i // 2 + 1))
                nc.scalar.copy(dst(HI), stage[i % 2]).then_inc(w_hi, 1)
            for t in range(TT):
                z_hi(-1, t)
            with act.Fori(0, B - 1) as b:
                batch(b, True)
            batch(B - 1, False)

        @block.vector
        def _(dve):
            dve.sem_inc(h_lo, 1)
            dve.wait_ge(consts, 16 * 4)

            def unit(b, *what):
                u = of(b)[0][what]
                if what[0] == "z":
                    dve.wait_ge(act_done, base(b, 2) + u["act"])
                else:
                    dve.wait_ge(unit_full, base(b, 1) + u["full"])
                return ring[:, u["bank"], :]

            def ln_stats(b, t):
                n = (b + 1) * TT + t
                dve.wait_ge(xln_in[t % 2], 16 * ((b + 1) * (TT // 2) + t // 2 + 1))
                nc.vector.bn_stats(stats[:, t % 2, :], xln[:, t % 2, :]).then_inc(stats_done, 1)
                dve.wait_ge(stats_done, n + 1)
                carry(dve)
                nc.vector.bn_aggr(mv[:, t % 2, :], stats[:, t % 2, :]).then_inc(mv_done, 1)

            def ln_apply(b, t):
                n = (b + 1) * TT + t
                dve.wait_ge(rstd_done, n + 1)
                nc.vector.tensor_scalar(z[:, t % 2, :], xln[:, t % 2, :], mv[:, t % 2, 0:1], rstd[:, t % 2, 1:2],
                                        ALU.subtract, ALU.mult).then_inc(z_done, 1)

            def z_lo(b, t):
                src = unit(b, "z", t).rearrange("p (c n) -> p c n", n=P)
                at = slice(t * P, (t + 1) * P)
                nc.vector.tensor_tensor(zT[:, LO, :, at], src, zT[:, HI, :, at].bitcast(FP32), ALU.subtract
                                        ).then_inc(dve_done, 1)

            def split_h(b, u):
                dve.wait_ge(act_done, base(b, 2) + of(b)[0]["h", u]["act"])
                nc.vector.tensor_copy(h[:, u % 3, HI, :], hf[:, u % 2, :]).then_inc(h_hi, 1)
                dve.wait_ge(h_hi, b * NU + u + 1)
                nc.vector.tensor_tensor(h[:, u % 3, LO, :], hf[:, u % 2, :], h[:, u % 3, HI, :].bitcast(FP32),
                                        ALU.subtract).then_inc(h_lo, 1)

            def error(b, u):
                blk, e = u // E, u % E
                dve.wait_ge(sq_done, 1 + b * NU + max(u - 1, 0))
                for c in range(KC):
                    nc.vector.scalar_tensor_tensor(diff[:, u % 2, c, :], unit(b, "rec", u, c), b2[:, e, c:c + 1],
                                                   zf[:, c, blk * 512:(blk + 1) * 512], ALU.add, ALU.subtract
                                                   ).then_inc(dve_done, 1)

            def argmin(b):
                src = unit(b, "loss")[0:1, 0:NU]
                nc.vector.tensor_reduce(l8[:, :], src.rearrange("p (k e) -> p e k", e=E), AX.X, ALU.add
                                        ).then_inc(dve_done, 1)
                dve.wait_ge(dve_done, base(b, 3) + of(b)[0]["loss",]["dve"])
                nc.vector.tensor_scalar(neg[:, :], l8[:, :], -1.0 / (S * D), None, ALU.mult).then_inc(argmin_step, 1)
                dve.wait_ge(argmin_step, 4 * b + 1)
                carry(dve)
                nc.vector.max(best[:, :], neg[:, :]).then_inc(argmin_step, 1)
                dve.wait_ge(argmin_step, 4 * b + 2)
                carry(dve)
                nc.vector.max_index(idx[:, :], best[:, :], neg[:, :]).then_inc(argmin_step, 2)

            def split_expert(b):
                dve.wait_ge(expert_in, 16 * NEXP * (b + 1))
                raw = dn_raw[:, :, None, :].broadcast_to((P, KC, 2, R))
                nc.vector.tensor_copy(dn[:, HI, :, :, :], raw).then_inc(dn_step, 1)
                nc.vector.tensor_copy(up[:, HI, :], up_raw[:, :]).then_inc(dn_step, 1)
                dve.wait_ge(dn_step, 4 * b + 2)
                nc.vector.tensor_tensor(dn[:, LO, :, :, :], raw, dn[:, HI, :, :, :].bitcast(FP32), ALU.subtract
                                        ).then_inc(dn_step, 1)
                nc.vector.tensor_tensor(up[:, LO, :], up_raw[:, :], up[:, HI, :].bitcast(FP32), ALU.subtract
                                        ).then_inc(dn_step, 1)

            def split_a(b, blk):
                dve.wait_ge(act_done, base(b, 2) + of(b)[0]["a", blk]["act"])
                nc.vector.tensor_copy(a_hl[:, blk, :], af[:, blk, :]).then_inc(a_hi, 1)
                dve.wait_ge(a_hi, b * NBLK + blk + 1)
                nc.vector.tensor_tensor(a_hl[R:P, blk, :], af[R:P, blk, :], a_hl[R:P, blk, :].bitcast(FP32),
                                        ALU.subtract).then_inc(a_lo, 1)

            def output(b, t):
                src = unit(b, "o", t)
                dve.wait_ge(xb_done, b * TT + t + 1)
                nc.vector.tensor_tensor(xres[:, t % 4, :], src, xres[:, t % 4, :], ALU.add).then_inc(dve_done, 1)

            def batch(b, prefetch):
                split_h(b, 0)
                split_h(b, 1)
                dve.wait_ge(zf_done, (b + 1) * TT)
                for u in range(NU):
                    if u + 2 < NU:
                        split_h(b, u + 2)
                    error(b, u)
                argmin(b)
                if prefetch:
                    ln_stats(b, 0)
                    ln_stats(b, 1)
                    ln_apply(b, 0)
                    ln_apply(b, 1)
                split_expert(b)
                for blk in range(NBLK):
                    split_a(b, blk)
                for t in range(3):
                    output(b, t)
                for t in range(3, TT):
                    output(b, t)
                    if prefetch:
                        z_lo(b, t - 3)
                        ln_stats(b, t - 1)
                        ln_apply(b, t - 1)
                if prefetch:
                    z_lo(b, TT - 3)
                    ln_stats(b, TT - 1)
                    ln_apply(b, TT - 1)
                    z_lo(b, TT - 2)
                    z_lo(b, TT - 1)

            for i, (_, dst) in enumerate(PIECES):
                dve.wait_ge(w_hi, i + 1)
                nc.vector.tensor_tensor(dst(LO), stage[i % 2], dst(HI).bitcast(FP32), ALU.subtract).then_inc(w_lo, 1)
            ln_stats(-1, 0)
            for t in range(TT):
                if t + 1 < TT:
                    ln_stats(-1, t + 1)
                ln_apply(-1, t)
                z_lo(-1, t)
            with dve.Fori(0, B - 1) as b:
                batch(b, True)
            batch(B - 1, False)

        @block.tensor
        def _(pe):
            pe.wait_ge(consts, 16 * 4)
            pe.wait_ge(ones_set, 1)

            def bank(b, *what):
                u = of(b)[0][what]
                if u["freed"]:
                    f = u["freed"]
                    if f["eng"] == "act":
                        pe.wait_ge(act_done, base(b, 2) + f["act"])
                    else:
                        pe.wait_ge(dve_done, base(b, 3) + f["dve"])
                return ring[:, u["bank"], :]

            def product(out, lhs, rhs, stop=True):
                for c in range(KC):
                    for n, (a, r) in enumerate(PARTS):
                        last = nc.tensor.matmul(out, lhs(a, c), rhs(r, c), start=(c == 0 and n == 0),
                                                stop=(stop and c == KC - 1 and n == len(PARTS) - 1))
                return last

            def transpose_z(b, t):
                out = bank(b, "z", t)
                pe.wait_ge(z_done, (b + 1) * TT + t + 1)
                for c in range(KC):
                    last = nc.tensor.transpose(out[:, c * P:(c + 1) * P], z[:, t % 2, c * P:(c + 1) * P], ident[:, :])
                last.then_inc(unit_full, 1)

            def encode(b, u):
                blk, e = u // E, u % E
                product(bank(b, "h", u), lambda a, c: w1[:, a, c, e * H:(e + 1) * H],
                        lambda r, c: zT[:, r, c, blk * 512:(blk + 1) * 512]).then_inc(unit_full, 1)

            def rebuild(b, u):
                e = u % E
                pe.wait_ge(h_lo, 1 + b * NU + u + 1)
                for c in range(KC):
                    out = bank(b, "rec", u, c)
                    for n, (a, r) in enumerate(PARTS):
                        last = nc.tensor.matmul(out, w2[:, a, e, c * P:(c + 1) * P], h[:, u % 3, r, :],
                                                start=(n == 0), stop=(n == len(PARTS) - 1))
                    last.then_inc(unit_full, 1)

            def loss(b):
                out = bank(b, "loss")
                pe.wait_ge(sq_done, 1 + (b + 1) * NU)
                nc.tensor.matmul(out[0:1, 0:NU], ones[:, :], sq[:, :, :].rearrange("p k e -> p (k e)"),
                                 start=True, stop=True).then_inc(unit_full, 1)

            def base_part(b, t):
                out = bank(b, "o", t)
                product(out, lambda a, c: zT[:, a, c, t * P:(t + 1) * P], lambda r, c: wbase[:, r, c, :], stop=False)
                return out

            def adapter_part(b, t, out):
                pe.wait_ge(a_lo, b * NBLK + t // 4 + 1)
                for r in (HI, LO):
                    last = nc.tensor.matmul(out, a_hl[:, t // 4, t % 4 * P:(t % 4 + 1) * P], up[:, r, :],
                                            start=False, stop=(r == LO))
                last.then_inc(unit_full, 1)

            def down(b, blk):
                out = bank(b, "a", blk)
                product(out, lambda a, c: dn[:, a, c, :, :].rearrange("p k r -> p (k r)"),
                        lambda r, c: zT[:, r, c, blk * 512:(blk + 1) * 512]).then_inc(unit_full, 1)

            def batch(b, prefetch):
                pe.wait_ge(act_done, base(b, 2))
                pe.wait_ge(dve_done, base(b, 3))
                encode(b, 0)
                encode(b, 1)
                for u in range(NU):
                    if u + 2 < NU:
                        encode(b, u + 2)
                    rebuild(b, u)
                loss(b)
                open_tiles = [base_part(b, t) for t in range(3)]
                pe.wait_ge(dn_step, 4 * (b + 1))
                down(b, 0)
                down(b, 1)
                for t in range(3):
                    adapter_part(b, t, open_tiles[t])
                for t in range(3, TT):
                    adapter_part(b, t, base_part(b, t))
                    if prefetch:
                        transpose_z(b, t - 3)
                if prefetch:
                    for t in range(TT - 3, TT):
                        transpose_z(b, t)

            for t in range(TT):
                transpose_z(-1, t)
            pe.wait_ge(w_lo, len(PIECES))
            with pe.Fori(0, B - 1) as b:
                batch(b, True)
            batch(B - 1, False)


def decoder_layer(nc, t):
    x1 = nc.dram_tensor("x_after_self_attention", (B * TT, P, D), FP32, kind="Internal").ap()
    x2 = nc.dram_tensor("x_after_cross_attention", (B * TT, P, D), FP32, kind="Internal").ap()
    keys = nc.dram_tensor("cross_keys", (B * STRIDE, P, 2, KEYS), FP32, kind="Internal").ap()
    values = nc.dram_tensor("cross_values", (B * STRIDE, P, KT, P), FP32, kind="Internal").ap()
    self_attention(nc, t["x"], t["s_wqT"], t["s_wkT"], t["s_wvT"], t["s_bq"], t["s_bk"], t["s_bv"],
                   t["ident"], t["causal"], x1)
    cross_keys_values(nc, t["ctxT"], t["c_wk"], t["c_wv"], t["c_bk"], t["c_bv"], t["ident"], keys, values)
    cross_attention(nc, x1, t["c_wq"], t["c_wo"], t["c_bq"], t["c_bo"], t["mask"], t["mask_keys"], keys,
                    values, t["ident"], x2)
    adapters(nc, x2, t["wd1"], t["wd2"], t["w_base"], t["bd1"], t["bd2"], t["b_base"], t["wa_down"], t["ba_down"],
             t["wa_up"], t["ba_up"], t["ident"], t["out"])


def kernel(**inputs):
    import concourse.bacc as bacc
    from concourse.bass_utils import run_bass_kernel_spmd

    a = {name: np.asarray(v) for name, v in inputs.items()}

    def rows(w):
        return w.reshape(KC, P, -1).transpose(1, 0, 2)

    def by_group(w):
        return w.reshape(D, GH, STRIDE, HD).transpose(0, 2, 1, 3).reshape(D, D)

    def group_bias(v):
        return v.reshape(GH, STRIDE, HD).transpose(0, 2, 1).reshape(P, STRIDE)

    arrays = {
        "x": a["x"].reshape(B * TT, P, D),
        "s_wqT": rows(a["L0_attn_Wq"].T), "s_wkT": rows(a["L0_attn_Wk"].T), "s_wvT": rows(a["L0_attn_Wv"].T),
        "s_bq": a["L0_attn_bq"].reshape(KC, P).T, "s_bk": a["L0_attn_bk"].reshape(KC, P).T, "s_bv": a["L0_attn_bv"],
        "ctxT": a["ctx_1024"].transpose(0, 2, 1).reshape(B, KC, P, KEYS, STRIDE).transpose(0, 2, 1, 4, 3).reshape(
            B, P, KC, S),
        "mask": a["mask_BxS2_bf0"].reshape(B, KEYS, STRIDE).transpose(0, 2, 1).reshape(B, S),
        "mask_keys": a["mask_BxS2_bf0"].reshape(B, KT, P, STRIDE).transpose(0, 2, 3, 1),
        "c_wq": rows(by_group(a["L0_xattn_Wq"])), "c_wk": rows(by_group(a["L0_xattn_Wk"])),
        "c_wv": rows(by_group(a["L0_xattn_Wv"])), "c_wo": rows(by_group(a["L0_xattn_Wo"].T).T),
        "c_bq": group_bias(a["L0_xattn_bq"]), "c_bk": group_bias(a["L0_xattn_bk"]),
        "c_bv": group_bias(a["L0_xattn_bv"]), "c_bo": a["L0_xattn_bo"],
        "wd1": rows(a["L0_ffn_Wd1"].transpose(1, 0, 2).reshape(D, E * H)), "wd2": a["L0_ffn_Wd2"].transpose(1, 0, 2),
        "w_base": rows(a["L0_ffn_W_base"]), "b_base": a["L0_ffn_b_base"],
        "bd1": a["L0_ffn_bd1"].T, "bd2": a["L0_ffn_bd2"].reshape(E, KC, P).transpose(2, 0, 1),
        "wa_down": a["L0_ffn_Wa_down"].reshape(E, KC, P, R).transpose(0, 2, 1, 3), "ba_down": a["L0_ffn_ba_down"],
        "wa_up": a["L0_ffn_Wa_up"], "ba_up": a["L0_ffn_ba_up"],
        "ident": np.eye(P, dtype=np.float32),
        "causal": np.triu(np.full((P, P), -1e30, np.float32), 1),
    }
    nc = bacc.Bacc("TRN2", target_bir_lowering=False, num_devices=1)
    arrays = {f"in_{name}": np.ascontiguousarray(v) for name, v in arrays.items()}
    tensors = {name[3:]: nc.dram_tensor(name, v.shape, mybir.dt.from_np(v.dtype), kind="ExternalInput").ap()
               for name, v in arrays.items()}
    tensors["out"] = nc.dram_tensor("out", (B * TT, P, D), FP32, kind="ExternalOutput").ap()
    decoder_layer(nc, tensors)
    got = run_bass_kernel_spmd(nc, [arrays], core_ids=[0])
    return got.results[0]["out"].reshape(B, S, D)
```

```python
import math
from contextlib import ExitStack

import numpy as np
import concourse.bass as bass
from concourse import mybir

FP32 = mybir.dt.float32
FP32R = mybir.dt.float32r
U8 = mybir.dt.uint8
U32 = mybir.dt.uint32
ALU = mybir.AluOpType
ACT = mybir.ActivationFunctionType
AX = mybir.AxisListType

P = 128
B, S, D = 4, 1024, 512
TT = S // P
KC = D // P
NBLK = S // 512
EPS = 1e-5
HI, LO = 0, 1
PARTS = ((HI, HI), (HI, LO), (LO, HI))
STRIDE = 4
HD = 32
GH = P // HD
KEYS = S // STRIDE
KT = KEYS // P
E, H, R = 8, 128, 64


def ahead(b):
    return isinstance(b, int) and b < 0


def self_attention(nc, x, wqT, wkT, wvT, bq, bk, bv, ident_in, causal_in, x1):
    scale = 1.0 / math.sqrt(D)
    RING = 3
    PT_UNITS = [-(-(i + 1) // 4) for i in range(TT)]
    K0, Q0 = 0, KC * NBLK
    V0 = Q0 + KC

    def plan(prefetch):
        at, k = {("q", 0): Q0}, V0 + TT
        for i in range(TT):
            if i == TT // 2 - 1:
                at["q", 1] = k
                k += KC
            at["pt", i] = k
            k += PT_UNITS[i]
            if prefetch and i >= TT // 2:
                at["ln", 2 * (i - TT // 2)] = k
                at["ln", 2 * (i - TT // 2) + 1] = k + 1
                k += 2
        return at, k

    LOOPED, PER = plan(True)
    LAST, _ = plan(False)
    assert PER % RING == TT % RING

    def order(b, *what):
        return (LAST if isinstance(b, int) and b == B - 1 else LOOPED)[what]

    ctx = ExitStack()
    with ctx:
        def sb(name, shape, dt=FP32):
            return ctx.enter_context(nc.sbuf_tensor("a_" + name, shape, dt))

        def sem(name):
            return ctx.enter_context(nc.semaphore("a_" + name))

        with ExitStack() as early:
            first_x = early.enter_context(nc.sbuf_tensor("a_first_x", [P, TT, D], FP32))
            wv_stage = early.enter_context(nc.sbuf_tensor("a_wv_stage", [P, KC, D], FP32))
            wq_stage = early.enter_context(nc.sbuf_tensor("a_wq_stage", [P, KC, D], FP32))
        kT = sb("kT", [P, 2, KC, S], FP32R)
        wq = sb("wq", [P, 2, KC, D], FP32R)
        wk = sb("wk", [P, 2, KC, D], FP32R)
        wv = sb("wv", [P, 2, KC, D], FP32R)
        zT = sb("zT", [P, 2, KC, S], FP32R)
        v = sb("v", [P, 2, TT, D], FP32R)
        qT = sb("qT", [P, 2, KC, 512], FP32R)
        probs = sb("probs", [P, 2, S])
        pT = sb("pT", [P, 2, 2, TT, P], FP32R)
        stage = [probs[:, :, :].rearrange("p a s -> p (a s)").rearrange("p (c n) -> p c n", c=KC),
                 wq_stage[:, :, :], wv_stage[:, :, :]]
        xln = sb("xln", [P, 2, D])
        z = sb("z", [P, 2, D])
        xres = sb("xres", [P, 2, D])
        xout = xres
        bv_rep = sb("bv_rep", [P, D])
        ident = sb("ident", [P, P])
        causal = sb("causal", [P, P])
        bqk = sb("bqk", [P, 2, KC])
        stats = sb("stats", [P, 2, 6])
        mv = sb("mv", [P, 2, 2])
        rstd = sb("rstd", [P, 2, 2])
        half = sb("half", [P, 1])
        mx = sb("mx", [P, TT])
        nbias = sb("nbias", [P, TT])
        rowsum = sb("rowsum", [P, TT])
        rinv = sb("rinv", [P, TT])

        ring = ctx.enter_context(nc.psum_tensor("a_ring", [P, RING, 512], FP32))
        zacc = ctx.enter_context(nc.psum_tensor("a_zacc", [P, 512], FP32))
        scores = ctx.enter_context(nc.psum_tensor("a_scores", [P, 2, S], FP32))

        waited = sem("waited")
        consts = sem("consts")
        w_loaded = [sem(f"w_loaded{w}") for w in range(3)]
        w_hi = sem("w_hi")
        w_lo = sem("w_lo")
        half_set = sem("half_set")
        first_in = [sem(f"first_in{t}") for t in range(2)]
        xln_in = [sem(f"xln_in{j}") for j in range(2)]
        xres_in = [sem(f"xres_in{j}") for j in range(2)]
        stored = [sem(f"stored{j}") for j in range(2)]
        stats_done = sem("stats_done")
        mv_done = sem("mv_done")
        var_eps = sem("var_eps")
        rstd_done = sem("rstd_done")
        z_done = sem("z_done")
        unit_full = sem("unit_full")
        hi_done = sem("hi_done")
        lo_done = sem("lo_done")
        s_full = sem("s_full")
        masked = sem("masked")
        max_done = sem("max_done")
        nbias_done = sem("nbias_done")
        p_done = sem("p_done")
        rinv_done = sem("rinv_done")
        zacc_full = sem("zacc_full")
        combined = sem("combined")
        xb_done = sem("xb_done")
        block = ctx.enter_context(nc.Block())

        def G(b, k):
            return k if ahead(b) else TT + b * PER + k

        def lag(k):
            return RING if k >= RING else k + 1 + (TT - 1 - k) % RING

        def tokens(b, t):
            return first_x[:, t, :] if ahead(b) else xln[:, t % 2, :]

        def carry(engine):
            engine.sem_inc(waited, 1)

        @block.sync
        def _(sp):
            for j in range(2):
                sp.sem_inc(stored[j], 16)
            sp.dma_start(ident[:, :], ident_in).then_inc(consts, 16)
            sp.dma_start(causal[:, :], causal_in).then_inc(consts, 16)
            sp.dma_start(bqk[:, 0, :], bq).then_inc(consts, 16)
            sp.dma_start(bqk[:, 1, :], bk).then_inc(consts, 16)
            sp.dma_start(bv_rep[:, :], bv.partition_broadcast(P)).then_inc(consts, 16)

            def load_ln(b, t):
                sp.wait_ge(z_done, (b + 1) * TT + t - 1)
                sp.dma_start(xln[:, t % 2, :], x[bass.ds((b + 1) * TT + t, 1), :, :].rearrange("o p d -> (o p) d")
                             ).then_inc(xln_in[t % 2], 16)

            for w, src in enumerate((wkT, wqT, wvT)):
                for t in range(4 * w, min(4 * w + 4, TT)):
                    sp.dma_start(tokens(-1, t), x[t]).then_inc(first_in[t // 4], 16)
                sp.dma_start(stage[w], src).then_inc(w_loaded[w], 16)

            def store(b, i):
                sp.wait_ge(combined, 1 + b * TT + i + 1)
                sp.dma_start(x1[bass.ds(b * TT + i, 1), :, :].rearrange("o p d -> (o p) d"),
                             xout[:, i % 2, :]).then_inc(stored[i % 2], 16)

            def batch(b, prefetch):
                for i in range(TT):
                    sp.wait_ge(stored[i % 2], 16 + 16 * (b * (TT // 2) + i // 2))
                    sp.dma_start(xres[:, i % 2, :], x[bass.ds(b * TT + i, 1), :, :].rearrange("o p d -> (o p) d")
                                 ).then_inc(xres_in[i % 2], 16)
                    if prefetch and TT // 2 - 1 <= i < TT - 1:
                        load_ln(b, 2 * (i + 1 - TT // 2))
                        load_ln(b, 2 * (i + 1 - TT // 2) + 1)
                    if i >= 1:
                        store(b, i - 1)
                store(b, TT - 1)

            with sp.Fori(0, B - 1) as b:
                batch(b, True)
            batch(B - 1, False)
            for j in range(2):
                sp.wait_ge(stored[j], 16 + 16 * B * TT // 2)

        @block.gpsimd
        def _(pool):
            nc.gpsimd.memset(half[:, :], -0.5).then_inc(half_set, 1)
            pool.wait_ge(half_set, 1)
            pool.wait_ge(consts, 16 * 5)

            def ln_rstd(b, t):
                n = (b + 1) * TT + t
                pool.wait_ge(mv_done, n + 1)
                carry(pool)
                nc.gpsimd.tensor_scalar(rstd[:, t % 2, 0:1], mv[:, t % 2, 1:2], EPS, None, ALU.add
                                        ).then_inc(var_eps, 1)
                pool.wait_ge(var_eps, n + 1)
                nc.gpsimd.tensor_tensor(rstd[:, t % 2, 1:2], rstd[:, t % 2, 0:1], half[:, :], ALU.pow
                                        ).then_inc(rstd_done, 1)

            def add_bv(b, i):
                pool.wait_ge(xres_in[i % 2], 16 * (b * (TT // 2) + i // 2 + 1))
                nc.gpsimd.tensor_tensor(xres[:, i % 2, :], xres[:, i % 2, :], bv_rep[:, :], ALU.add
                                        ).then_inc(xb_done, 1)

            def batch(b, prefetch):
                for i in range(TT):
                    if prefetch and i >= TT // 2:
                        ln_rstd(b, 2 * (i - TT // 2))
                        ln_rstd(b, 2 * (i - TT // 2) + 1)
                    add_bv(b, i)

            for t in range(TT):
                ln_rstd(-1, t)
            with pool.Fori(0, B - 1) as b:
                batch(b, True)
            batch(B - 1, False)

        @block.scalar
        def _(act):
            act.sem_inc(p_done, 1)
            act.wait_ge(consts, 16 * 5)

            def evacuate(b, k, out, bias=None):
                act.wait_ge(unit_full, G(b, k) + 1)
                src = ring[:, k % RING, :]
                if len(out.shape) == 3:
                    src = src.rearrange("p (c n) -> p c n", n=P)[:, 0:out.shape[1], :]
                if bias is None:
                    nc.scalar.copy(out, src).then_inc(hi_done, 1)
                else:
                    nc.scalar.activation(out, src, ACT.Identity, bias=bias).then_inc(hi_done, 1)

            def split_w(w, dst):
                act.wait_ge(w_loaded[w], 16)
                nc.scalar.copy(dst[:, HI, :, :], stage[w]).then_inc(w_hi, 1)

            def ln_unit(b, t):
                evacuate(b, t if ahead(b) else order(b, "ln", t), zT[:, HI, :, t * P:(t + 1) * P])

            def softmax_exp(b, i):
                n = (i + 1) * P
                act.wait_ge(nbias_done, b * TT + i + 1)
                nc.scalar.activation(probs[:, i % 2, 0:n], scores[:, i % 2, 0:n], ACT.Exp, scale=scale,
                                     bias=nbias[:, i:i + 1], accum_out=rowsum[:, i:i + 1]).then_inc(p_done, 1)

            def pt_units(b, i):
                act.wait_ge(zacc_full, 1 + (b * TT + i - 1 if i >= 2 else b * TT))
                for u in range(PT_UNITS[i]):
                    m = min(4, i + 1 - 4 * u)
                    evacuate(b, order(b, "pt", i) + u, pT[:, i % 2, HI, 4 * u:4 * u + m, :])

            def batch(b, prefetch):
                act.wait_ge(s_full, 1 + b * TT)
                for n in range(NBLK):
                    for c in range(KC):
                        evacuate(b, K0 + n * KC + c, kT[:, HI, c, n * 512:(n + 1) * 512], bqk[:, 1, c:c + 1])
                for c in range(KC):
                    evacuate(b, order(b, "q", 0) + c, qT[:, HI, c, :], bqk[:, 0, c:c + 1])
                act.wait_ge(zacc_full, 1 + b * TT)
                for t in range(TT):
                    evacuate(b, V0 + t, v[:, HI, t, :])
                softmax_exp(b, 0)
                for i in range(TT):
                    if i == TT // 2 - 1:
                        act.wait_ge(s_full, 1 + b * TT + TT // 2)
                        for c in range(KC):
                            evacuate(b, order(b, "q", 1) + c, qT[:, HI, c, :], bqk[:, 0, c:c + 1])
                    pt_units(b, i)
                    if i + 1 < TT:
                        softmax_exp(b, i + 1)
                    if prefetch and i >= TT // 2:
                        ln_unit(b, 2 * (i - TT // 2))
                        ln_unit(b, 2 * (i - TT // 2) + 1)

            for t in range(TT):
                ln_unit(-1, t)
                if t == TT // 2 - 1:
                    split_w(0, wk)
            split_w(1, wq)
            split_w(2, wv)
            with act.Fori(0, B - 1) as b:
                batch(b, True)
            batch(B - 1, False)

        @block.vector
        def _(dve):
            dve.sem_inc(combined, 1)
            dve.wait_ge(consts, 16 * 5)

            def remainder(b, k, out, hi, bias=None):
                dve.wait_ge(hi_done, G(b, k) + 1)
                src = ring[:, k % RING, :]
                if len(out.shape) == 3:
                    src = src.rearrange("p (c n) -> p c n", n=P)[:, 0:out.shape[1], :]
                hi = hi.bitcast(FP32)
                if bias is None:
                    nc.vector.tensor_tensor(out, src, hi, ALU.subtract).then_inc(lo_done, 1)
                else:
                    nc.vector.scalar_tensor_tensor(out, src, bias, hi, ALU.add, ALU.subtract).then_inc(lo_done, 1)

            def split_w(w, dst):
                dve.wait_ge(w_hi, w + 1)
                nc.vector.tensor_tensor(dst[:, LO, :, :], stage[w], dst[:, HI, :, :].bitcast(FP32), ALU.subtract
                                        ).then_inc(w_lo, 1)

            def ln_stats(b, t):
                n = (b + 1) * TT + t
                if ahead(b):
                    dve.wait_ge(first_in[t // 4], 16 * 4)
                else:
                    dve.wait_ge(xln_in[t % 2], 16 * (b * (TT // 2) + t // 2 + 1))
                nc.vector.bn_stats(stats[:, t % 2, :], tokens(b, t)).then_inc(stats_done, 1)
                dve.wait_ge(stats_done, n + 1)
                carry(dve)
                nc.vector.bn_aggr(mv[:, t % 2, :], stats[:, t % 2, :]).then_inc(mv_done, 1)

            def ln_apply(b, t):
                n = (b + 1) * TT + t
                dve.wait_ge(rstd_done, n + 1)
                nc.vector.tensor_scalar(z[:, t % 2, :], tokens(b, t), mv[:, t % 2, 0:1], rstd[:, t % 2, 1:2],
                                        ALU.subtract, ALU.mult).then_inc(z_done, 1)

            def ln_unit(b, t):
                k = t if ahead(b) else order(b, "ln", t)
                at = slice(t * P, (t + 1) * P)
                remainder(b, k, zT[:, LO, :, at], zT[:, HI, :, at])

            def row_max(b, i):
                n = (i + 1) * P
                dve.wait_ge(s_full, 1 + b * TT + i + 1)
                nc.vector.tensor_tensor(scores[:, i % 2, n - P:n], scores[:, i % 2, n - P:n], causal[:, :], ALU.add
                                        ).then_inc(masked, 1)
                dve.wait_ge(masked, b * TT + i + 1)
                nc.vector.tensor_reduce(mx[:, i:i + 1], scores[:, i % 2, 0:n], AX.X, ALU.max).then_inc(max_done, 1)
                dve.wait_ge(max_done, b * TT + i + 1)
                nc.vector.tensor_scalar(nbias[:, i:i + 1], mx[:, i:i + 1], -scale, None, ALU.mult
                                        ).then_inc(nbias_done, 1)

            def pt_units(b, i):
                for u in range(PT_UNITS[i]):
                    m = min(4, i + 1 - 4 * u)
                    at = slice(4 * u, 4 * u + m)
                    remainder(b, order(b, "pt", i) + u, pT[:, i % 2, LO, at, :], pT[:, i % 2, HI, at, :])

            def combine(b, i):
                dve.wait_ge(p_done, 1 + b * TT + i + 1)
                nc.vector.reciprocal(rinv[:, i:i + 1], rowsum[:, i:i + 1]).then_inc(rinv_done, 1)
                dve.wait_ge(rinv_done, b * TT + i + 1)
                dve.wait_ge(xb_done, b * TT + i + 1)
                dve.wait_ge(zacc_full, 1 + b * TT + i + 1)
                nc.vector.scalar_tensor_tensor(xout[:, i % 2, :], zacc[:, :], rinv[:, i:i + 1], xres[:, i % 2, :],
                                               ALU.mult, ALU.add).then_inc(combined, 1)

            def batch(b, prefetch):
                for n in range(NBLK):
                    at = slice(n * 512, (n + 1) * 512)
                    for c in range(KC):
                        remainder(b, K0 + n * KC + c, kT[:, LO, c, at], kT[:, HI, c, at], bqk[:, 1, c:c + 1])
                for c in range(KC):
                    remainder(b, order(b, "q", 0) + c, qT[:, LO, c, :], qT[:, HI, c, :], bqk[:, 0, c:c + 1])
                for t in range(TT):
                    remainder(b, V0 + t, v[:, LO, t, :], v[:, HI, t, :])
                row_max(b, 0)
                for i in range(TT):
                    if i == TT // 2 - 1:
                        for c in range(KC):
                            remainder(b, order(b, "q", 1) + c, qT[:, LO, c, :], qT[:, HI, c, :], bqk[:, 0, c:c + 1])
                    if i + 1 < TT:
                        row_max(b, i + 1)
                    pt_units(b, i)
                    if prefetch and i >= TT // 2:
                        t = 2 * (i - TT // 2)
                        ln_stats(b, t)
                        ln_stats(b, t + 1)
                        ln_apply(b, t)
                        ln_apply(b, t + 1)
                    if i >= 1:
                        combine(b, i - 1)
                    if prefetch and i >= TT // 2:
                        ln_unit(b, t)
                        ln_unit(b, t + 1)
                combine(b, TT - 1)

            ln_stats(-1, 0)
            ln_stats(-1, 1)
            ln_apply(-1, 0)
            for t in range(TT):
                if t + 2 < TT:
                    ln_stats(-1, t + 2)
                if t + 1 < TT:
                    ln_apply(-1, t + 1)
                ln_unit(-1, t)
                if t == TT // 2 - 1:
                    split_w(0, wk)
            split_w(1, wq)
            split_w(2, wv)
            dve.wait_ge(w_lo, 3)
            with dve.Fori(0, B - 1) as b:
                batch(b, True)
            batch(B - 1, False)

        @block.tensor
        def _(pe):
            pe.sem_inc(zacc_full, 1)
            pe.sem_inc(s_full, 1)
            pe.wait_ge(consts, 16 * 5)

            def bank(b, k):
                if not (ahead(b) and k < RING):
                    pe.wait_ge(lo_done, G(b, k) - lag(k) + 1)
                return ring[:, k % RING, :]

            def product(out, lhs, rhs):
                for c in range(KC):
                    for n, (a, r) in enumerate(PARTS):
                        last = nc.tensor.matmul(out, lhs(a, c), rhs(r, c), start=(c == 0 and n == 0),
                                                stop=(c == KC - 1 and n == len(PARTS) - 1))
                return last

            def transpose_z(b, t):
                out = bank(b, t if ahead(b) else order(b, "ln", t))
                pe.wait_ge(z_done, (b + 1) * TT + t + 1)
                for c in range(KC):
                    last = nc.tensor.transpose(out[:, c * P:(c + 1) * P], z[:, t % 2, c * P:(c + 1) * P], ident[:, :])
                last.then_inc(unit_full, 1)

            def score(b, i):
                if i == 0:
                    pe.wait_ge(lo_done, G(b, order(b, "q", 0) + KC - 1) + 1)
                if i == TT // 2:
                    pe.wait_ge(lo_done, G(b, order(b, "q", 1) + KC - 1) + 1)
                pe.wait_ge(p_done, 1 + (b * TT + i - 1 if i >= 2 else b * TT))
                q = slice((i % 4) * P, (i % 4 + 1) * P)
                for at in range(0, (i + 1) * P, 512):
                    n = at + min(512, max(256, (i + 1) * P - at))
                    last = product(scores[:, i % 2, at:n], lambda a, c: qT[:, a, c, q],
                                   lambda r, c: kT[:, r, c, at:n])
                last.then_inc(s_full, 1)

            def transpose_p(b, i):
                pe.wait_ge(p_done, 1 + b * TT + i + 1)
                for u in range(PT_UNITS[i]):
                    out = bank(b, order(b, "pt", i) + u)
                    for j in range(4 * u, min(4 * u + 4, i + 1)):
                        last = nc.tensor.transpose(out[:, (j % 4) * P:(j % 4 + 1) * P],
                                                   probs[:, i % 2, j * P:(j + 1) * P], ident[:, :])
                    last.then_inc(unit_full, 1)

            def times_v(b, i):
                pe.wait_ge(lo_done, G(b, order(b, "pt", i) + PT_UNITS[i]))
                pe.wait_ge(combined, 1 + b * TT + i)
                for j in range(i + 1):
                    for n, (a, r) in enumerate(PARTS):
                        last = nc.tensor.matmul(zacc[:, :], pT[:, i % 2, a, j, :], v[:, r, j, :],
                                                start=(j == 0 and n == 0), stop=(j == i and n == len(PARTS) - 1))
                last.then_inc(zacc_full, 1)

            def q_units(b, blk):
                for c in range(KC):
                    out = bank(b, order(b, "q", blk) + c)
                    product(out, lambda a, d: wq[:, a, d, c * P:(c + 1) * P],
                            lambda r, d: zT[:, r, d, blk * 512:(blk + 1) * 512]).then_inc(unit_full, 1)

            def batch(b, prefetch):
                pe.wait_ge(w_lo, 1)
                for n in range(NBLK):
                    pe.wait_ge(lo_done, G(b, 0) - TT // 2 * (1 - n))
                    for c in range(KC):
                        out = bank(b, K0 + n * KC + c)
                        product(out, lambda a, d: wk[:, a, d, c * P:(c + 1) * P],
                                lambda r, d: zT[:, r, d, n * 512:(n + 1) * 512]).then_inc(unit_full, 1)
                pe.wait_ge(w_lo, 2)
                q_units(b, 0)
                pe.wait_ge(w_lo, 3)
                for t in range(TT):
                    out = bank(b, V0 + t)
                    product(out, lambda a, d: zT[:, a, d, t * P:(t + 1) * P],
                            lambda r, d: wv[:, r, d, :]).then_inc(unit_full, 1)
                score(b, 0)
                for i in range(TT):
                    if i == TT // 2 - 1:
                        q_units(b, 1)
                    elif i + 1 < TT:
                        score(b, i + 1)
                    transpose_p(b, i)
                    if i >= 1:
                        times_v(b, i - 1)
                    if i == TT // 2 - 1:
                        score(b, i + 1)
                    if prefetch and i >= TT // 2:
                        transpose_z(b, 2 * (i - TT // 2))
                        transpose_z(b, 2 * (i - TT // 2) + 1)
                times_v(b, TT - 1)

            for t in range(TT):
                transpose_z(-1, t)
            with pe.Fori(0, B - 1) as b:
                batch(b, True)
            batch(B - 1, False)


def cross_keys_values(nc, ctxT, wkT, wvT, bk, bv, ident_in, k_out, v_out):
    R = STRIDE
    AHEAD = 2
    ctx = ExitStack()
    with ctx:
        def sb(name, shape, dt=FP32):
            return ctx.enter_context(nc.sbuf_tensor("kv_" + name, shape, dt))

        def sem(name):
            return ctx.enter_context(nc.semaphore("kv_" + name))

        wk = sb("wk", [P, 2, KC, D], FP32R)
        wv = sb("wv", [P, 2, KC, D], FP32R)
        w_stage = sb("w_stage", [P, 2, KC, D])
        raw = sb("raw", [P, R, KC, KEYS])
        c_hl = sb("c_hl", [P, R, 2, KC, KEYS], FP32R)
        k_hl = sb("k_hl", [P, 2, 2, KEYS], FP32R)
        vT = sb("vT", [P, 2, KEYS])
        v_sb = sb("v_sb", [P, 2, KT, P])
        bkv = sb("bkv", [P, 2, STRIDE])
        ident = sb("ident", [P, P])
        k_ps = [ctx.enter_context(nc.psum_tensor(f"kv_k{i}", [P, KEYS], FP32)) for i in range(2)]
        vT_ps = [ctx.enter_context(nc.psum_tensor(f"kv_vT{i}", [P, KEYS], FP32)) for i in range(2)]
        v_ps = [ctx.enter_context(nc.psum_tensor(f"kv_v{i}", [P, KT * P], FP32)) for i in range(2)]

        consts = sem("consts")
        w_loaded = [sem(f"w_loaded{w}") for w in range(2)]
        w_hi = sem("w_hi")
        w_lo = sem("w_lo")
        raw_in = [sem(f"raw_in{r}") for r in range(R)]
        c_hi = sem("c_hi")
        c_lo = sem("c_lo")
        k_full = sem("k_full")
        k_lo = sem("k_lo")
        vT_full = sem("vT_full")
        vT_done = sem("vT_done")
        v_full = sem("v_full")
        v_done = sem("v_done")
        k_hi = sem("k_hi")
        k_stored = [sem(f"k_stored{i}") for i in range(2)]
        v_stored = [sem(f"v_stored{i}") for i in range(2)]
        block = ctx.enter_context(nc.Block())

        def units(b, prefetch):
            return [(r, b * R + r, prefetch or r + AHEAD < R) for r in range(R)]

        @block.sync
        def _(sp):
            for j in range(2):
                sp.sem_inc(k_stored[j], 16)
                sp.sem_inc(v_stored[j], 16)

            def load(b, r):
                sp.dma_start(raw[:, r, :, :], ctxT[bass.ds(b, 1), :, :, r * KEYS:(r + 1) * KEYS].rearrange(
                    "o p c s -> p (o c) s")).then_inc(raw_in[r], 16)

            load(0, 0)
            sp.dma_start(w_stage[:, 0, :, :], wvT).then_inc(w_loaded[0], 16)
            load(0, 1)
            sp.dma_start(w_stage[:, 1, :, :], wkT).then_inc(w_loaded[1], 16)
            sp.dma_start(ident[:, :], ident_in).then_inc(consts, 16)
            sp.dma_start(bkv[:, 0, :], bk).then_inc(consts, 16)
            sp.dma_start(bkv[:, 1, :], bv).then_inc(consts, 16)
            load(0, 2)
            load(0, 3)

            def batch(b, prefetch):
                for r, n, _ in units(b, prefetch):
                    if prefetch:
                        sp.wait_ge(c_lo, n + 1)
                        load(b + 1, r)
                    sp.wait_ge(k_lo, 2 + n + 1)
                    sp.dma_start(k_out[bass.ds(n, 1), :, :, :].rearrange("o p h s -> p (o h) s"),
                                 k_hl[:, r % 2, :, :].bitcast(FP32)).then_inc(k_stored[r % 2], 16)
                    sp.wait_ge(v_done, 2 + n + 1)
                    sp.dma_start(v_out[bass.ds(n, 1), :, :, :].rearrange("o p c d -> p (o c) d"),
                                 v_sb[:, r % 2, :, :]).then_inc(v_stored[r % 2], 16)

            with sp.Fori(0, B - 1) as b:
                batch(b, True)
            batch(B - 1, False)
            for i in range(2):
                sp.wait_ge(k_stored[i], 16 + 16 * B * R // 2)
                sp.wait_ge(v_stored[i], 16 + 16 * B * R // 2)

        @block.scalar
        def _(act):
            act.sem_inc(vT_done, 2)

            def split(b, r):
                act.wait_ge(raw_in[r % R], 16 * (b + r // R + 1))
                if not (isinstance(b, int) and b * R + r < R):
                    act.wait_ge(k_full, 2 + b * R + r - R + 1)
                nc.scalar.copy(c_hl[:, r % R, HI, :, :], raw[:, r % R, :, :]).then_inc(c_hi, 1)

            def split_w(w, dst):
                act.wait_ge(w_loaded[w], 16)
                nc.scalar.copy(dst[:, HI, :, :], w_stage[:, w, :, :]).then_inc(w_hi, 1)

            def batch(b, prefetch):
                for r, n, more in units(b, prefetch):
                    if more:
                        split(b, r + AHEAD)
                    act.wait_ge(vT_full, 2 + n + 1)
                    act.wait_ge(v_full, n + 1)
                    nc.scalar.activation(vT[:, r % 2, :], vT_ps[r % 2][:, :], ACT.Identity,
                                         bias=bkv[:, 1, r:r + 1]).then_inc(vT_done, 1)
                    act.wait_ge(k_full, 2 + n + 1)
                    act.wait_ge(k_stored[r % 2], 16 + 16 * (b * (R // 2) + r // 2))
                    nc.scalar.activation(k_hl[:, r % 2, HI, :], k_ps[r % 2][:, :], ACT.Identity,
                                         bias=bkv[:, 0, r:r + 1]).then_inc(k_hi, 1)

            split(0, 0)
            split_w(0, wv)
            split(0, 1)
            split_w(1, wk)
            act.wait_ge(consts, 48)
            with act.Fori(0, B - 1) as b:
                batch(b, True)
            batch(B - 1, False)

        @block.vector
        def _(dve):
            dve.sem_inc(k_lo, 2)
            dve.sem_inc(v_done, 2)

            def split(b, r):
                dve.wait_ge(c_hi, b * R + r + 1)
                nc.vector.tensor_tensor(c_hl[:, r % R, LO, :, :], raw[:, r % R, :, :],
                                        c_hl[:, r % R, HI, :, :].bitcast(FP32), ALU.subtract).then_inc(c_lo, 1)

            def split_w(w, dst):
                dve.wait_ge(w_hi, w + 1)
                nc.vector.tensor_tensor(dst[:, LO, :, :], w_stage[:, w, :, :], dst[:, HI, :, :].bitcast(FP32),
                                        ALU.subtract).then_inc(w_lo, 1)

            def batch(b, prefetch):
                for r, n, more in units(b, prefetch):
                    if more:
                        split(b, r + AHEAD)
                    dve.wait_ge(k_hi, n + 1)
                    nc.vector.scalar_tensor_tensor(k_hl[:, r % 2, LO, :], k_ps[r % 2][:, :], bkv[:, 0, r:r + 1],
                                                   k_hl[:, r % 2, HI, :].bitcast(FP32), ALU.add, ALU.subtract
                                                   ).then_inc(k_lo, 1)
                    dve.wait_ge(v_full, 2 + n + 1)
                    dve.wait_ge(v_stored[r % 2], 16 + 16 * (b * (R // 2) + r // 2))
                    nc.vector.tensor_copy(v_sb[:, r % 2, :, :], v_ps[r % 2][:, :].rearrange("p (c d) -> p c d", d=P)
                                          ).then_inc(v_done, 1)

            split(0, 0)
            split_w(0, wv)
            split(0, 1)
            split_w(1, wk)
            dve.wait_ge(consts, 48)
            with dve.Fori(0, B - 1) as b:
                batch(b, True)
            batch(B - 1, False)

        @block.tensor
        def _(pe):
            pe.sem_inc(k_full, 2)
            pe.sem_inc(vT_full, 2)
            pe.sem_inc(v_full, 2)
            pe.wait_ge(consts, 48)

            def project(out, w, r):
                for c in range(KC):
                    for n, (a, h) in enumerate(PARTS):
                        last = nc.tensor.matmul(out, w[:, a, c, r * P:(r + 1) * P], c_hl[:, r, h, c, :],
                                                start=(c == 0 and n == 0), stop=(c == KC - 1 and n == 2))
                return last

            with pe.Fori(0, B) as b:
                for r in range(R):
                    n = b * R + r
                    pe.wait_ge(c_lo, n + 1)
                    pe.wait_ge(w_lo, 1)
                    pe.wait_ge(vT_done, n + 1)
                    project(vT_ps[r % 2][:, :], wv, r).then_inc(vT_full, 1)
                    pe.wait_ge(w_lo, 2)
                    pe.wait_ge(k_lo, n + 1)
                    project(k_ps[r % 2][:, :], wk, r).then_inc(k_full, 1)
                    pe.wait_ge(vT_done, 2 + n + 1)
                    pe.wait_ge(v_done, n + 1)
                    for c in range(KT):
                        last = nc.tensor.transpose(v_ps[r % 2][:, c * P:(c + 1) * P],
                                                   vT[:, r % 2, c * P:(c + 1) * P], ident[:, :])
                    last.then_inc(v_full, 1)


def cross_attention(nc, x1, wqT, woT, bq, bo, mask, mask_keys, k_in, v_in, ident_in, x2):
    scale = float(HD) ** -0.5
    QT = 4
    NG = NBLK * STRIDE
    NH = NG * GH
    RING = 4
    MBUF = 4
    STACKED = 16 * 4
    SPH = QT // 2
    JR, JQ, JC = 0, 1, 2
    OUT_TILES = {(1, j): (j,) for j in range(GH)}
    LN_TILES = ((), (0, 1), (2, 3), ())

    def plan(prefetch, first=False):
        units = [("z", 2, t) for t in range(QT)] + [("q", NG), ("q", NG + 1)] if first else []
        for n in range(NG if first else 2, NG + 2 if prefetch else NG):
            for j in range(GH):
                if n % 4 == 1 and prefetch:
                    units += [("z", n // 4 + 1, t) for t in LN_TILES[j - 1]]
                if j == JQ and (n + 2 < NG or prefetch):
                    units += [("q", n + 2)]
                if j == JC and not (first and n == NG):
                    units += [("c", n - 1)]
                if not first:
                    units += [("o", n // 4 - 1, t) for t in OUT_TILES.get((n % 4, j), ())]
                if j == JR and not (first and n == NG):
                    units += [("r", n - 1)]
        if not prefetch:
            units += [("r", NG - 1), ("c", NG - 1)] + [("o", 1, t) for t in range(QT)]
        table, acts = {}, 0
        for i, what in enumerate(units):
            acts += what[0] in "zq"
            table[what] = dict(full=i + 1, act=acts, bank=(i - (len(units) if first else 0)) % RING)
        assert first or not prefetch or len(units) % RING == 0
        return table, len(units), acts

    FIRST, LOOPED, LAST = plan(True, True), plan(True), plan(False)

    def of(b):
        return FIRST if ahead(b) else LAST if isinstance(b, int) and b == B - 1 else LOOPED

    def base(b, which):
        return 0 if ahead(b) else FIRST[which] + b * LOOPED[which]

    def behind(b, n):
        return not (ahead(b) and n == NG)

    def ctx_groups(b, n, j):
        if ahead(b) and n == NG or n % 4 == 1:
            return []
        return [n - 2] if n % 4 == 2 and j == 0 else [n - 1] if j == GH - 1 else []

    def out_tiles(b, n, j):
        return [] if ahead(b) else [(n // 4 - 1, t) for t in OUT_TILES.get((n % 4, j), ())]

    def steps(b, prefetch):
        return [(n, j, n * GH + j) for n in range(NG if ahead(b) else 2, NG + 2 if prefetch else NG)
                for j in range(GH)]

    ctx = ExitStack()
    with ctx:
        def sb(name, shape, dt=FP32):
            return ctx.enter_context(nc.sbuf_tensor("x_" + name, shape, dt))

        def sem(name):
            return ctx.enter_context(nc.semaphore("x_" + name))

        wq = sb("wq", [P, 2, KC, D], FP32R)
        wo = sb("wo", [P, 2, KC, D], FP32R)
        k_st = sb("k_st", [P, STRIDE, GH, KEYS], FP32R)
        v_sb = sb("v_sb", [P, STRIDE, KT, P])
        q_hl = sb("q_hl", [P, 2, 2, 512], FP32R)
        q_st = sb("q_st", [P, 2, GH, 512], FP32R)
        zT = sb("zT", [P, 2, KC, 512], FP32R)
        masked = sb("masked", [P, 2, QT, KEYS])
        diag = sb("diag", [P, 2, QT, P], FP32R)
        neg_ones = sb("neg_ones", [P, P], FP32R)
        ones = sb("ones", [P, HD])
        pT = sb("pT", [P, 2, GH, KT, 512])
        ctxn = sb("ctxn", [P, 2, 512])
        r_sb = sb("r_sb", [P, 2, 512])
        cT = sb("cT", [P, 2, STRIDE, 512], FP32R)
        xln = sb("xln", [P, QT, D])
        z = sb("z", [P, 2, D])
        xres = sb("xres", [P, QT, D])
        bo_rep = sb("bo_rep", [P, D])
        ident = sb("ident", [P, P])
        bq_sb = sb("bq_sb", [P, STRIDE])
        mask_u8 = sb("mask_u8", [P, STRIDE, KEYS], U8)
        mask_add = sb("mask_add", [P, STRIDE, KEYS])
        mask_keys_u8 = sb("mask_keys_u8", [P, STRIDE, KT], U8)
        mask_bias = sb("mask_bias", [P, STRIDE, KT])
        stats = sb("stats", [P, 2, 6])
        mv = sb("mv", [P, 2, 2])
        rstd = sb("rstd", [P, 2, 2])
        half = sb("half", [P, 1])
        mx = sb("mx", [P, MBUF, QT])
        w_stage = pT[:, 0, :, :, :].rearrange("p j c q -> p (j c) q")

        ring = ctx.enter_context(nc.psum_tensor("x_ring", [P, RING, 512], FP32))
        sps = ctx.enter_context(nc.psum_tensor("x_sps", [P, SPH, 512], FP32))
        stps = ctx.enter_context(nc.psum_tensor("x_stps", [P, KT, 512], FP32))

        waited = sem("waited")
        consts = sem("consts")
        wq_loaded = sem("wq_loaded")
        wo_loaded = sem("wo_loaded")
        w_hi = sem("w_hi")
        w_lo = sem("w_lo")
        half_set = sem("half_set")
        xln_in = [sem(f"xln_in{j}") for j in range(QT)]
        xres_in = [sem(f"xres_in{j}") for j in range(QT)]
        stored = [sem(f"stored{j}") for j in range(QT)]
        k_loaded = [sem(f"k_loaded{r}") for r in range(STRIDE)]
        v_loaded = [sem(f"v_loaded{r}") for r in range(STRIDE)]
        mask_in = sem("mask_in")
        mask_done = sem("mask_done")
        q_stacked = [[sem(f"q_stacked{p}{j}") for j in range(GH)] for p in range(2)]
        stats_done = sem("stats_done")
        mv_done = sem("mv_done")
        var_eps = sem("var_eps")
        rstd_done = sem("rstd_done")
        z_done = sem("z_done")
        unit_full = sem("unit_full")
        act_done = sem("act_done")
        s_full = sem("s_full")
        max_done = sem("max_done")
        diag_done = sem("diag_done")
        st_full = sem("st_full")
        p_done = sem("p_done")
        dve_done = sem("dve_done")
        half_inverted = sem("half_inverted")
        ones_set = sem("ones_set")
        cT_hi = sem("cT_hi")
        cT_lo = sem("cT_lo")
        xb_done = sem("xb_done")
        block = ctx.enter_context(nc.Block())

        def carry(engine):
            engine.sem_inc(waited, 1)

        @block.sync
        def _(sp):
            for j in range(4):
                sp.sem_inc(stored[j], 16)
            def tile_of(b, blk, t):
                return b * TT + blk * QT + t

            def load_ln(b, blk, t):
                n = tile_of(b, blk, t)
                if not (isinstance(n, int) and n < QT):
                    sp.wait_ge(z_done, n - QT + 1)
                sp.dma_start(xln[:, t, :], x1[bass.ds(n, 1), :, :].rearrange("o p d -> (o p) d")
                             ).then_inc(xln_in[t], 16)

            def load_res(b, blk):
                for t in range(QT):
                    sp.wait_ge(stored[t], 16 + 16 * (b * NBLK + blk))
                    sp.dma_start(xres[:, t, :], x1[bass.ds(tile_of(b, blk, t), 1), :, :].rearrange("o p d -> (o p) d")
                                 ).then_inc(xres_in[t], 16)

            def store(b, blk):
                for t in range(QT):
                    sp.wait_ge(dve_done, base(b, 1) + of(b)[0]["o", blk, t]["full"])
                    sp.dma_start(x2[bass.ds(tile_of(b, blk, t), 1), :, :].rearrange("o p d -> (o p) d"),
                                 xres[:, t, :]).then_inc(stored[t], 16)

            def load_k(b, r):
                if not (isinstance(b, int) and b == 0):
                    sp.wait_ge(st_full, ((b - 1) * NH + (STRIDE + r + 1) * GH) * KT)
                for part in range(4):
                    sp.dma_start(k_st[part * HD:(part + 1) * HD, r, :, :].bitcast(FP32),
                                 k_in[bass.ds(b * STRIDE + r, 1), :, part % 2, :].rearrange(
                                     "o (j d) s -> d (o j) s", d=HD)).then_inc(k_loaded[r], 16)

            def load_v(b, r):
                if not (isinstance(b, int) and b == 0):
                    sp.wait_ge(unit_full, base(b - 1, 1) + LOOPED[0]["c", STRIDE + r]["full"])
                sp.dma_start(v_sb[:, r, :, :], v_in[bass.ds(b * STRIDE + r, 1), :, :, :].rearrange(
                    "o p c d -> p (o c) d")).then_inc(v_loaded[r], 16)

            def load_mask(b):
                sp.dma_start(mask_u8[:, :, :].rearrange("p r s -> p (r s)"), mask[bass.ds(b, 1), :].rearrange(
                    "o s -> (o s)").partition_broadcast(P)).then_inc(mask_in, 16)
                sp.dma_start(mask_keys_u8[:, :, :], mask_keys[bass.ds(b, 1), :, :, :].rearrange(
                    "o p r c -> (o p) r c")).then_inc(mask_in, 16)

            def stack_q(b, n):
                sp.wait_ge(dve_done, base(b, 1) + of(b)[0]["q", n]["full"])
                for j in range(GH):
                    if not ahead(b) or n >= NG + 2:
                        sp.wait_ge(st_full, (b * NH + (n - 2) * GH + j + 1) * KT)
                    for part in range(4):
                        sp.dma_start(q_st[part * HD:(part + 1) * HD, n % 2, j, :].bitcast(FP32),
                                     q_hl[j * HD:(j + 1) * HD, n % 2, part // 2, :].bitcast(FP32)
                                     ).then_inc(q_stacked[n % 2][j], 16)

            for t in range(QT):
                load_ln(-1, 2, t)
            sp.dma_start(ident[:, :], ident_in).then_inc(consts, 16)
            sp.dma_start(w_stage[:, 0:KC, :], wqT).then_inc(wq_loaded, 16)
            sp.dma_start(bq_sb[:, :], bq).then_inc(consts, 16)
            sp.dma_start(bo_rep[:, :], bo.partition_broadcast(P)).then_inc(consts, 16)
            sp.dma_start(w_stage[:, KC:2 * KC, :], woT).then_inc(wo_loaded, 16)
            load_mask(0)
            for r in range(STRIDE):
                load_k(0, r)
                load_v(0, r)
            for t in range(QT):
                load_ln(-1, 3, t)
            stack_q(-1, NG)
            stack_q(-1, NG + 1)
            stack_q(-1, NG + 2)
            stack_q(-1, NG + 3)

            def batch(b, prefetch):
                stack_q(b, 4)
                load_res(b, 0)
                stack_q(b, 5)
                if prefetch:
                    sp.wait_ge(mask_done, (b + 1) * STRIDE * 2)
                    carry(sp)
                    load_mask(b + 1)
                stack_q(b, 6)
                if prefetch:
                    load_k(b + 1, 0)
                    for t in range(QT):
                        load_ln(b, 2, t)
                stack_q(b, 7)
                store(b, 0)
                if prefetch:
                    load_k(b + 1, 1)
                    load_v(b + 1, 0)
                    stack_q(b, 8)
                    load_k(b + 1, 2)
                    load_v(b + 1, 1)
                load_res(b, 1)
                if prefetch:
                    stack_q(b, 9)
                    load_k(b + 1, 3)
                    load_v(b + 1, 2)
                    for t in range(QT):
                        load_ln(b, 3, t)
                    stack_q(b, 10)
                    load_v(b + 1, 3)
                    stack_q(b, 11)
                store(b, 1)

            with sp.Fori(0, B - 1) as b:
                batch(b, True)
            batch(B - 1, False)
            for j in range(QT):
                sp.wait_ge(stored[j], 16 + 16 * B * NBLK)

        def ln_tiles(b, n, j, late=0):
            blk, j = n // 4 + 1, j - late
            if n % 4 != 1 or not 0 <= j < GH:
                return []
            return [(blk, t, b * TT + blk * QT + t) for t in LN_TILES[j]]

        @block.gpsimd
        def _(pool):
            pool.sem_inc(cT_lo, 1)
            nc.gpsimd.memset(half[:, :], -0.5).then_inc(half_set, 1)
            nc.gpsimd.memset(ones[:, :], 1.0).then_inc(ones_set, 1)
            pool.wait_ge(half_set, 1)

            def ln_rstd(t, n):
                pool.wait_ge(mv_done, n + 1)
                carry(pool)
                nc.gpsimd.tensor_scalar(rstd[:, t % 2, 0:1], mv[:, t % 2, 1:2], EPS, None, ALU.add
                                        ).then_inc(var_eps, 1)
                pool.wait_ge(var_eps, n + 1)
                nc.gpsimd.tensor_tensor(rstd[:, t % 2, 1:2], rstd[:, t % 2, 0:1], half[:, :], ALU.pow
                                        ).then_inc(rstd_done, 1)

            def add_bo(b, blk):
                for t in range(QT):
                    pool.wait_ge(xres_in[t], 16 * (b * NBLK + blk + 1))
                    nc.gpsimd.tensor_tensor(xres[:, t, :], xres[:, t, :], bo_rep[:, :], ALU.add).then_inc(xb_done, 1)

            def ctx_lo(b, n):
                g = b * NG + n
                pool.wait_ge(cT_hi, g + 1)
                nc.gpsimd.tensor_tensor(cT[:, LO, n % 4, :], ctxn[:, n % 2, :], cT[:, HI, n % 4, :].bitcast(FP32),
                                        ALU.subtract).then_inc(cT_lo, 1)

            def diagonal(b, k):
                pool.wait_ge(max_done, (b * NH + k + 1) * QT)
                if not (ahead(b) and k < NH + 2):
                    pool.wait_ge(st_full, (b * NH + k - 1) * KT)
                nc.gpsimd.tensor_tensor(diag[:, k % 2, :, :], ident[:, None, :].broadcast_to((P, QT, P)),
                                        mx[:, k % MBUF, :][:, :, None].broadcast_to((P, QT, P)), ALU.mult
                                        ).then_inc(diag_done, 1)

            def batch(b, prefetch):
                for n, j, k in steps(b, prefetch):
                    if k + 2 < NH or prefetch:
                        diagonal(b, k + 2)
                    if prefetch:
                        for blk, t, m in ln_tiles(b, n, j):
                            ln_rstd(t, m)
                    for g in ctx_groups(b, n, j):
                        ctx_lo(b, g)
                    if j == GH - 1 and n % 4 == 3 and not ahead(b):
                        add_bo(b, n // 4)
                if not prefetch:
                    ctx_lo(b, NG - 1)

            for t in range(QT):
                ln_rstd(t, t)
            pool.wait_ge(consts, 16 * 3)
            diagonal(-1, NH)
            diagonal(-1, NH + 1)
            batch(-1, True)
            with pool.Fori(0, B - 1) as b:
                batch(b, True)
            batch(B - 1, False)

        @block.scalar
        def _(act):

            def unit(b, *what):
                u = of(b)[0][what]
                act.wait_ge(unit_full, base(b, 1) + u["full"])
                return ring[:, u["bank"], :]

            def z_hi(b, blk, t):
                src = unit(b, "z", blk, t).rearrange("p (c n) -> p c n", n=P)
                nc.scalar.copy(zT[:, HI, :, t * P:(t + 1) * P], src).then_inc(act_done, 1)

            def q_hi(b, n):
                src = unit(b, "q", n)
                if not (ahead(b) and n < NG + 2):
                    for j in range(GH):
                        act.wait_ge(q_stacked[n % 2][j], STACKED * (b * (NG // 2) + n // 2))
                nc.scalar.activation(q_hl[:, n % 2, HI, :], src, ACT.Identity,
                                     bias=bq_sb[:, n % 4:n % 4 + 1]).then_inc(act_done, 1)

            def exps(b, k):
                n, j = k // GH, k % GH
                for c in range(KT):
                    act.wait_ge(st_full, (b * NH + k) * KT + c + 1)
                    nc.scalar.activation(pT[:, n % 2, j, c, :], stps[:, c, :], ACT.Exp, scale=scale,
                                         bias=mask_bias[:, n % 4, c:c + 1]).then_inc(p_done, 1)

            def ctx_hi(b, n):
                act.wait_ge(dve_done, base(b, 1) + (of(b)[0]["c", n]["full"] if n > 0 else 0))
                nc.scalar.copy(cT[:, HI, n % 4, :], ctxn[:, n % 2, :]).then_inc(cT_hi, 1)

            def batch(b, prefetch):
                for n, j, k in steps(b, prefetch):
                    if prefetch:
                        for blk, t, m in ln_tiles(b, n, j, late=1):
                            z_hi(b, blk, t)
                    exps(b, k)
                    if j == JQ and (n + 2 < NG or prefetch):
                        q_hi(b, n + 2)
                    for g in ctx_groups(b, n, j):
                        ctx_hi(b, g)
                if not prefetch:
                    ctx_hi(b, NG - 1)

            def split(w, dst, loaded):
                act.wait_ge(loaded, 16)
                nc.scalar.copy(dst[:, HI, :, :], w_stage[:, w * KC:(w + 1) * KC, :]).then_inc(w_hi, 1)

            z_hi(-1, 2, 0)
            z_hi(-1, 2, 1)
            split(0, wq, wq_loaded)
            z_hi(-1, 2, 2)
            z_hi(-1, 2, 3)
            act.wait_ge(consts, 16 * 3)
            q_hi(-1, NG)
            q_hi(-1, NG + 1)
            split(1, wo, wo_loaded)
            batch(-1, True)
            with act.Fori(0, B - 1) as b:
                batch(b, True)
            batch(B - 1, False)

        @block.vector
        def _(dve):

            def unit(b, *what):
                u = of(b)[0][what]
                if what[0] in "zq":
                    dve.wait_ge(act_done, base(b, 2) + u["act"])
                else:
                    dve.wait_ge(unit_full, base(b, 1) + u["full"])
                return ring[:, u["bank"], :]

            def ln_stats(t, n):
                dve.wait_ge(xln_in[t], 4 * (n - t) + 16)
                nc.vector.bn_stats(stats[:, t % 2, :], xln[:, t, :]).then_inc(stats_done, 1)
                dve.wait_ge(stats_done, n + 1)
                carry(dve)
                nc.vector.bn_aggr(mv[:, t % 2, :], stats[:, t % 2, :]).then_inc(mv_done, 1)

            def ln_apply(t, n):
                dve.wait_ge(rstd_done, n + 1)
                nc.vector.tensor_scalar(z[:, t % 2, :], xln[:, t, :], mv[:, t % 2, 0:1], rstd[:, t % 2, 1:2],
                                        ALU.subtract, ALU.mult).then_inc(z_done, 1)

            def z_lo(b, blk, t):
                src = unit(b, "z", blk, t).rearrange("p (c n) -> p c n", n=P)
                at = slice(t * P, (t + 1) * P)
                nc.vector.tensor_tensor(zT[:, LO, :, at], src, zT[:, HI, :, at].bitcast(FP32), ALU.subtract
                                        ).then_inc(dve_done, 1)

            def q_lo(b, n):
                nc.vector.scalar_tensor_tensor(q_hl[:, n % 2, LO, :], unit(b, "q", n), bq_sb[:, n % 4:n % 4 + 1],
                                               q_hl[:, n % 2, HI, :].bitcast(FP32), ALU.add, ALU.subtract
                                               ).then_inc(dve_done, 1)

            def mask_to_add(b, r):
                dve.wait_ge(mask_in, 32 * (b + 1))
                if not (isinstance(b, int) and b == 0):
                    dve.wait_ge(p_done, ((b - 1) * NH + (STRIDE + r + 1) * GH) * KT)
                nc.vector.tensor_scalar(mask_bias[:, r, :], mask_keys_u8[:, r, :], -1e30, None, ALU.mult
                                        ).then_inc(mask_done, 1)
                nc.vector.tensor_scalar(mask_add[:, r, :], mask_u8[:, r, :], -1e30, None, ALU.mult
                                        ).then_inc(mask_done, 1)

            def maxima(b, k):
                r = k // GH % STRIDE
                if not (ahead(b) and k < NH + 2):
                    dve.wait_ge(max_done, (b * NH + k - 1) * QT)
                for q in range(QT):
                    u = k * SPH + q // 2
                    if q % 2 == 0:
                        dve.wait_ge(s_full, b * NH * SPH + u + 1)
                        carry(dve)
                    nc.vector.tensor_tensor_reduce(
                        out=masked[:, k % 2, q, :], in0=sps[:, u % SPH, q % 2 * KEYS:(q % 2 + 1) * KEYS],
                        in1=mask_add[:, r, :], scale=1.0, scalar=-3.4e38, op0=ALU.add, op1=ALU.max,
                        accum_out=mx[:, k % MBUF, q:q + 1]).then_inc(max_done, 1)

            def reciprocal(b, n, part):
                at = slice(part * 256, (part + 1) * 256)
                inverse = nc.vector.reciprocal(r_sb[:, n % 2, at], unit(b, "r", n)[:, at])
                inverse.then_inc(dve_done if part else half_inverted, 1)

            def normalise(b, n):
                src = unit(b, "c", n)
                dve.wait_ge(half_inverted, b * NG + n + 1)
                dve.wait_ge(dve_done, base(b, 1) + of(b)[0]["r", n]["full"])
                if not ahead(b):
                    dve.wait_ge(cT_lo, 1 + b * NG + n - 1)
                nc.vector.tensor_tensor(ctxn[:, n % 2, :], src, r_sb[:, n % 2, :], ALU.mult).then_inc(dve_done, 1)

            def output(b, blk, t):
                src = unit(b, "o", blk, t)
                dve.wait_ge(xb_done, (b * NBLK + blk) * QT + t + 1)
                nc.vector.tensor_tensor(xres[:, t, :], src, xres[:, t, :], ALU.add).then_inc(dve_done, 1)

            def batch(b, prefetch):
                for n, j, k in steps(b, prefetch):
                    if k + 2 < NH or prefetch:
                        if j == 1 and 5 <= n <= NG and prefetch and not ahead(b):
                            mask_to_add(b + 1, n - 5)
                        maxima(b, k + 2)
                    if j == JR + 1 and behind(b, n):
                        reciprocal(b, n - 1, 1)
                    if prefetch:
                        for blk, t, m in ln_tiles(b, n, j, late=1):
                            z_lo(b, blk, t)
                    if j == JQ and (n + 2 < NG or prefetch):
                        q_lo(b, n + 2)
                    if j == JC and behind(b, n):
                        normalise(b, n - 1)
                    for blk, t in out_tiles(b, n, j):
                        output(b, blk, t)
                    if prefetch:
                        for blk, t, m in ln_tiles(b, n, j):
                            ln_apply(t, m)
                        for blk, t, m in ln_tiles(b, n, j, late=-1):
                            ln_stats(t, m)
                    if j == JR and behind(b, n):
                        reciprocal(b, n - 1, 0)
                if not prefetch:
                    reciprocal(b, NG - 1, 0)
                    reciprocal(b, NG - 1, 1)
                    normalise(b, NG - 1)
                    for t in range(QT):
                        output(b, 1, t)

            def split(w, dst):
                dve.wait_ge(w_hi, w + 1)
                nc.vector.tensor_tensor(dst[:, LO, :, :], w_stage[:, w * KC:(w + 1) * KC, :],
                                        dst[:, HI, :, :].bitcast(FP32), ALU.subtract).then_inc(w_lo, 1)

            ln_stats(0, 0)
            ln_stats(1, 1)
            ln_apply(0, 0)
            for t in range(QT):
                if t + 2 < QT:
                    ln_stats(t + 2, t + 2)
                if t == 2:
                    split(0, wq)
                if t + 1 < QT:
                    ln_apply(t + 1, t + 1)
                z_lo(-1, 2, t)
            mask_to_add(0, 0)
            dve.wait_ge(consts, 16 * 3)
            nc.vector.tensor_scalar(neg_ones[:, :], ident[:, :], 0.0, -1.0, ALU.mult, ALU.add).then_inc(ones_set, 1)
            q_lo(-1, NG)
            for r in range(1, STRIDE):
                mask_to_add(0, r)
            q_lo(-1, NG + 1)
            maxima(-1, NH)
            maxima(-1, NH + 1)
            split(1, wo)
            batch(-1, True)
            with dve.Fori(0, B - 1) as b:
                batch(b, True)
            batch(B - 1, False)

        @block.tensor
        def _(pe):
            pe.wait_ge(consts, 16 * 3)

            def bank(b, *what):
                u = of(b)[0][what]
                if not (ahead(b) and u["full"] <= RING):
                    pe.wait_ge(dve_done, base(b, 1) + u["full"] - RING)
                return ring[:, u["bank"], :]

            def product(out, lhs, rhs):
                for c in range(KC):
                    for n, (a, r) in enumerate(PARTS):
                        last = nc.tensor.matmul(out, lhs(a, c), rhs(r, c), start=(c == 0 and n == 0),
                                                stop=(c == KC - 1 and n == len(PARTS) - 1))
                return last

            def transpose_z(b, blk, t, m):
                out = bank(b, "z", blk, t)
                pe.wait_ge(z_done, m + 1)
                for c in range(KC):
                    last = nc.tensor.transpose(out[:, c * P:(c + 1) * P], z[:, t % 2, c * P:(c + 1) * P], ident[:, :])
                last.then_inc(unit_full, 1)

            def queries(b, n):
                if n == 4:
                    pe.wait_ge(dve_done, base(b, 1))
                elif n % 4 == 0:
                    pe.wait_ge(dve_done, base(b, 1) + of(b)[0]["z", n // 4, QT - 1]["full"])
                r = n % 4
                out = bank(b, "q", n)
                product(out, lambda a, c: wq[:, a, c, r * P:(r + 1) * P], lambda h, c: zT[:, h, c, :]
                        ).then_inc(unit_full, 1)

            def scores(b, k):
                n, j = k // GH, k % GH
                r, nb = n % 4, n // NG
                pe.wait_ge(q_stacked[n % 2][j], STACKED * (b * (NG // 2) + n // 2 + 1))
                if j == 0:
                    pe.wait_ge(k_loaded[r], 64 * (b + nb + 1))
                for s in range(SPH):
                    u = k * SPH + s
                    if not (ahead(b) and u < (NH + 1) * SPH):
                        pe.wait_ge(max_done, (b * NH * SPH + u - SPH + 1) * 2)
                    for q in (2 * s, 2 * s + 1):
                        last = nc.tensor.matmul(sps[:, u % SPH, q % 2 * KEYS:(q % 2 + 1) * KEYS],
                                                q_st[:, n % 2, j, q * P:(q + 1) * P], k_st[:, r, j, :],
                                                start=True, stop=True)
                    last.then_inc(s_full, 1)

            def scores_by_key(b, n, j):
                k = n * GH + j
                for c in range(KT):
                    if not (ahead(b) and k == NH):
                        pe.wait_ge(p_done, (b * NH + k - 1) * KT + c + 1)
                    nc.tensor.matmul(stps[:, c, :], k_st[:, n % 4, j, c * P:(c + 1) * P], q_st[:, n % 2, j, :],
                                     start=True, stop=False)
                    if c == 0:
                        pe.wait_ge(diag_done, b * NH + k + 1)
                    nc.tensor.matmul(stps[:, c, :], neg_ones[:, :],
                                     diag[:, k % 2, :, :].rearrange("p q n -> p (q n)"), start=False, stop=True
                                     ).then_inc(st_full, 1)

            def sums(b, n):
                pe.wait_ge(p_done, (b * NH + (n + 1) * GH) * KT)
                out = bank(b, "r", n)
                for c in range(KT):
                    for j in range(GH):
                        last = nc.tensor.matmul(out[j * HD:(j + 1) * HD, :], ones[:, :], pT[:, n % 2, j, c, :],
                                                start=(c == 0), stop=(c == KT - 1))
                last.then_inc(unit_full, 1)

            def times_v(b, n):
                if n % NG < STRIDE:
                    pe.wait_ge(v_loaded[n % NG], 16 * (b + n // NG + 1))
                out = bank(b, "c", n)
                for c in range(KT):
                    for j in range(GH):
                        last = nc.tensor.matmul(out[j * HD:(j + 1) * HD, :], v_sb[:, n % 4, c, j * HD:(j + 1) * HD],
                                                pT[:, n % 2, j, c, :], start=(c == 0), stop=(c == KT - 1))
                last.then_inc(unit_full, 1)

            def outputs(b, tiles):
                for blk, t in tiles:
                    pe.wait_ge(cT_lo, 1 + b * NG + (blk + 1) * STRIDE)
                    out = bank(b, "o", blk, t)
                    product(out, lambda a, c: cT[:, a, c, t * P:(t + 1) * P], lambda h, c: wo[:, h, c, :]
                            ).then_inc(unit_full, 1)

            def batch(b, prefetch):
                for n, j, k in steps(b, prefetch):
                    if k + 2 < NH or prefetch:
                        scores(b, k + 2)
                    if prefetch:
                        for blk, t, m in ln_tiles(b, n, j, late=1):
                            transpose_z(b, blk, t, m)
                    scores_by_key(b, n, j)
                    if j == JQ and (n + 2 < NG or prefetch):
                        queries(b, n + 2)
                    if j == JC and behind(b, n):
                        times_v(b, n - 1)
                    outputs(b, out_tiles(b, n, j))
                    if j == JR and behind(b, n):
                        sums(b, n - 1)
                if not prefetch:
                    sums(b, NG - 1)
                    times_v(b, NG - 1)
                    outputs(b, [(1, t) for t in range(QT)])

            for t in range(QT):
                transpose_z(-1, 2, t, t)
            pe.wait_ge(w_lo, 1)
            queries(-1, NG)
            queries(-1, NG + 1)
            scores(-1, NH)
            scores(-1, NH + 1)
            pe.wait_ge(ones_set, 2)
            pe.wait_ge(w_lo, 2)
            batch(-1, True)
            with pe.Fori(0, B - 1) as b:
                batch(b, True)
            batch(B - 1, False)


def adapters(nc, x2, wd1, wd2, wb, bd1, bd2, b_base, wa_down, ba_down, wa_up, ba_up, ident_in, out):
    RING = 8
    NU = NBLK * E
    OPEN = 3
    BEFORE = 0

    TAIL = [("z", TT - 3), ("h", NU), ("z", TT - 2), ("h", NU + 1), ("z", TT - 1)]

    def plan(prefetch, first=False):
        if first:
            alloc = [("z", t) for t in range(TT - 3)] + TAIL
            read = list(alloc)
        else:
            alloc = []
            for u in range(NU):
                alloc += [("h", u + 2)] * (u + 2 < NU) + [("rec", u, c) for c in range(KC)]
            read = list(alloc)
            opened = [("o", t) for t in range(OPEN)]
            alloc += opened[:BEFORE] + [("loss",)] + opened[BEFORE:] + [("a", 0), ("a", 1)]
            read += [("loss",), ("a", 0), ("a", 1)] + opened[:3]
            for t in range(3, TT):
                both = [("o", t)] + [("z", t - 3)] * prefetch
                alloc += both[t < OPEN:]
                read += both
            if prefetch:
                alloc += TAIL
                read += TAIL
        acts = dves = 0
        table = {}
        for what in read:
            acts += what[0] in ("z", "h", "a")
            dves += what[0] in ("z", "rec", "loss", "o")
            table[what] = dict(full=len(table) + 1, act=acts, dve=dves, eng="act" if what[0] in ("h", "a") else "dve")
        mid = 0 if first else len(alloc) // 2
        alloc[mid:mid] = [("skip",)] * (-len(alloc) % RING)
        for i, what in enumerate(alloc):
            if what != ("skip",):
                last = i - RING
                while last >= 0 and alloc[last] == ("skip",):
                    last -= RING
                freed = None
                if last >= 0:
                    freed = table[alloc[last]]["eng"], table[alloc[last]][table[alloc[last]]["eng"]]
                elif not first:
                    later = TAIL[max(i + 1 + len(TAIL) - RING, 0):]
                    if i >= RING - len(TAIL) and TAIL[i + len(TAIL) - RING][0] == "h":
                        freed = "act", -len(later)
                    else:
                        freed = "dve", -(sum(w[0] == "z" for w in later) + max(RING - len(TAIL) - i - 1, 0))
                table[what].update(i=i, bank=i % RING, freed=freed)
        return table, len(table), acts, dves

    FIRST, LOOPED, LAST = plan(False, True), plan(True), plan(False)

    def of(b):
        return FIRST if ahead(b) else LAST if isinstance(b, int) and b == B - 1 else LOOPED

    def base(b, which):
        return 0 if ahead(b) else FIRST[which] + b * LOOPED[which]

    ctx = ExitStack()
    with ctx:
        def sb(name, shape, dt=FP32):
            return ctx.enter_context(nc.sbuf_tensor("f_" + name, shape, dt))

        def sem(name):
            return ctx.enter_context(nc.semaphore("f_" + name))

        with nc.sbuf_tensor("f_w2_stage", [P, 4, 512], FP32) as early:
            w2_stage = early
        h = sb("h", [P, 3, 2, 512], FP32R)
        w1 = sb("w1", [P, 2, KC, E * H], FP32R)
        w2 = sb("w2", [H, 2, E, D], FP32R)
        wbase = sb("wbase", [P, 2, KC, D], FP32R)
        zT = sb("zT", [P, 2, KC, S], FP32R)
        zf = sb("zf", [P, KC, S])
        hf = sb("hf", [P, 2, 512])
        diff = sb("diff", [P, 2, KC, 512])
        dn_raw = sb("dn_raw", [P, KC, R])
        dn = sb("dn", [P, 2, KC, 2, R], FP32R)
        up_raw = sb("up_raw", [P, D])
        up = sb("up", [P, 2, D], FP32R)
        ba_dn = sb("ba_dn", [P, 1])
        ba_up_rep = sb("ba_up_rep", [P, D])
        af = sb("af", [P, 2, 512])
        a_hl = sb("a_hl", [P, 2, 512], FP32R)
        bb_rep = sb("bb_rep", [P, D])
        bsum = sb("bsum", [P, D])
        xln = sb("xln", [P, 2, D])
        z = sb("z", [P, 2, D])
        xres = sb("xres", [P, 4, D])
        ident = sb("ident", [P, P])
        b1 = sb("b1", [P, E])
        b2 = sb("b2", [P, E, KC])
        ones = sb("ones", [P, 1])
        sq = sb("sq", [P, 2, NBLK, E])
        l8 = sb("l8", [1, E])
        neg = sb("neg", [1, E])
        best = sb("best", [1, 8])
        idx = sb("idx", [1, 8], U32)
        stats = sb("stats", [P, 2, 6])
        mv = sb("mv", [P, 2, 2])
        rstd = sb("rstd", [P, 2, 2])
        half = sb("half", [P, 1])
        stage = [diff[:, 0, :, :], diff[:, 1, :, :], w2_stage[:, :, :],
                 diff[:, 0, :, :], diff[:, 1, :, :]]
        ring = ctx.enter_context(nc.psum_tensor("f_ring", [P, RING, 512], FP32))

        waited = sem("waited")
        consts = sem("consts")
        w_loaded = [sem(f"w_loaded{i}") for i in range(5)]
        first_in = [sem(f"first_in{t}") for t in range(2)]
        w_hi = sem("w_hi")
        w_lo = sem("w_lo")
        half_set = sem("half_set")
        ones_set = sem("ones_set")
        xln_in = [sem(f"xln_in{j}") for j in range(2)]
        xres_in = [sem(f"xres_in{j}") for j in range(4)]
        stored = [sem(f"stored{j}") for j in range(4)]
        stats_done = sem("stats_done")
        mv_done = sem("mv_done")
        var_eps = sem("var_eps")
        rstd_done = sem("rstd_done")
        z_done = sem("z_done")
        zf_done = sem("zf_done")
        unit_full = sem("unit_full")
        act_done = sem("act_done")
        dve_done = sem("dve_done")
        h_hi = sem("h_hi")
        h_lo = sem("h_lo")
        sq_done = sem("sq_done")
        argmin_step = sem("argmin_step")
        expert_in = sem("expert_in")
        dn_step = sem("dn_step")
        a_hi = sem("a_hi")
        a_lo = sem("a_lo")
        bsum_done = sem("bsum_done")
        xb_done = sem("xb_done")
        block = ctx.enter_context(nc.Block())
        NEXP = 6
        PIECES = [(wd1[:, :, 0:512], lambda a: w1[:, a, :, 0:512]),
                  (wd1[:, :, 512:1024], lambda a: w1[:, a, :, 512:1024]),
                  (wd2[:, 0:4, :], lambda a: w2[:, a, 0:4, :]), (wd2[:, 4:8, :], lambda a: w2[:, a, 4:8, :]),
                  (wb, lambda a: wbase[:, a, :, :])]

        def tokens(b, t):
            if ahead(b) and t >= 2:
                return xres[:, t - 2, :] if t < 6 else af[:, t - 6, :]
            return xln[:, t % 2, :]

        def carry(engine):
            engine.sem_inc(waited, 1)

        @block.sync
        def _(sp):
            for j in range(4):
                sp.sem_inc(stored[j], 16)

            def load_ln(b, t):
                n = (b + 1) * TT + t
                sp.wait_ge(z_done, n - 1)
                sp.dma_start(xln[:, t % 2, :], x2[bass.ds(n, 1), :, :].rearrange("o p d -> (o p) d")
                             ).then_inc(xln_in[t % 2], 16)

            def load_res(b, t):
                sp.wait_ge(stored[t % 4], 16 + 16 * (b * 2 + t // 4))
                sp.dma_start(xres[:, t % 4, :], x2[bass.ds(b * TT + t, 1), :, :].rearrange("o p d -> (o p) d")
                             ).then_inc(xres_in[t % 4], 16)

            def store(b, t):
                sp.wait_ge(dve_done, base(b, 3) + of(b)[0]["o", t]["dve"])
                sp.dma_start(out[bass.ds(b * TT + t, 1), :, :].rearrange("o p d -> (o p) d"),
                             xres[:, t % 4, :]).then_inc(stored[t % 4], 16)

            sp.dma_start(ident[:, :], ident_in).then_inc(consts, 16)
            sp.dma_start(b1[:, :], bd1).then_inc(consts, 16)
            sp.dma_start(b2[:, :, :], bd2).then_inc(consts, 16)
            sp.dma_start(bb_rep[:, :], b_base.partition_broadcast(P)).then_inc(consts, 16)
            for i, (src, _) in enumerate(PIECES):
                for t in range(4 * i, min(4 * i + 4, TT)):
                    sp.dma_start(tokens(-1, t), x2[t]).then_inc(first_in[t // 4], 16)
                if i >= 3:
                    sp.wait_ge(w_lo, i - 2)
                sp.dma_start(stage[i], src).then_inc(w_loaded[i], 16)

            sp.wait_ge(z_done, TT)

            def batch(b, prefetch):
                for t in range(4):
                    load_res(b, t)
                if prefetch:
                    load_ln(b, 0)
                    load_ln(b, 1)
                sp.wait_ge(argmin_step, 4 * (b + 1))
                carry(sp)
                e = sp.value_load(idx[0:1, 0:1], min_val=0, max_val=E - 1)
                sp.dma_start(dn_raw[:, :, :], wa_down[bass.ds(e, 1), :, :, :].rearrange("o p c r -> p (o c) r")
                             ).then_inc(expert_in, 16)
                for half_at in (0, R):
                    sp.dma_start(ba_dn[half_at:half_at + R, :], ba_down[bass.ds(e, 1), :].rearrange("o r -> r o")
                                 ).then_inc(expert_in, 16)
                    sp.dma_start(up_raw[half_at:half_at + R, :], wa_up[bass.ds(e, 1), :, :].rearrange("o r d -> (o r) d")
                                 ).then_inc(expert_in, 16)
                sp.dma_start(ba_up_rep[:, :], ba_up[bass.ds(e, 1), :].rearrange("o d -> (o d)").partition_broadcast(P)
                             ).then_inc(expert_in, 16)
                for t in range(TT):
                    if prefetch and t + 2 < TT:
                        load_ln(b, t + 2)
                    store(b, t)
                    if 1 <= t <= TT - 4:
                        load_res(b, t + 3)

            with sp.Fori(0, B - 1) as b:
                batch(b, True)
            batch(B - 1, False)
            for j in range(4):
                sp.wait_ge(stored[j], 16 + 16 * B * 2)

        @block.gpsimd
        def _(pool):
            nc.gpsimd.memset(half[:, :], -0.5).then_inc(half_set, 1)
            nc.gpsimd.memset(ones[:, :], 1.0).then_inc(ones_set, 1)
            pool.wait_ge(half_set, 1)
            pool.wait_ge(consts, 16 * 4)

            def ln_rstd(b, t):
                n = (b + 1) * TT + t
                pool.wait_ge(mv_done, n + 1)
                carry(pool)
                nc.gpsimd.tensor_scalar(rstd[:, t % 2, 0:1], mv[:, t % 2, 1:2], EPS, None, ALU.add
                                        ).then_inc(var_eps, 1)
                pool.wait_ge(var_eps, n + 1)
                nc.gpsimd.tensor_tensor(rstd[:, t % 2, 1:2], rstd[:, t % 2, 0:1], half[:, :], ALU.pow
                                        ).then_inc(rstd_done, 1)

            def z_whole(b, t):
                pool.wait_ge(dve_done, base(b, 3) + of(b)[0]["z", t]["dve"])
                at = slice(t * P, (t + 1) * P)
                nc.gpsimd.tensor_tensor(zf[:, :, at], zT[:, HI, :, at].bitcast(FP32), zT[:, LO, :, at].bitcast(FP32),
                                        ALU.add).then_inc(zf_done, 1)

            def add_bias(b, t):
                pool.wait_ge(xres_in[t % 4], 16 * (b * 2 + t // 4 + 1))
                nc.gpsimd.tensor_tensor(xres[:, t % 4, :], xres[:, t % 4, :], bsum[:, :], ALU.add).then_inc(xb_done, 1)

            def batch(b, prefetch):
                if prefetch:
                    ln_rstd(b, 0)
                    ln_rstd(b, 1)
                pool.wait_ge(expert_in, 16 * NEXP * (b + 1))
                nc.gpsimd.tensor_tensor(bsum[:, :], bb_rep[:, :], ba_up_rep[:, :], ALU.add).then_inc(bsum_done, 1)
                pool.wait_ge(bsum_done, b + 1)
                for t in range(4):
                    add_bias(b, t)
                for t in range(3, TT):
                    if prefetch:
                        ln_rstd(b, t - 1)
                        z_whole(b, t - 3)
                    if t + 1 < TT:
                        add_bias(b, t + 1)
                if prefetch:
                    ln_rstd(b, TT - 1)
                    z_whole(b, TT - 3)
                    z_whole(b, TT - 2)
                    z_whole(b, TT - 1)

            for t in range(TT):
                ln_rstd(-1, t)
            for t in range(TT):
                z_whole(-1, t)
            with pool.Fori(0, B - 1) as b:
                batch(b, True)
            batch(B - 1, False)

        @block.scalar
        def _(act):
            act.sem_inc(sq_done, 1)
            act.wait_ge(consts, 16 * 4)

            def unit(b, *what):
                u = of(b)[0][what]
                act.wait_ge(unit_full, base(b, 1) + u["full"])
                return ring[:, u["bank"], :]

            def z_hi(b, t):
                src = unit(b, "z", t).rearrange("p (c n) -> p c n", n=P)
                nc.scalar.copy(zT[:, HI, :, t * P:(t + 1) * P], src).then_inc(act_done, 1)

            def hidden(b, u):
                e = u % E
                src = unit(b, "h", u)
                if not ahead(b):
                    act.wait_ge(h_lo, 1 + b * NU + u - 1)
                nc.scalar.activation(hf[:, u % 2, :], src, ACT.Relu, bias=b1[:, e:e + 1]).then_inc(act_done, 1)

            def squares(b, u):
                for part in range(2):
                    at = slice(2 * part, 2 * part + 2)
                    act.wait_ge(dve_done, base(b, 3) + of(b)[0]["rec", u, 2 * part + 1]["dve"])
                    nc.scalar.activation(diff[:, u % 2, at, :], diff[:, u % 2, at, :], ACT.Square,
                                         accum_out=sq[:, part, u // E, u % E:u % E + 1]).then_inc(sq_done, 1)

            def batch(b, prefetch):
                for u in range(NU):
                    if u + 2 < NU:
                        hidden(b, u + 2)
                    if u >= 1:
                        squares(b, u - 1)
                squares(b, NU - 1)
                act.wait_ge(expert_in, 16 * NEXP * (b + 1))
                for blk in range(NBLK):
                    src = unit(b, "a", blk)
                    nc.scalar.activation(af[:, blk, :], src, ACT.Relu, bias=ba_dn[:, 0:1]).then_inc(act_done, 1)
                if prefetch:
                    for t in range(TT - 3):
                        z_hi(b, t)
                    for what, x in TAIL:
                        (z_hi if what == "z" else hidden)(b, x)

            def split(i):
                act.wait_ge(w_loaded[i], 16)
                nc.scalar.copy(PIECES[i][1](HI), stage[i]).then_inc(w_hi, 1)

            for t in range(TT - 3):
                z_hi(-1, t)
                if t == 3:
                    split(0)
            for what, x in TAIL:
                (z_hi if what == "z" else hidden)(-1, x)
            for i in range(1, len(PIECES)):
                split(i)
            with act.Fori(0, B - 1) as b:
                batch(b, True)
            batch(B - 1, False)

        @block.vector
        def _(dve):
            dve.sem_inc(h_lo, 1)
            dve.wait_ge(consts, 16 * 4)

            def unit(b, *what):
                u = of(b)[0][what]
                if what[0] == "z":
                    dve.wait_ge(act_done, base(b, 2) + u["act"])
                else:
                    dve.wait_ge(unit_full, base(b, 1) + u["full"])
                return ring[:, u["bank"], :]

            def ln_stats(b, t):
                n = (b + 1) * TT + t
                if ahead(b):
                    dve.wait_ge(first_in[t // 4], 16 * 4)
                else:
                    dve.wait_ge(xln_in[t % 2], 16 * (b * (TT // 2) + t // 2 + 1))
                nc.vector.bn_stats(stats[:, t % 2, :], tokens(b, t)).then_inc(stats_done, 1)
                dve.wait_ge(stats_done, n + 1)
                carry(dve)
                nc.vector.bn_aggr(mv[:, t % 2, :], stats[:, t % 2, :]).then_inc(mv_done, 1)

            def ln_apply(b, t):
                n = (b + 1) * TT + t
                dve.wait_ge(rstd_done, n + 1)
                nc.vector.tensor_scalar(z[:, t % 2, :], tokens(b, t), mv[:, t % 2, 0:1], rstd[:, t % 2, 1:2],
                                        ALU.subtract, ALU.mult).then_inc(z_done, 1)

            def z_lo(b, t):
                src = unit(b, "z", t).rearrange("p (c n) -> p c n", n=P)
                at = slice(t * P, (t + 1) * P)
                nc.vector.tensor_tensor(zT[:, LO, :, at], src, zT[:, HI, :, at].bitcast(FP32), ALU.subtract
                                        ).then_inc(dve_done, 1)

            def split_h(b, u):
                dve.wait_ge(act_done, base(b, 2) + of(b)[0]["h", u]["act"])
                nc.vector.tensor_copy(h[:, u % NU % 3, HI, :], hf[:, u % 2, :]).then_inc(h_hi, 1)
                dve.wait_ge(h_hi, b * NU + u + 1)
                nc.vector.tensor_tensor(h[:, u % NU % 3, LO, :], hf[:, u % 2, :], h[:, u % NU % 3, HI, :].bitcast(FP32),
                                        ALU.subtract).then_inc(h_lo, 1)

            def error(b, u):
                blk, e = u // E, u % E
                dve.wait_ge(sq_done, 1 + 2 * (b * NU + max(u - 1, 0)))
                for c in range(KC):
                    nc.vector.scalar_tensor_tensor(diff[:, u % 2, c, :], unit(b, "rec", u, c), b2[:, e, c:c + 1],
                                                   zf[:, c, blk * 512:(blk + 1) * 512], ALU.add, ALU.subtract
                                                   ).then_inc(dve_done, 1)

            def argmin(b):
                src = unit(b, "loss")[0:1, 0:2 * NU]
                nc.vector.tensor_reduce(l8[:, :], src.rearrange("p (k e) -> p e k", e=E), AX.X, ALU.add
                                        ).then_inc(dve_done, 1)
                dve.wait_ge(dve_done, base(b, 3) + of(b)[0]["loss",]["dve"])
                nc.vector.tensor_scalar(neg[:, :], l8[:, :], -1.0 / (S * D), None, ALU.mult).then_inc(argmin_step, 1)
                dve.wait_ge(argmin_step, 4 * b + 1)
                carry(dve)
                nc.vector.max(best[:, :], neg[:, :]).then_inc(argmin_step, 1)
                dve.wait_ge(argmin_step, 4 * b + 2)
                carry(dve)
                nc.vector.max_index(idx[:, :], best[:, :], neg[:, :]).then_inc(argmin_step, 2)

            def split_expert(b):
                dve.wait_ge(expert_in, 16 * NEXP * (b + 1))
                raw = dn_raw[:, :, None, :].broadcast_to((P, KC, 2, R))
                nc.vector.tensor_copy(dn[:, HI, :, :, :], raw).then_inc(dn_step, 1)
                nc.vector.tensor_copy(up[:, HI, :], up_raw[:, :]).then_inc(dn_step, 1)
                dve.wait_ge(dn_step, 4 * b + 2)
                nc.vector.tensor_tensor(dn[:, LO, :, :, :], raw, dn[:, HI, :, :, :].bitcast(FP32), ALU.subtract
                                        ).then_inc(dn_step, 1)
                nc.vector.tensor_tensor(up[:, LO, :], up_raw[:, :], up[:, HI, :].bitcast(FP32), ALU.subtract
                                        ).then_inc(dn_step, 1)

            def split_a(b, blk):
                dve.wait_ge(act_done, base(b, 2) + of(b)[0]["a", blk]["act"])
                nc.vector.tensor_copy(a_hl[:, blk, :], af[:, blk, :]).then_inc(a_hi, 1)
                dve.wait_ge(a_hi, b * NBLK + blk + 1)
                nc.vector.tensor_tensor(a_hl[R:P, blk, :], af[R:P, blk, :], a_hl[R:P, blk, :].bitcast(FP32),
                                        ALU.subtract).then_inc(a_lo, 1)

            def output(b, t):
                src = unit(b, "o", t)
                dve.wait_ge(xb_done, b * TT + t + 1)
                nc.vector.tensor_tensor(xres[:, t % 4, :], src, xres[:, t % 4, :], ALU.add).then_inc(dve_done, 1)

            def batch(b, prefetch):
                for u in range(NU):
                    if u % E == 0:
                        dve.wait_ge(zf_done, (b + 1) * TT - (TT // 2 if u == 0 else 0))
                    if u + 2 < NU:
                        split_h(b, u + 2)
                    error(b, u)
                argmin(b)
                if prefetch:
                    ln_stats(b, 0)
                    ln_stats(b, 1)
                    ln_apply(b, 0)
                    ln_apply(b, 1)
                split_expert(b)
                for blk in range(NBLK):
                    split_a(b, blk)
                for t in range(3):
                    output(b, t)
                for t in range(3, TT):
                    output(b, t)
                    if prefetch:
                        ln_stats(b, t - 1)
                        z_lo(b, t - 3)
                        ln_apply(b, t - 1)
                if prefetch:
                    ln_stats(b, TT - 1)
                    for what, x in TAIL:
                        (z_lo if what == "z" else split_h)(b, x)
                        if (what, x) == ("z", TT - 3):
                            ln_apply(b, TT - 1)

            def split(i):
                dve.wait_ge(w_hi, i + 1)
                dst = PIECES[i][1]
                nc.vector.tensor_tensor(dst(LO), stage[i], dst(HI).bitcast(FP32), ALU.subtract).then_inc(w_lo, 1)

            ln_stats(-1, 0)
            ln_stats(-1, 1)
            ln_apply(-1, 0)
            for t in range(TT):
                if t + 2 < TT:
                    ln_stats(-1, t + 2)
                if t + 1 < TT:
                    ln_apply(-1, t + 1)
                z_lo(-1, t)
                if t == 3:
                    split(0)
            for i in range(1, 3):
                split(i)
            dve.wait_ge(w_lo, 3)
            split_h(-1, NU)
            split_h(-1, NU + 1)
            for i in range(3, len(PIECES)):
                split(i)
            dve.wait_ge(w_lo, len(PIECES))
            with dve.Fori(0, B - 1) as b:
                batch(b, True)
            batch(B - 1, False)

        @block.tensor
        def _(pe):
            pe.wait_ge(consts, 16 * 4)
            pe.wait_ge(ones_set, 1)

            def bank(b, *what):
                u = of(b)[0][what]
                if u["freed"]:
                    eng, count = u["freed"]
                    if eng == "act":
                        pe.wait_ge(act_done, base(b, 2) + count)
                    else:
                        pe.wait_ge(dve_done, base(b, 3) + count)
                return ring[:, u["bank"], :]

            def product(out, lhs, rhs, stop=True):
                for c in range(KC):
                    for n, (a, r) in enumerate(PARTS):
                        last = nc.tensor.matmul(out, lhs(a, c), rhs(r, c), start=(c == 0 and n == 0),
                                                stop=(stop and c == KC - 1 and n == len(PARTS) - 1))
                return last

            def transpose_z(b, t):
                out = bank(b, "z", t)
                pe.wait_ge(z_done, (b + 1) * TT + t + 1)
                for c in range(KC):
                    last = nc.tensor.transpose(out[:, c * P:(c + 1) * P], z[:, t % 2, c * P:(c + 1) * P], ident[:, :])
                last.then_inc(unit_full, 1)

            def encode(b, u):
                blk, e = u % NU // E, u % E
                if e == 0:
                    pe.wait_ge(dve_done, base(b, 3) + (of(b)[0]["z", TT // 2 - 1]["dve"] if u == NU else 0))
                    pe.wait_ge(w_lo, 1)
                if e == E // 2:
                    pe.wait_ge(w_lo, 2)
                product(bank(b, "h", u), lambda a, c: w1[:, a, c, e * H:(e + 1) * H],
                        lambda r, c: zT[:, r, c, blk * 512:(blk + 1) * 512]).then_inc(unit_full, 1)

            def rebuild(b, u):
                e = u % E
                pe.wait_ge(h_lo, 1 + b * NU + u + 1)
                if e % (E // 2) == 0:
                    pe.wait_ge(w_lo, 3 if e == 0 else 4)
                for c in range(KC):
                    out = bank(b, "rec", u, c)
                    for n, (a, r) in enumerate(PARTS):
                        last = nc.tensor.matmul(out, w2[:, a, e, c * P:(c + 1) * P], h[:, u % NU % 3, r, :],
                                                start=(n == 0), stop=(n == len(PARTS) - 1))
                    last.then_inc(unit_full, 1)

            def loss(b):
                out = bank(b, "loss")
                pe.wait_ge(sq_done, 1 + 2 * (b + 1) * NU)
                nc.tensor.matmul(out[0:1, 0:2 * NU], ones[:, :], sq[:, :, :, :].rearrange("p a k e -> p (a k e)"),
                                 start=True, stop=True).then_inc(unit_full, 1)

            def base_part(b, t):
                out = bank(b, "o", t)
                product(out, lambda a, c: zT[:, a, c, t * P:(t + 1) * P], lambda r, c: wbase[:, r, c, :], stop=False)
                return out

            def adapter_part(b, t, out):
                pe.wait_ge(a_lo, b * NBLK + t // 4 + 1)
                for r in (HI, LO):
                    last = nc.tensor.matmul(out, a_hl[:, t // 4, t % 4 * P:(t % 4 + 1) * P], up[:, r, :],
                                            start=False, stop=(r == LO))
                last.then_inc(unit_full, 1)

            def down(b, blk):
                out = bank(b, "a", blk)
                product(out, lambda a, c: dn[:, a, c, :, :].rearrange("p k r -> p (k r)"),
                        lambda r, c: zT[:, r, c, blk * 512:(blk + 1) * 512]).then_inc(unit_full, 1)

            def transposes_and_encoders(b):
                for what, x in TAIL:
                    (transpose_z if what == "z" else encode)(b, x)

            def batch(b, prefetch):
                for u in range(NU):
                    if u + 2 < NU:
                        encode(b, u + 2)
                    rebuild(b, u)
                pe.wait_ge(w_lo, len(PIECES))
                open_tiles = [base_part(b, t) for t in range(BEFORE)]
                loss(b)
                open_tiles += [base_part(b, t) for t in range(BEFORE, OPEN)]
                pe.wait_ge(dn_step, 4 * (b + 1))
                down(b, 0)
                down(b, 1)
                for t in range(3):
                    adapter_part(b, t, open_tiles[t])
                for t in range(3, TT):
                    adapter_part(b, t, base_part(b, t) if t >= OPEN else open_tiles[t])
                    if prefetch:
                        transpose_z(b, t - 3)
                if prefetch:
                    transposes_and_encoders(b)

            for t in range(TT - 3):
                transpose_z(-1, t)
            transposes_and_encoders(-1)
            with pe.Fori(0, B - 1) as b:
                batch(b, True)
            batch(B - 1, False)


def decoder_layer(nc, t):
    x1 = nc.dram_tensor("x_after_self_attention", (B * TT, P, D), FP32, kind="Internal").ap()
    x2 = nc.dram_tensor("x_after_cross_attention", (B * TT, P, D), FP32, kind="Internal").ap()
    keys = nc.dram_tensor("cross_keys", (B * STRIDE, P, 2, KEYS), FP32, kind="Internal").ap()
    values = nc.dram_tensor("cross_values", (B * STRIDE, P, KT, P), FP32, kind="Internal").ap()
    self_attention(nc, t["x"], t["s_wqT"], t["s_wkT"], t["s_wvT"], t["s_bq"], t["s_bk"], t["s_bv"],
                   t["ident"], t["causal"], x1)
    cross_keys_values(nc, t["ctxT"], t["c_wk"], t["c_wv"], t["c_bk"], t["c_bv"], t["ident"], keys, values)
    cross_attention(nc, x1, t["c_wq"], t["c_wo"], t["c_bq"], t["c_bo"], t["mask"], t["mask_keys"], keys,
                    values, t["ident"], x2)
    adapters(nc, x2, t["wd1"], t["wd2"], t["w_base"], t["bd1"], t["bd2"], t["b_base"], t["wa_down"], t["ba_down"],
             t["wa_up"], t["ba_up"], t["ident"], t["out"])


def kernel(**inputs):
    import concourse.bacc as bacc
    from concourse.bass_utils import run_bass_kernel_spmd

    a = {name: np.asarray(v) for name, v in inputs.items()}

    def rows(w):
        return w.reshape(KC, P, -1).transpose(1, 0, 2)

    def by_group(w):
        return w.reshape(D, GH, STRIDE, HD).transpose(0, 2, 1, 3).reshape(D, D)

    def group_bias(v):
        return v.reshape(GH, STRIDE, HD).transpose(0, 2, 1).reshape(P, STRIDE)

    arrays = {
        "x": a["x"].reshape(B * TT, P, D),
        "s_wqT": rows(a["L0_attn_Wq"].T), "s_wkT": rows(a["L0_attn_Wk"].T), "s_wvT": rows(a["L0_attn_Wv"].T),
        "s_bq": a["L0_attn_bq"].reshape(KC, P).T, "s_bk": a["L0_attn_bk"].reshape(KC, P).T, "s_bv": a["L0_attn_bv"],
        "ctxT": a["ctx_1024"].transpose(0, 2, 1).reshape(B, KC, P, KEYS, STRIDE).transpose(0, 2, 1, 4, 3).reshape(
            B, P, KC, S),
        "mask": a["mask_BxS2_bf0"].reshape(B, KEYS, STRIDE).transpose(0, 2, 1).reshape(B, S),
        "mask_keys": a["mask_BxS2_bf0"].reshape(B, KT, P, STRIDE).transpose(0, 2, 3, 1),
        "c_wq": rows(by_group(a["L0_xattn_Wq"])), "c_wk": rows(by_group(a["L0_xattn_Wk"])),
        "c_wv": rows(by_group(a["L0_xattn_Wv"])), "c_wo": rows(by_group(a["L0_xattn_Wo"].T).T),
        "c_bq": group_bias(a["L0_xattn_bq"]), "c_bk": group_bias(a["L0_xattn_bk"]),
        "c_bv": group_bias(a["L0_xattn_bv"]), "c_bo": a["L0_xattn_bo"],
        "wd1": rows(a["L0_ffn_Wd1"].transpose(1, 0, 2).reshape(D, E * H)), "wd2": a["L0_ffn_Wd2"].transpose(1, 0, 2),
        "w_base": rows(a["L0_ffn_W_base"]), "b_base": a["L0_ffn_b_base"],
        "bd1": a["L0_ffn_bd1"].T, "bd2": a["L0_ffn_bd2"].reshape(E, KC, P).transpose(2, 0, 1),
        "wa_down": a["L0_ffn_Wa_down"].reshape(E, KC, P, R).transpose(0, 2, 1, 3), "ba_down": a["L0_ffn_ba_down"],
        "wa_up": a["L0_ffn_Wa_up"], "ba_up": a["L0_ffn_ba_up"],
        "ident": np.eye(P, dtype=np.float32),
        "causal": np.triu(np.full((P, P), -1e30, np.float32), 1),
    }
    nc = bacc.Bacc("TRN2", target_bir_lowering=False, num_devices=1)
    arrays = {f"in_{name}": np.ascontiguousarray(v) for name, v in arrays.items()}
    tensors = {name[3:]: nc.dram_tensor(name, v.shape, mybir.dt.from_np(v.dtype), kind="ExternalInput").ap()
               for name, v in arrays.items()}
    tensors["out"] = nc.dram_tensor("out", (B * TT, P, D), FP32, kind="ExternalOutput").ap()
    decoder_layer(nc, tensors)
    got = run_bass_kernel_spmd(nc, [arrays], core_ids=[0])
    return got.results[0]["out"].reshape(B, S, D)
```
